# Optimizing a Trainium2 kernel written in Bass

```python
import numpy as np
import jax
import jax.numpy as jnp

def _softmax(x, axis=-1):
    return jax.nn.softmax(x, axis=axis)

def _gelu(x):
    return jax.nn.gelu(x, approximate=True)

def _silu(x):
    return jax.nn.silu(x)

def _sigmoid(x):
    return jax.nn.sigmoid(x)

def _layernorm(x, axis=-1, eps=1e-05):
    m = jnp.mean(x, axis=axis, keepdims=True)
    v = jnp.var(x, axis=axis, keepdims=True)
    return (x - m) / jnp.sqrt(v + eps)

def _scatter_add(tgt, idx, src, axis=0):
    return tgt.at[idx].add(src)

def _segment_sum(src, seg, n):
    return jax.ops.segment_sum(src, seg, n)
kernel_name = 'mk_conv_attn_hybrid_d4_conv_nchw512_r4_17e2eb'

def setup_inputs(seed: int=0):
    np.random.seed(seed)
    _w = jnp.asarray

    def _rec_inputs():
        import jax
        import jax.numpy as jnp
        _gk = jax.random.key(seed)
        x = -0.000929 + 1 * jax.random.normal(jax.random.fold_in(_gk, 1), (2, 128, 32, 32), jnp.float32)
        return x
    x = _rec_inputs()

    def _L0_conv_setup():
        import jax, jax.numpy as jnp
        import numpy as np
        B, C, H, W = (2, 128, 32, 32)
        HEADS = 8
        GROUPS = 8
        DH = 16
        DF = 4
        OFF_SCALE = 4.0
        EPS = 1e-05

        def _bn(t, gamma, beta):
            s = gamma / jnp.sqrt(1.0 + EPS)
            return t * s[None, :, None, None] + beta[None, :, None, None]

        def _gconv1x1(t, w):
            b, c, h, ww = t.shape
            o = jnp.einsum('bgci,goc->bgoi', t.reshape(b, GROUPS, c // GROUPS, h * ww), w)
            return o.reshape(b, GROUPS * w.shape[1], h, ww)

        def _grid_sample(img, grid):
            N, Ci, Hi, Wi = img.shape
            gx = (grid[..., 0] + 1.0) * (Wi / 2.0) - 0.5
            gy = (grid[..., 1] + 1.0) * (Hi / 2.0) - 0.5
            x0 = jnp.floor(gx)
            y0 = jnp.floor(gy)
            wx = gx - x0
            wy = gy - y0

            def gather(im, ix, iy):
                valid = (ix >= 0) & (ix < Wi) & (iy >= 0) & (iy < Hi)
                ixc = jnp.clip(ix, 0, Wi - 1).astype(jnp.int32)
                iyc = jnp.clip(iy, 0, Hi - 1).astype(jnp.int32)
                return im[:, iyc, ixc] * valid[None].astype(im.dtype)

            def sample_one(im, x0, y0, wx, wy):
                v00 = gather(im, x0, y0)
                v01 = gather(im, x0 + 1, y0)
                v10 = gather(im, x0, y0 + 1)
                v11 = gather(im, x0 + 1, y0 + 1)
                wx = wx[None]
                wy = wy[None]
                return v00 * (1 - wx) * (1 - wy) + v01 * wx * (1 - wy) + v10 * (1 - wx) * wy + v11 * wx * wy
            return jax.vmap(sample_one)(img, x0, y0, wx, wy)

        def _forward(x, bn1_g, bn1_b, bn2_g, bn2_b, qw, kw, vw, out_w, out_b, off_dw_w, off_dw_b, off_pw_w, cpb_w1, cpb_b1, cpb_w2, cpb_b2, cpb_w3, cpb_b3, mlp_w1, mlp_b1, mlp_w2, mlp_b2):
            b = x.shape[0]
            xn = _bn(x, bn1_g, bn1_b)
            q = _gconv1x1(xn, qw)
            qg = q.reshape(b * GROUPS, DH, H, W)
            off = jax.lax.conv_general_dilated(qg, off_dw_w, (DF, DF), ((1, 1), (1, 1)), dimension_numbers=('NCHW', 'OIHW', 'NCHW'), feature_group_count=DH)
            off = jax.nn.gelu(off + off_dw_b[None, :, None, None], approximate=False)
            off = jnp.tanh(jnp.einsum('bchw,oc->bohw', off, off_pw_w)) * OFF_SCALE
            Hd, Wd = (off.shape[-2], off.shape[-1])
            gy, gx = jnp.meshgrid(jnp.arange(Hd, dtype=x.dtype), jnp.arange(Wd, dtype=x.dtype), indexing='ij')
            vx = gx[None] + off[:, 0]
            vy = gy[None] + off[:, 1]
            nx = 2.0 * vx / max(Hd - 1, 1) - 1.0
            ny = 2.0 * vy / max(Wd - 1, 1) - 1.0
            vgrid_scaled = jnp.stack((nx, ny), axis=-1)
            kv = _grid_sample(xn.reshape(b * GROUPS, DH, H, W), vgrid_scaled)
            kv = kv.reshape(b, GROUPS * DH, Hd, Wd)
            k = _gconv1x1(kv, kw)
            v = _gconv1x1(kv, vw)
            scale = DH ** (-0.5)
            qh = q.reshape(b, HEADS, DH, H * W).transpose(0, 1, 3, 2) * scale
            kh = k.reshape(b, HEADS, DH, Hd * Wd).transpose(0, 1, 3, 2)
            vh = v.reshape(b, HEADS, DH, Hd * Wd).transpose(0, 1, 3, 2)
            qgy, qgx = jnp.meshgrid(jnp.arange(H, dtype=x.dtype), jnp.arange(W, dtype=x.dtype), indexing='ij')
            grid_q = jnp.stack((2.0 * qgx / max(H - 1, 1) - 1.0, 2.0 * qgy / max(W - 1, 1) - 1.0), axis=-1).reshape(1, H * W, 2)
            grid_kv = vgrid_scaled.reshape(b * GROUPS, Hd * Wd, 2)
            pos = grid_q[:, :, None, :] - grid_kv[:, None, :, :]
            bias = jnp.sign(pos) * jnp.log1p(jnp.abs(pos))
            bias = jax.nn.relu(bias @ cpb_w1 + cpb_b1)
            bias = jax.nn.relu(bias @ cpb_w2 + cpb_b2)
            bias = (bias @ cpb_w3 + cpb_b3).reshape(b, GROUPS, H * W, Hd * Wd)
            sim = jnp.einsum('bhid,bhjd->bhij', qh, kh) + bias
            attn = jax.nn.softmax(sim, axis=-1)
            out = jnp.einsum('bhij,bhjd->bhid', attn, vh)
            out = out.transpose(0, 1, 3, 2).reshape(b, HEADS * DH, H, W)
            out = jnp.einsum('bchw,oc->bohw', out, out_w) + out_b[None, :, None, None]
            x = x + out
            xn2 = _bn(x, bn2_g, bn2_b)
            h1 = jax.nn.gelu(jnp.einsum('bchw,oc->bohw', xn2, mlp_w1) + mlp_b1[None, :, None, None], approximate=False)
            return x + jnp.einsum('bchw,oc->bohw', h1, mlp_w2) + mlp_b2[None, :, None, None]
        ks = jax.random.split(jax.random.key(seed), 16)
        w = lambda k, shape: jax.random.normal(k, shape, dtype=jnp.float32) * 0.02
        return {'x': jax.random.normal(ks[0], (B, C, H, W), dtype=jnp.float32), 'bn1_g': jnp.ones((C,), jnp.float32), 'bn1_b': jnp.zeros((C,), jnp.float32), 'bn2_g': jnp.ones((C,), jnp.float32), 'bn2_b': jnp.zeros((C,), jnp.float32), 'qw': w(ks[1], (GROUPS, DH, C // GROUPS)), 'kw': w(ks[2], (GROUPS, DH, C // GROUPS)), 'vw': w(ks[3], (GROUPS, DH, C // GROUPS)), 'out_w': w(ks[4], (C, HEADS * DH)), 'out_b': jnp.zeros((C,), jnp.float32), 'off_dw_w': w(ks[5], (DH, 1, 6, 6)), 'off_dw_b': jnp.zeros((DH,), jnp.float32), 'off_pw_w': w(ks[6], (2, DH)), 'cpb_w1': w(ks[7], (2, 32)), 'cpb_b1': jnp.zeros((32,), jnp.float32), 'cpb_w2': w(ks[8], (32, 32)), 'cpb_b2': jnp.zeros((32,), jnp.float32), 'cpb_w3': w(ks[9], (32, 1)), 'cpb_b3': jnp.zeros((1,), jnp.float32), 'mlp_w1': w(ks[10], (4 * C, C)), 'mlp_b1': jnp.zeros((4 * C,), jnp.float32), 'mlp_w2': w(ks[11], (C, 4 * C)), 'mlp_b2': jnp.zeros((C,), jnp.float32)}
    _L0_conv_all = _L0_conv_setup()
    _L0_conv_in = {k: v for k, v in _L0_conv_all.items() if k in ('bn1_g', 'bn1_b', 'bn2_g', 'bn2_b', 'qw', 'kw', 'vw', 'out_w', 'out_b', 'off_dw_w', 'off_dw_b', 'off_pw_w', 'cpb_w1', 'cpb_b1', 'cpb_w2', 'cpb_b2', 'cpb_w3', 'cpb_b3', 'mlp_w1', 'mlp_b1', 'mlp_w2', 'mlp_b2')}
    del _L0_conv_all

    def _L1_conv_setup():
        import jax, jax.numpy as jnp
        import numpy as np
        B, C, H, W = (2, 128, 16, 16)
        G = 32
        EPS = 1e-06
        key = jax.random.key(seed)
        ks = jax.random.split(key, 10)
        s = 1.0 / np.sqrt(C)
        return {'x': jax.random.normal(ks[0], (B, C, H, W), dtype=jnp.float32), 'gn_w': jnp.ones((C,), jnp.float32), 'gn_b': jnp.zeros((C,), jnp.float32), 'wq': jax.random.normal(ks[1], (C, C), jnp.float32) * s, 'bq': jnp.zeros((C,), jnp.float32), 'wk': jax.random.normal(ks[2], (C, C), jnp.float32) * s, 'bk': jnp.zeros((C,), jnp.float32), 'wv': jax.random.normal(ks[3], (C, C), jnp.float32) * s, 'bv': jnp.zeros((C,), jnp.float32), 'wo': jax.random.normal(ks[4], (C, C), jnp.float32) * s, 'bo': jnp.zeros((C,), jnp.float32)}
    _L1_conv_all = _L1_conv_setup()
    _L1_conv_in = {k: v for k, v in _L1_conv_all.items() if k in ('gn_w', 'gn_b', 'wq', 'bq', 'wk', 'bk', 'wv', 'bv', 'wo', 'bo')}
    del _L1_conv_all

    def _L2_attn_setup():
        import jax, jax.numpy as jnp
        import numpy as np
        HEADS = 8
        DIM_HEAD = 16
        MAX_POS = 128
        SCALE = DIM_HEAD ** (-0.5)
        key = jax.random.key(seed)
        ks = jax.random.split(key, 4)
        b, n, dim = (32, 128, 128)
        x = jax.random.normal(ks[0], (b, n, dim), dtype=jnp.float32)
        W_qkv = jax.random.normal(ks[1], (dim, 3 * HEADS * DIM_HEAD), dtype=jnp.float32) * dim ** (-0.5)
        rel_table = jax.random.normal(ks[2], (2 * MAX_POS + 1, DIM_HEAD), dtype=jnp.float32) * 0.02
        W_out = jax.random.normal(ks[3], (HEADS * DIM_HEAD, dim), dtype=jnp.float32) * (HEADS * DIM_HEAD) ** (-0.5)
        b_out = jnp.zeros((dim,), dtype=jnp.float32)
        return {'x': x, 'W_qkv': W_qkv, 'rel_table': rel_table, 'W_out': W_out, 'b_out': b_out}
    _L2_attn_all = _L2_attn_setup()
    _L2_attn_in = {k: v for k, v in _L2_attn_all.items() if k in ('W_qkv', 'rel_table', 'W_out', 'b_out')}
    del _L2_attn_all

    def _L2_ffn_setup():
        import jax, jax.numpy as jnp
        import numpy as np
        STEP_SIZE = 0.1

        def _mlp(y, W1, b1, W2, b2, W3, b3):
            h = jnp.tanh(y @ W1.T + b1)
            h = jnp.tanh(h @ W2.T + b2)
            return h @ W3.T + b3

        def _rk4_step(y, dt, params):
            f = lambda z: _mlp(z, *params)
            k1 = f(y)
            k2 = f(y + dt / 2 * k1)
            k3 = f(y + dt / 2 * k2)
            k4 = f(y + dt * k3)
            return y + dt * (k1 + 2 * k2 + 2 * k3 + k4) / 6
        key = jax.random.key(seed)
        ks = jax.random.split(key, 7)
        B, S, D, H = (64, 16, 128, 512)
        return {'x': jax.random.normal(ks[0], (B, S, D), dtype=jnp.float32), 'W1': jax.random.normal(ks[1], (H, D), dtype=jnp.float32) * (1.0 / np.sqrt(D)), 'b1': jax.random.normal(ks[2], (H,), dtype=jnp.float32) * 0.01, 'W2': jax.random.normal(ks[3], (H, H), dtype=jnp.float32) * (1.0 / np.sqrt(H)), 'b2': jax.random.normal(ks[4], (H,), dtype=jnp.float32) * 0.01, 'W3': jax.random.normal(ks[5], (D, H), dtype=jnp.float32) * (1.0 / np.sqrt(H)), 'b3': jax.random.normal(ks[6], (D,), dtype=jnp.float32) * 0.01}
    _L2_ffn_all = _L2_ffn_setup()
    _L2_ffn_in = {k: v for k, v in _L2_ffn_all.items() if k in ('W1', 'b1', 'W2', 'b2', 'W3', 'b3')}
    del _L2_ffn_all

    def _L3_attn_setup():
        import jax, jax.numpy as jnp
        import numpy as np
        B, T, D, H = (8, 2048, 128, 4)
        DK, DV = (64, 128)
        HK, HV = (DK // H, DV // H)
        C = 16
        LOW = 16
        GATE_NORM = 16.0
        EPS = 1e-05

        def _gla_forward(x, Wq, Wk, Wv, Wg, Wgk1, Wgk2, bgk2, g_norm_w, Wo):
            b, t, _ = x.shape
            n = t // C
            scale = HK ** (-0.5)
            q = x @ Wq.T
            k = x @ Wk.T
            v = x @ Wv.T
            g = x @ Wg.T
            gk = jax.nn.log_sigmoid(x @ Wgk1.T @ Wgk2.T + bgk2) / GATE_NORM

            def to_chunks(tensor, hd):
                return tensor.reshape(b, n, C, H, hd).transpose(1, 0, 3, 2, 4)
            qc = to_chunks(q, HK)
            kc = to_chunks(k, HK)
            vc = to_chunks(v, HV)
            bc = jnp.cumsum(to_chunks(gk, HK), axis=3)
            mask = jnp.tril(jnp.ones((C, C), bool))

            def chunk_step(S, xs):
                qi, ki, vi, bi = xs
                eb = jnp.exp(bi)
                q_e = qi * eb * scale
                k_e = ki * jnp.exp(-bi)
                A = jnp.einsum('bhcd,bhed->bhce', q_e, k_e)
                A = jnp.where(mask, A, 0.0)
                o = jnp.einsum('bhce,bhev->bhcv', A, vi) + jnp.einsum('bhcd,bhdv->bhcv', q_e, S)
                b_last = bi[:, :, -1:, :]
                k_dec = ki * jnp.exp(b_last - bi)
                S_new = jnp.exp(b_last[:, :, 0, :])[..., None] * S + jnp.einsum('bhcd,bhcv->bhdv', k_dec, vi)
                return (S_new, o)
            S0 = jnp.zeros((b, H, HK, HV), x.dtype)
            _, o = jax.lax.scan(chunk_step, S0, (qc, kc, vc, bc))
            o = o.transpose(1, 0, 3, 2, 4).reshape(b, t, H, HV)
            gh = g.reshape(b, t, H, HV)
            rms = jax.lax.rsqrt(jnp.mean(o * o, axis=-1, keepdims=True) + EPS)
            o = o * rms * g_norm_w * (gh * jax.nn.sigmoid(gh))
            return o.reshape(b, t, DV) @ Wo.T
        key = jax.random.key(seed)
        ks = jax.random.split(key, 8)
        s = 0.02
        return {'x': jax.random.normal(ks[0], (B, T, D), jnp.float32), 'Wq': jax.random.normal(ks[1], (DK, D), jnp.float32) * s, 'Wk': jax.random.normal(ks[2], (DK, D), jnp.float32) * s, 'Wv': jax.random.normal(ks[3], (DV, D), jnp.float32) * s, 'Wg': jax.random.normal(ks[4], (DV, D), jnp.float32) * s, 'Wgk1': jax.random.normal(ks[5], (LOW, D), jnp.float32) * s, 'Wgk2': jax.random.normal(ks[6], (DK, LOW), jnp.float32) * s, 'bgk2': jnp.zeros((DK,), jnp.float32), 'g_norm_w': jnp.ones((HV,), jnp.float32), 'Wo': jax.random.normal(ks[7], (D, D), jnp.float32) * s}
    _L3_attn_all = _L3_attn_setup()
    _L3_attn_in = {k: v for k, v in _L3_attn_all.items() if k in ('Wq', 'Wk', 'Wv', 'Wg', 'Wgk1', 'Wgk2', 'bgk2', 'g_norm_w', 'Wo')}
    del _L3_attn_all

    def _L3_ffn_setup():
        import jax, jax.numpy as jnp
        import numpy as np
        TOP_K = 2
        key = jax.random.key(seed)
        k1, k2, k3, k4 = jax.random.split(key, 4)
        B, S, d = (4, 512, 128)
        E, H = (32, 32)
        x = jax.random.normal(k1, (B, S, d), dtype=jnp.float32)
        expert_sel = jax.random.normal(k2, (E, d), dtype=jnp.float32) / np.sqrt(d).astype(np.float32)
        keys = jax.random.normal(k3, (E, d, H), dtype=jnp.float32) / np.sqrt(d).astype(np.float32)
        values = jax.random.normal(k4, (E, H, d), dtype=jnp.float32) / np.sqrt(E * H).astype(np.float32)
        return {'x': x, 'expert_sel': expert_sel, 'keys': keys, 'values': values}
    _L3_ffn_all = _L3_ffn_setup()
    _L3_ffn_in = {k: v for k, v in _L3_ffn_all.items() if k in ('expert_sel', 'keys', 'values')}
    del _L3_ffn_all
    return {'x': x, 'L0_conv_bn1_g': _L0_conv_in['bn1_g'], 'L0_conv_bn1_b': _L0_conv_in['bn1_b'], 'L0_conv_bn2_g': _L0_conv_in['bn2_g'], 'L0_conv_bn2_b': _L0_conv_in['bn2_b'], 'L0_conv_qw': _L0_conv_in['qw'], 'L0_conv_kw': _L0_conv_in['kw'], 'L0_conv_vw': _L0_conv_in['vw'], 'L0_conv_out_w': _L0_conv_in['out_w'], 'L0_conv_out_b': _L0_conv_in['out_b'], 'L0_conv_off_dw_w': _L0_conv_in['off_dw_w'], 'L0_conv_off_dw_b': _L0_conv_in['off_dw_b'], 'L0_conv_off_pw_w': _L0_conv_in['off_pw_w'], 'L0_conv_cpb_w1': _L0_conv_in['cpb_w1'], 'L0_conv_cpb_b1': _L0_conv_in['cpb_b1'], 'L0_conv_cpb_w2': _L0_conv_in['cpb_w2'], 'L0_conv_cpb_b2': _L0_conv_in['cpb_b2'], 'L0_conv_cpb_w3': _L0_conv_in['cpb_w3'], 'L0_conv_cpb_b3': _L0_conv_in['cpb_b3'], 'L0_conv_mlp_w1': _L0_conv_in['mlp_w1'], 'L0_conv_mlp_b1': _L0_conv_in['mlp_b1'], 'L0_conv_mlp_w2': _L0_conv_in['mlp_w2'], 'L0_conv_mlp_b2': _L0_conv_in['mlp_b2'], 'L1_conv_gn_w': _L1_conv_in['gn_w'], 'L1_conv_gn_b': _L1_conv_in['gn_b'], 'L1_conv_wq': _L1_conv_in['wq'], 'L1_conv_bq': _L1_conv_in['bq'], 'L1_conv_wk': _L1_conv_in['wk'], 'L1_conv_bk': _L1_conv_in['bk'], 'L1_conv_wv': _L1_conv_in['wv'], 'L1_conv_bv': _L1_conv_in['bv'], 'L1_conv_wo': _L1_conv_in['wo'], 'L1_conv_bo': _L1_conv_in['bo'], 'L2_attn_W_qkv': _L2_attn_in['W_qkv'], 'L2_attn_rel_table': _L2_attn_in['rel_table'], 'L2_attn_W_out': _L2_attn_in['W_out'], 'L2_attn_b_out': _L2_attn_in['b_out'], 'L2_ffn_W1': _L2_ffn_in['W1'], 'L2_ffn_b1': _L2_ffn_in['b1'], 'L2_ffn_W2': _L2_ffn_in['W2'], 'L2_ffn_b2': _L2_ffn_in['b2'], 'L2_ffn_W3': _L2_ffn_in['W3'], 'L2_ffn_b3': _L2_ffn_in['b3'], 'L3_attn_Wq': _L3_attn_in['Wq'], 'L3_attn_Wk': _L3_attn_in['Wk'], 'L3_attn_Wv': _L3_attn_in['Wv'], 'L3_attn_Wg': _L3_attn_in['Wg'], 'L3_attn_Wgk1': _L3_attn_in['Wgk1'], 'L3_attn_Wgk2': _L3_attn_in['Wgk2'], 'L3_attn_bgk2': _L3_attn_in['bgk2'], 'L3_attn_g_norm_w': _L3_attn_in['g_norm_w'], 'L3_attn_Wo': _L3_attn_in['Wo'], 'L3_ffn_expert_sel': _L3_ffn_in['expert_sel'], 'L3_ffn_keys': _L3_ffn_in['keys'], 'L3_ffn_values': _L3_ffn_in['values']}

def reference(x, L0_conv_bn1_g, L0_conv_bn1_b, L0_conv_bn2_g, L0_conv_bn2_b, L0_conv_qw, L0_conv_kw, L0_conv_vw, L0_conv_out_w, L0_conv_out_b, L0_conv_off_dw_w, L0_conv_off_dw_b, L0_conv_off_pw_w, L0_conv_cpb_w1, L0_conv_cpb_b1, L0_conv_cpb_w2, L0_conv_cpb_b2, L0_conv_cpb_w3, L0_conv_cpb_b3, L0_conv_mlp_w1, L0_conv_mlp_b1, L0_conv_mlp_w2, L0_conv_mlp_b2, L1_conv_gn_w, L1_conv_gn_b, L1_conv_wq, L1_conv_bq, L1_conv_wk, L1_conv_bk, L1_conv_wv, L1_conv_bv, L1_conv_wo, L1_conv_bo, L2_attn_W_qkv, L2_attn_rel_table, L2_attn_W_out, L2_attn_b_out, L2_ffn_W1, L2_ffn_b1, L2_ffn_W2, L2_ffn_b2, L2_ffn_W3, L2_ffn_b3, L3_attn_Wq, L3_attn_Wk, L3_attn_Wv, L3_attn_Wg, L3_attn_Wgk1, L3_attn_Wgk2, L3_attn_bgk2, L3_attn_g_norm_w, L3_attn_Wo, L3_ffn_expert_sel, L3_ffn_keys, L3_ffn_values):
    import jax
    import jax.numpy as jnp

    def _L0_conv_ref(x, bn1_g, bn1_b, bn2_g, bn2_b, qw, kw, vw, out_w, out_b, off_dw_w, off_dw_b, off_pw_w, cpb_w1, cpb_b1, cpb_w2, cpb_b2, cpb_w3, cpb_b3, mlp_w1, mlp_b1, mlp_w2, mlp_b2):
        import jax, jax.numpy as jnp
        import numpy as np
        B, C, H, W = (2, 128, 32, 32)
        HEADS = 8
        GROUPS = 8
        DH = 16
        DF = 4
        OFF_SCALE = 4.0
        EPS = 1e-05

        def _bn(t, gamma, beta):
            s = gamma / jnp.sqrt(1.0 + EPS)
            return t * s[None, :, None, None] + beta[None, :, None, None]

        def _gconv1x1(t, w):
            b, c, h, ww = t.shape
            o = jnp.einsum('bgci,goc->bgoi', t.reshape(b, GROUPS, c // GROUPS, h * ww), w)
            return o.reshape(b, GROUPS * w.shape[1], h, ww)

        def _grid_sample(img, grid):
            N, Ci, Hi, Wi = img.shape
            gx = (grid[..., 0] + 1.0) * (Wi / 2.0) - 0.5
            gy = (grid[..., 1] + 1.0) * (Hi / 2.0) - 0.5
            x0 = jnp.floor(gx)
            y0 = jnp.floor(gy)
            wx = gx - x0
            wy = gy - y0

            def gather(im, ix, iy):
                valid = (ix >= 0) & (ix < Wi) & (iy >= 0) & (iy < Hi)
                ixc = jnp.clip(ix, 0, Wi - 1).astype(jnp.int32)
                iyc = jnp.clip(iy, 0, Hi - 1).astype(jnp.int32)
                return im[:, iyc, ixc] * valid[None].astype(im.dtype)

            def sample_one(im, x0, y0, wx, wy):
                v00 = gather(im, x0, y0)
                v01 = gather(im, x0 + 1, y0)
                v10 = gather(im, x0, y0 + 1)
                v11 = gather(im, x0 + 1, y0 + 1)
                wx = wx[None]
                wy = wy[None]
                return v00 * (1 - wx) * (1 - wy) + v01 * wx * (1 - wy) + v10 * (1 - wx) * wy + v11 * wx * wy
            return jax.vmap(sample_one)(img, x0, y0, wx, wy)

        def _forward(x, bn1_g, bn1_b, bn2_g, bn2_b, qw, kw, vw, out_w, out_b, off_dw_w, off_dw_b, off_pw_w, cpb_w1, cpb_b1, cpb_w2, cpb_b2, cpb_w3, cpb_b3, mlp_w1, mlp_b1, mlp_w2, mlp_b2):
            b = x.shape[0]
            xn = _bn(x, bn1_g, bn1_b)
            q = _gconv1x1(xn, qw)
            qg = q.reshape(b * GROUPS, DH, H, W)
            off = jax.lax.conv_general_dilated(qg, off_dw_w, (DF, DF), ((1, 1), (1, 1)), dimension_numbers=('NCHW', 'OIHW', 'NCHW'), feature_group_count=DH)
            off = jax.nn.gelu(off + off_dw_b[None, :, None, None], approximate=False)
            off = jnp.tanh(jnp.einsum('bchw,oc->bohw', off, off_pw_w)) * OFF_SCALE
            Hd, Wd = (off.shape[-2], off.shape[-1])
            gy, gx = jnp.meshgrid(jnp.arange(Hd, dtype=x.dtype), jnp.arange(Wd, dtype=x.dtype), indexing='ij')
            vx = gx[None] + off[:, 0]
            vy = gy[None] + off[:, 1]
            nx = 2.0 * vx / max(Hd - 1, 1) - 1.0
            ny = 2.0 * vy / max(Wd - 1, 1) - 1.0
            vgrid_scaled = jnp.stack((nx, ny), axis=-1)
            kv = _grid_sample(xn.reshape(b * GROUPS, DH, H, W), vgrid_scaled)
            kv = kv.reshape(b, GROUPS * DH, Hd, Wd)
            k = _gconv1x1(kv, kw)
            v = _gconv1x1(kv, vw)
            scale = DH ** (-0.5)
            qh = q.reshape(b, HEADS, DH, H * W).transpose(0, 1, 3, 2) * scale
            kh = k.reshape(b, HEADS, DH, Hd * Wd).transpose(0, 1, 3, 2)
            vh = v.reshape(b, HEADS, DH, Hd * Wd).transpose(0, 1, 3, 2)
            qgy, qgx = jnp.meshgrid(jnp.arange(H, dtype=x.dtype), jnp.arange(W, dtype=x.dtype), indexing='ij')
            grid_q = jnp.stack((2.0 * qgx / max(H - 1, 1) - 1.0, 2.0 * qgy / max(W - 1, 1) - 1.0), axis=-1).reshape(1, H * W, 2)
            grid_kv = vgrid_scaled.reshape(b * GROUPS, Hd * Wd, 2)
            pos = grid_q[:, :, None, :] - grid_kv[:, None, :, :]
            bias = jnp.sign(pos) * jnp.log1p(jnp.abs(pos))
            bias = jax.nn.relu(bias @ cpb_w1 + cpb_b1)
            bias = jax.nn.relu(bias @ cpb_w2 + cpb_b2)
            bias = (bias @ cpb_w3 + cpb_b3).reshape(b, GROUPS, H * W, Hd * Wd)
            sim = jnp.einsum('bhid,bhjd->bhij', qh, kh) + bias
            attn = jax.nn.softmax(sim, axis=-1)
            out = jnp.einsum('bhij,bhjd->bhid', attn, vh)
            out = out.transpose(0, 1, 3, 2).reshape(b, HEADS * DH, H, W)
            out = jnp.einsum('bchw,oc->bohw', out, out_w) + out_b[None, :, None, None]
            x = x + out
            xn2 = _bn(x, bn2_g, bn2_b)
            h1 = jax.nn.gelu(jnp.einsum('bchw,oc->bohw', xn2, mlp_w1) + mlp_b1[None, :, None, None], approximate=False)
            return x + jnp.einsum('bchw,oc->bohw', h1, mlp_w2) + mlp_b2[None, :, None, None]
        return _forward(x, bn1_g, bn1_b, bn2_g, bn2_b, qw, kw, vw, out_w, out_b, off_dw_w, off_dw_b, off_pw_w, cpb_w1, cpb_b1, cpb_w2, cpb_b2, cpb_w3, cpb_b3, mlp_w1, mlp_b1, mlp_w2, mlp_b2)

    def _L1_conv_ref(x, gn_w, gn_b, wq, bq, wk, bk, wv, bv, wo, bo):
        import jax, jax.numpy as jnp
        import numpy as np
        B, C, H, W = (2, 128, 16, 16)
        G = 32
        EPS = 1e-06
        b, c, h, w = x.shape
        n = h * w
        xg = x.reshape(b, G, c // G, h, w)
        mu = xg.mean(axis=(2, 3, 4), keepdims=True)
        var = ((xg - mu) ** 2).mean(axis=(2, 3, 4), keepdims=True)
        hn = ((xg - mu) * jax.lax.rsqrt(var + EPS)).reshape(b, c, h, w)
        hn = hn * gn_w[None, :, None, None] + gn_b[None, :, None, None]
        hf = hn.reshape(b, c, n)
        q = jnp.einsum('oc,bcn->bno', wq, hf) + bq
        k = jnp.einsum('oc,bcn->bno', wk, hf) + bk
        v = jnp.einsum('oc,bcn->bno', wv, hf) + bv
        scale = jnp.asarray(c, x.dtype) ** (-0.5)
        att = jax.nn.softmax(jnp.einsum('bic,bjc->bij', q, k) * scale, axis=-1)
        o = jnp.einsum('bij,bjc->bic', att, v)
        out = jnp.einsum('oc,bnc->bno', wo, o) + bo
        return x + out.transpose(0, 2, 1).reshape(b, c, h, w)

    def _L2_attn_ref(x, W_qkv, rel_table, W_out, b_out):
        import jax, jax.numpy as jnp
        import numpy as np
        HEADS = 8
        DIM_HEAD = 16
        MAX_POS = 128
        SCALE = DIM_HEAD ** (-0.5)
        b, n, dim = x.shape
        qkv = x @ W_qkv
        q, k, v = jnp.split(qkv, 3, axis=-1)

        def heads(t):
            return t.reshape(b, n, HEADS, DIM_HEAD).transpose(0, 2, 1, 3)
        q, k, v = (heads(q), heads(k), heads(v))
        dots = jnp.einsum('bhid,bhjd->bhij', q, k) * SCALE
        seq = jnp.arange(n)
        dist = jnp.clip(seq[:, None] - seq[None, :], -MAX_POS, MAX_POS) + MAX_POS
        rel = rel_table[dist]
        pos_attn = jnp.einsum('bhnd,nrd->bhnr', q, rel) * SCALE
        dots = dots + pos_attn
        attn = jax.nn.softmax(dots.astype(jnp.float32), axis=-1).astype(q.dtype)
        out = jnp.einsum('bhij,bhjd->bhid', attn, v)
        out = out.transpose(0, 2, 1, 3).reshape(b, n, HEADS * DIM_HEAD)
        return out @ W_out + b_out

    def _L2_ffn_ref(x, W1, b1, W2, b2, W3, b3):
        import jax, jax.numpy as jnp
        import numpy as np
        STEP_SIZE = 0.1

        def _mlp(y, W1, b1, W2, b2, W3, b3):
            h = jnp.tanh(y @ W1.T + b1)
            h = jnp.tanh(h @ W2.T + b2)
            return h @ W3.T + b3

        def _rk4_step(y, dt, params):
            f = lambda z: _mlp(z, *params)
            k1 = f(y)
            k2 = f(y + dt / 2 * k1)
            k3 = f(y + dt / 2 * k2)
            k4 = f(y + dt * k3)
            return y + dt * (k1 + 2 * k2 + 2 * k3 + k4) / 6
        B, S, D = x.shape
        params = (W1, b1, W2, b2, W3, b3)
        span = 1.0 / (S - 1)
        steps = max(1, int(span / STEP_SIZE))
        dt = span / steps

        def interval(y, _):
            for _s in range(steps):
                y = _rk4_step(y, dt, params)
            return (y, y)
        y0 = x[:, 0]
        _, ys = jax.lax.scan(interval, y0, None, length=S - 1)
        return jnp.concatenate([y0[:, None], jnp.moveaxis(ys, 0, 1)], axis=1)

    def _L3_attn_ref(x, Wq, Wk, Wv, Wg, Wgk1, Wgk2, bgk2, g_norm_w, Wo):
        import jax, jax.numpy as jnp
        import numpy as np
        B, T, D, H = (8, 2048, 128, 4)
        DK, DV = (64, 128)
        HK, HV = (DK // H, DV // H)
        C = 16
        LOW = 16
        GATE_NORM = 16.0
        EPS = 1e-05

        def _gla_forward(x, Wq, Wk, Wv, Wg, Wgk1, Wgk2, bgk2, g_norm_w, Wo):
            b, t, _ = x.shape
            n = t // C
            scale = HK ** (-0.5)
            q = x @ Wq.T
            k = x @ Wk.T
            v = x @ Wv.T
            g = x @ Wg.T
            gk = jax.nn.log_sigmoid(x @ Wgk1.T @ Wgk2.T + bgk2) / GATE_NORM

            def to_chunks(tensor, hd):
                return tensor.reshape(b, n, C, H, hd).transpose(1, 0, 3, 2, 4)
            qc = to_chunks(q, HK)
            kc = to_chunks(k, HK)
            vc = to_chunks(v, HV)
            bc = jnp.cumsum(to_chunks(gk, HK), axis=3)
            mask = jnp.tril(jnp.ones((C, C), bool))

            def chunk_step(S, xs):
                qi, ki, vi, bi = xs
                eb = jnp.exp(bi)
                q_e = qi * eb * scale
                k_e = ki * jnp.exp(-bi)
                A = jnp.einsum('bhcd,bhed->bhce', q_e, k_e)
                A = jnp.where(mask, A, 0.0)
                o = jnp.einsum('bhce,bhev->bhcv', A, vi) + jnp.einsum('bhcd,bhdv->bhcv', q_e, S)
                b_last = bi[:, :, -1:, :]
                k_dec = ki * jnp.exp(b_last - bi)
                S_new = jnp.exp(b_last[:, :, 0, :])[..., None] * S + jnp.einsum('bhcd,bhcv->bhdv', k_dec, vi)
                return (S_new, o)
            S0 = jnp.zeros((b, H, HK, HV), x.dtype)
            _, o = jax.lax.scan(chunk_step, S0, (qc, kc, vc, bc))
            o = o.transpose(1, 0, 3, 2, 4).reshape(b, t, H, HV)
            gh = g.reshape(b, t, H, HV)
            rms = jax.lax.rsqrt(jnp.mean(o * o, axis=-1, keepdims=True) + EPS)
            o = o * rms * g_norm_w * (gh * jax.nn.sigmoid(gh))
            return o.reshape(b, t, DV) @ Wo.T
        return _gla_forward(x, Wq, Wk, Wv, Wg, Wgk1, Wgk2, bgk2, g_norm_w, Wo)

    def _L3_ffn_ref(x, expert_sel, keys, values):
        import jax, jax.numpy as jnp
        import numpy as np
        TOP_K = 2
        B, S, d = x.shape
        E = keys.shape[0]
        xt = x.reshape(-1, d)
        T = xt.shape[0]
        sel = jax.nn.sigmoid(xt @ expert_sel.T)
        sel_val, sel_idx = jax.lax.top_k(sel, TOP_K)
        w = jnp.zeros((T, E), dtype=xt.dtype).at[jnp.arange(T)[:, None], sel_idx].add(sel_val)
        h = jax.nn.relu(jnp.einsum('td,edh->teh', xt, keys))
        out = jnp.einsum('teh,te,ehv->tv', h, w, values)
        return out.reshape(B, S, -1)

    def _gn(v, G=32, eps=1e-05):
        B_, C_, H_, W_ = v.shape
        g = v.reshape(B_, G, C_ // G, H_, W_)
        m = jnp.mean(g, axis=(2, 3, 4), keepdims=True)
        s = jnp.var(g, axis=(2, 3, 4), keepdims=True)
        return ((g - m) / jnp.sqrt(s + eps)).reshape(v.shape)

    def _ln_c(v, eps=1e-06):
        m = jnp.mean(v, axis=1, keepdims=True)
        s = jnp.var(v, axis=1, keepdims=True)
        return (v - m) / jnp.sqrt(s + eps)

    def _ln_t(v, eps=1e-05):
        m = jnp.mean(v, axis=-1, keepdims=True)
        s = jnp.var(v, axis=-1, keepdims=True)
        return (v - m) / jnp.sqrt(s + eps)

    def _to_tokens(v):
        B_, C_, H_, W_ = v.shape
        return v.reshape(B_, C_, H_ * W_).transpose(0, 2, 1)

    def _from_tokens(t, like):
        B_, C_, H_, W_ = like.shape
        return t.transpose(0, 2, 1).reshape(B_, C_, H_, W_)
    x = _L0_conv_ref(x, L0_conv_bn1_g, L0_conv_bn1_b, L0_conv_bn2_g, L0_conv_bn2_b, L0_conv_qw, L0_conv_kw, L0_conv_vw, L0_conv_out_w, L0_conv_out_b, L0_conv_off_dw_w, L0_conv_off_dw_b, L0_conv_off_pw_w, L0_conv_cpb_w1, L0_conv_cpb_b1, L0_conv_cpb_w2, L0_conv_cpb_b2, L0_conv_cpb_w3, L0_conv_cpb_b3, L0_conv_mlp_w1, L0_conv_mlp_b1, L0_conv_mlp_w2, L0_conv_mlp_b2)
    x = _L1_conv_ref(x, L1_conv_gn_w, L1_conv_gn_b, L1_conv_wq, L1_conv_bq, L1_conv_wk, L1_conv_bk, L1_conv_wv, L1_conv_bv, L1_conv_wo, L1_conv_bo)
    t = _to_tokens(x)
    t = t + _L2_attn_ref(_ln_t(t), L2_attn_W_qkv, L2_attn_rel_table, L2_attn_W_out, L2_attn_b_out)
    t = t + _L2_ffn_ref(_ln_t(t), L2_ffn_W1, L2_ffn_b1, L2_ffn_W2, L2_ffn_b2, L2_ffn_W3, L2_ffn_b3)
    t = t + _L3_attn_ref(_ln_t(t), L3_attn_Wq, L3_attn_Wk, L3_attn_Wv, L3_attn_Wg, L3_attn_Wgk1, L3_attn_Wgk2, L3_attn_bgk2, L3_attn_g_norm_w, L3_attn_Wo)
    t = t + _L3_ffn_ref(_ln_t(t), L3_ffn_expert_sel, L3_ffn_keys, L3_ffn_values)
    x = _from_tokens(t, x)
    return x

_drawn_inputs = setup_inputs


def setup_inputs(seed=0):
    import zlib

    import numpy as np

    out = dict(_drawn_inputs(seed))
    spreads = {'L0_conv_bn1_g': (1.0, 0.6),
     'L0_conv_bn1_b': (0.0, 0.795),
     'L0_conv_bn2_g': (1.0, 0.6),
     'L0_conv_bn2_b': (0.0, 0.411),
     'L0_conv_out_b': (0.0, 0.1),
     'L0_conv_off_dw_b': (0.0, 0.8),
     'L0_conv_cpb_b1': (0.0, 2.0),
     'L0_conv_cpb_b2': (0.0, 2.0),
     'L0_conv_mlp_b1': (0.0, 0.1),
     'L0_conv_mlp_b2': (0.0, 0.1),
     'L1_conv_gn_w': (1.0, 0.2),
     'L1_conv_gn_b': (0.0, 0.1),
     'L1_conv_bq': (0.0, 0.326),
     'L1_conv_bk': (0.0, 2.0),
     'L1_conv_bv': (0.0, 0.1),
     'L1_conv_bo': (0.0, 0.1),
     'L2_attn_b_out': (0.0, 0.1),
     'L3_attn_bgk2': (0.0, 2.0),
     'L3_attn_g_norm_w': (1.0, 0.6)}
    factors = {'L0_conv_qw': 8.0,
     'L0_conv_kw': 8.0,
     'L0_conv_vw': 6.091,
     'L0_conv_out_w': 5.344,
     'L0_conv_off_dw_w': 8.0,
     'L0_conv_off_pw_w': 8.0,
     'L0_conv_cpb_w1': 40.463,
     'L0_conv_cpb_w2': 28.75,
     'L0_conv_cpb_w3': 32.666,
     'L2_attn_rel_table': 58.104,
     'L2_ffn_b1': 29.243,
     'L2_ffn_b2': 8.0,
     'L2_ffn_b3': 6.101,
     'L3_attn_Wgk1': 28.499,
     'L3_attn_Wgk2': 25.129}
    for name, (base, spread) in spreads.items():
        noise = np.random.default_rng([zlib.crc32(name.encode()), seed]).standard_normal(out[name].shape)
        drawn = base * np.exp(spread * noise) if base else spread * noise
        out[name] = jnp.asarray(drawn.astype(out[name].dtype))
    for name, factor in factors.items():
        out[name] = (out[name] * factor).astype(out[name].dtype)
    return out
```

```python
from contextlib import ExitStack

import numpy as np
import concourse.bass as bass
from concourse import mybir

F32 = mybir.dt.float32
I32 = mybir.dt.int32
ALU = mybir.AluOpType
ACT = mybir.ActivationFunctionType
AX = mybir.AxisListType

P = 128
NB = 2
PIX = 1024
T = NB * PIX
CH = 512
NCH = T // CH
BN_SCALE = float(1.0 / np.sqrt(np.float32(1.0 + 1e-5)))


class Stage:

    def __init__(self, nc, ctx):
        self.nc, self.ctx, self.sems = nc, ctx, {}
        ctx.callback(self.clear)

    def sb(self, name, shape, dt=F32):
        return self.ctx.enter_context(self.nc.sbuf_tensor(name, shape, dt))

    def sem(self, name):
        if name not in self.sems:
            self.sems[name] = self.nc.alloc_semaphore(name)
        return self.sems[name]

    def clear(self):
        with self.nc.Block() as block:
            @block.gpsimd
            def _(pool):
                for s in self.sems.values():
                    pool.sem_clear(s)
        for s in self.sems.values():
            self.nc.release_semaphore(s)


class Chain:

    def __init__(self, eng, sem):
        self.eng, self.sem, self.n = eng, sem, 0

    def __call__(self, ins):
        ins.then_inc(self.sem, 1)
        self.n += 1
        self.eng.wait_ge(self.sem, self.n)


def bc(ap, axis, n):
    shape = list(ap.shape)
    ap = ap.unsqueeze(axis)
    shape.insert(axis, n)
    return ap.broadcast_to(shape)


class Pack:
    def __init__(self):
        self.parts, self.at, self.n = [], {}, 0

    def add(self, name, a):
        a = a.reshape(a.shape[0], -1)
        full = np.zeros((P, a.shape[1]), np.float32)
        full[: a.shape[0]] = a
        self.at[name] = (self.n, a.shape[0], a.shape[1])
        self.parts.append(full)
        self.n += a.shape[1]

    def array(self):
        return np.ascontiguousarray(np.concatenate(self.parts, axis=1))


class Weights:

    def __init__(self, tile, at):
        self.tile, self.at = tile, at

    def __getitem__(self, name):
        c, rows, n = self.at[name]
        return self.tile[0:rows, c:c + n]


HEADS = 8
DH = 16
HW = 32
HK = 8
KEYS = HK * HK
TAPS = 36
PADW = HW + 2
HID = 32
PAIRS = HEADS // 2
BATCHES = 8
HALF = PIX // 2
GCOLS = NB * HEADS * KEYS


def block_diag(w):
    g, o, i = w.shape
    full = np.zeros((g * i, g * o), w.dtype)
    for n in range(g):
        full[n * i:(n + 1) * i, n * o:(n + 1) * o] = w[n].T
    return full


def l0_pack(w):
    p = Pack()
    L = lambda n: w["L0_conv_" + n]
    for n in ("bn1_g", "bn1_b", "bn2_g", "bn2_b", "out_b", "mlp_b2"):
        p.add(n, L(n).reshape(P, 1))
    p.add("off_dw_b", np.tile(L("off_dw_b"), HEADS).reshape(P, 1))
    p.add("off_dw_w", np.tile(L("off_dw_w").reshape(DH, TAPS), (HEADS, 1)))
    p.add("qw", block_diag(L("qw")))
    p.add("kw", block_diag(L("kw")))
    p.add("vw", block_diag(L("vw")))
    p.add("off_pw", np.repeat(np.tile(L("off_pw_w").T, (HEADS, 1))[:, :, None], P, axis=2))
    p.add("out_w", L("out_w").T)
    p.add("mlp_w1", L("mlp_w1").T)
    p.add("mlp_b1", L("mlp_b1").reshape(4, P).T)
    p.add("mlp_w2", L("mlp_w2").T.reshape(4, P, P).transpose(1, 0, 2))
    w1 = np.zeros((2, NB, HEADS, 4, HEADS, 4, HID), np.float32)
    for c in range(2):
        for g in range(HEADS):
            for t in range(4):
                w1[c, :, g, t, g, t] = L("cpb_w1")[c]
    p.add("cpb_w1", w1.reshape(P, HEADS * P))
    p.add("cpb_w2", block_diag(np.tile(L("cpb_w2").T[None], (4, 1, 1))))
    w3 = np.zeros((4, HID, BATCHES, HID), np.float32)
    for j in range(4):
        for n in range(BATCHES):
            w3[j, :, n, 4 * n + j] = L("cpb_w3")[:, 0]
    p.add("cpb_w3", w3.reshape(P, BATCHES * HID))
    p.add("cpb_b1", np.tile(L("cpb_b1"), 4).reshape(P, 1))
    p.add("cpb_b2", np.tile(L("cpb_b2"), 4).reshape(P, 1))
    p.add("cpb_b3", np.tile(L("cpb_b3"), P).reshape(P, 1))
    p.add("ident", np.eye(P, dtype=np.float32))
    p.add("gmask", np.repeat(np.eye(HEADS, dtype=np.float32), DH, axis=0))
    ar = np.arange(KEYS)
    p.add("kgrid", np.tile(np.stack([ar % HK, ar // HK]).astype(np.float32).reshape(1, 2 * KEYS), (P, 1)))
    cq = (np.float32(2.0) * np.arange(HW, dtype=np.float32) / np.float32(HW - 1) - np.float32(1.0)).astype(np.float32)
    p.add("qgrid", np.tile(cq.reshape(1, HW), (P, 1)))
    rows = np.arange(P)
    p.add("minus_x", -(rows % HW + 0.5).astype(np.float32).reshape(P, 1))
    p.add("minus_y", np.stack([-(4 * c + rows // HW + 0.5) for c in range(8)], axis=1).astype(np.float32))
    return p


def l0_prepare(nc, X, PS, W, loaded, KM, VT, Q, A, B, x_dram, wait_x):
    with ExitStack() as ctx:
        st = Stage(nc, ctx)
        sb, sem = st.sb, st.sem
        s1 = sb("l0_s1", [P, 1])
        XN = sb("l0_xn", [P, T])
        qpad = sb("l0_qpad", [P, NB, PADW, PADW])
        conv = sb("l0_conv", [P, NB, HK, HK])
        off = sb("l0_off", [P, NB, KEYS])
        offm = sb("l0_offm", [P, NB, HEADS, KEYS])
        V = sb("l0_v", [P, 2, NB * HEADS, KEYS])
        PX = sb("l0_px", [P, 2, GCOLS])
        hx = sb("l0_hx", [P, GCOLS])
        hy = sb("l0_hy", [P, 2, GCOLS])
        wt = sb("l0_wt", [P, 2, GCOLS])
        XT = sb("l0_xt", [P, NB * 8, P])
        kvm = offm
        kv = sb("l0_kv", [P, NB, KEYS])
        vm = hx[:].rearrange("p (b g k) -> p b g k", b=NB, g=HEADS)
        sel = PX[:].rearrange("p c (g k t) -> p (c g) k t", t=4, k=16)
        own = sb("l0_own", [P, 16])
        pos = sb("l0_pos", [P, 16, HW])
        mag = sb("l0_mag", [P, 16 * HW])
        sgn = sb("l0_sgn", [P, 16 * HW])
        F = pos[:].rearrange("p k q -> p (k q)")
        inner = lambda b, y0, n: qpad[:, b, 1 + y0:1 + y0 + n, 1:1 + HW]

        block = ctx.enter_context(nc.Block())

        @block.sync
        def _(sp):
            for b in range(NB):
                sp.dma_start(X[:, b * PIX:(b + 1) * PIX], x_dram[b].rearrange("c h w -> c (h w)")).then_inc(wait_x, 16)

        @block.gpsimd
        def _(pool):
            pool.memset(qpad[:], 0.0).then_inc(sem("border"), 1)

        @block.vector
        def _(dve):
            link = Chain(dve, sem("dve_chain"))
            dve.wait_ge(loaded, 16)
            dve.wait_ge(wait_x, 32)
            link(dve.tensor_scalar(s1[:], W["bn1_g"], BN_SCALE, None, ALU.mult))
            dve.tensor_scalar(XN[:], X[:], s1[:, 0:1], W["bn1_b"], ALU.mult, ALU.add).then_inc(sem("xn"), 1)
            dve.wait_ge(sem("q_out"), NCH)
            for t in range(TAPS):
                ky, kx = divmod(t, 6)
                src = qpad[:, :, ky:ky + 29:4, kx:kx + 29:4]
                for b in range(NB):
                    if t == 0:
                        ins = dve.tensor_scalar(conv[:, b], src[:, b], W["off_dw_w"][:, 0:1], None, ALU.mult)
                    else:
                        ins = dve.scalar_tensor_tensor(conv[:, b], src[:, b], W["off_dw_w"][:, t:t + 1], conv[:, b],
                                                       ALU.mult, ALU.add)
                    if b == 0:
                        ins.then_inc(sem("tap0"), 1)
                link(ins)
                dve.wait_ge(sem("tap0"), t + 1)
            dve.sem_inc(sem("conv"), 1)
            dve.wait_ge(sem("off"), 1)
            link(dve.tensor_tensor(offm[:], bc(off[:], 2, HEADS), bc(bc(W["gmask"], 1, NB), 3, KEYS), ALU.mult))
            dve.sem_inc(sem("offm"), 1)
            dve.wait_ge(sem("tanh"), 1)
            for c in range(2):
                grid = bc(W["kgrid"][:, c * KEYS:(c + 1) * KEYS], 1, NB * HEADS)
                link(dve.scalar_tensor_tensor(V[:, c], V[:, c], 4.0, grid, ALU.mult, ALU.add))
            link(dve.tensor_scalar(V[:], V[:], 2.0 / 7.0, -1.0, ALU.mult, ALU.add))
            link(dve.tensor_scalar(PX[:], V[:].rearrange("p c g k -> p c (g k)"), 1.0, HW / 2.0, ALU.add, ALU.mult))
            dve.sem_inc(sem("pixels"), 1)
            dve.wait_ge(sem("hx"), 1)
            for c in range(8):
                dve.wait_ge(sem("hy"), c + 1)
                if c >= 2:
                    dve.wait_ge(sem("sampled"), c - 1)
                dve.tensor_tensor(wt[:, c % 2], hx[:], hy[:, c % 2], ALU.mult).then_inc(sem("wt"), 1)
            link(dve.tensor_tensor(sel, V[:].rearrange("p c g (k t) -> p (c g) k t", t=4),
                                   bc(W["ident"].rearrange("p (g t) -> p g t", t=4), 2, 16), ALU.mult))
            link(dve.tensor_reduce(own[:], sel.rearrange("p g k t -> p k g t"), AX.XY, ALU.add))
            link(dve.tensor_tensor(pos[:], bc(W["qgrid"], 1, 16), bc(own[:], 2, HW), ALU.subtract))
            dve.sem_inc(sem("pos"), 1)
            dve.wait_ge(sem("sampled"), 8)
            for b in range(NB):
                dve.tensor_tensor(kvm[:, b], PS[:, 4 + b].rearrange("p (g k) -> p g k", g=HEADS),
                                  bc(W["gmask"], 2, KEYS), ALU.mult).then_inc(sem("kvm"), 1)
            dve.wait_ge(sem("kvm"), NB)
            link(dve.tensor_reduce(kv[:], kvm[:].rearrange("p b g k -> p b k g"), AX.X, ALU.add))
            dve.sem_inc(sem("kv"), 1)
            dve.wait_ge(sem("k"), 1)
            for b in range(NB):
                m = bc(W["gmask"], 2, KEYS)
                dve.scalar_tensor_tensor(KM[:, b], bc(PS[:, 6, b * KEYS:(b + 1) * KEYS], 1, HEADS), DH ** -0.5, m,
                                         ALU.mult, ALU.mult).then_inc(sem("km"), 1)
                dve.tensor_tensor(vm[:, b], bc(PS[:, 7, b * KEYS:(b + 1) * KEYS], 1, HEADS), m,
                                  ALU.mult).then_inc(sem("vm"), 1)
            dve.wait_ge(sem("logs"), 1)
            dve.tensor_tensor(F, sgn[:], mag[:], ALU.mult).then_inc(sem("f"), 1)
            for n in range(NB * HEADS):
                dve.wait_ge(sem("ab"), n + 1)
                dve.tensor_copy(B[:, n // 2, (n % 2) * 16:(n % 2) * 16 + 16].rearrange("p u q -> p (u q)"),
                                PS[:, 2 * (n % 2) + 1]).then_inc(sem("b_out"), 1)

        @block.scalar
        def _(act):
            for n in range(NCH):
                act.wait_ge(sem("q"), n + 1)
                if n == 0:
                    act.wait_ge(sem("border"), 1)
                act.activation(inner(n // 2, 16 * (n % 2), 16), PS[:, n].rearrange("p (y x) -> p y x", x=HW),
                               ACT.Copy).then_inc(sem("q_out"), 1)
            for n in range(NCH):
                act.activation(Q[:, n * CH:(n + 1) * CH], PS[:, n], ACT.Copy).then_inc(sem("q_flat"), 1)
            for n in range(4):
                act.wait_ge(sem("xt"), n + 1)
                act.activation(XT[:, 4 * n:4 * n + 4].rearrange("p c k -> p (c k)"), PS[:, n],
                               ACT.Copy).then_inc(sem("xt_out"), 1)
            act.wait_ge(sem("conv"), 1)
            act.activation(off[:].rearrange("p b k -> p (b k)"), conv[:].rearrange("p b y x -> p (b y x)"), ACT.Gelu,
                           bias=W["off_dw_b"]).then_inc(sem("off"), 1)
            act.wait_ge(sem("shift"), 1)
            act.activation(V[:].rearrange("p c g k -> p (c g k)"), PS[:, 4:8].rearrange("p a n -> p (a n)"),
                           ACT.Tanh).then_inc(sem("tanh"), 1)
            act.wait_ge(sem("pixels"), 1)
            act.activation(hy[:, 0], PX[:, 0], ACT.Abs, bias=W["minus_x"]).then_inc(sem("ax"), 1)
            act.wait_ge(sem("ax"), 1)
            act.activation(hx[:], hy[:, 0], ACT.Relu, bias=1.0, scale=-1.0).then_inc(sem("hx"), 1)
            act.wait_ge(sem("hx"), 1)
            for c in range(8):
                if c >= 2:
                    act.wait_ge(sem("wt"), c - 1)
                act.activation(hy[:, c % 2], PX[:, 1], ACT.Abs, bias=W["minus_y"][:, c:c + 1]).then_inc(sem("ay"), 1)
                act.wait_ge(sem("ay"), c + 1)
                act.activation(hy[:, c % 2], hy[:, c % 2], ACT.Relu, bias=1.0, scale=-1.0).then_inc(sem("hy"), 1)
            act.wait_ge(sem("pos"), 1)
            flat = pos[:].rearrange("p k q -> p (k q)")
            act.activation(mag[:], flat, ACT.Abs).then_inc(sem("mag"), 1)
            act.activation(sgn[:], flat, ACT.Sign).then_inc(sem("sgn"), 1)
            act.wait_ge(sem("mag"), 1)
            act.wait_ge(sem("sgn"), 1)
            act.activation(mag[:], mag[:], ACT.Ln, bias=1.0).then_inc(sem("logs"), 1)
            for n in range(NB * HEADS):
                act.wait_ge(sem("ab"), n + 1)
                act.activation(A[:, n // 2, (n % 2) * 16:(n % 2) * 16 + 16].rearrange("p u q -> p (u q)"),
                               PS[:, 2 * (n % 2)], ACT.Identity, bias=W["cpb_b1"]).then_inc(sem("a_out"), 1)
            for n in range(2):
                act.wait_ge(sem("vt"), n + 1)
                act.activation(VT[:, 4 * n:4 * n + 4].rearrange("p c k -> p (c k)"), PS[:, 4 + n],
                               ACT.Copy).then_inc(sem("vt_out"), 1)

        @block.tensor
        def _(pe):
            pe.wait_ge(sem("xn"), 1)
            for n in range(NCH):
                pe.matmul(PS[:, n], W["qw"], XN[:, n * CH:(n + 1) * CH], start=True, stop=True).then_inc(sem("q"), 1)
            for n in range(16):
                if n % 4 == 0:
                    pe.wait_ge(sem("q_flat"), n // 4 + 1)
                ins = pe.transpose(PS[:, n // 4, (n % 4) * P:(n % 4 + 1) * P], XN[:, n * P:(n + 1) * P], W["ident"])
                if n % 4 == 3:
                    ins.then_inc(sem("xt"), 1)
            pe.wait_ge(sem("offm"), 1)
            for c in range(2):
                for b in range(NB):
                    ins = pe.matmul(PS[:, 4 + 2 * c + b], W["off_pw"][:, c * P:(c + 1) * P],
                                    offm[:, b].rearrange("p g k -> p (g k)"), start=True, stop=True)
            ins.then_inc(sem("shift"), 1)
            pe.wait_ge(sem("xt_out"), 4)
            pe.wait_ge(sem("tanh"), 1)
            for c in range(8):
                pe.wait_ge(sem("wt"), c + 1)
                for b in range(NB):
                    ins = pe.matmul(PS[:, 4 + b], XT[:, b * 8 + c], wt[:, c % 2, b * CH:(b + 1) * CH],
                                    start=(c == 0), stop=(c == 7))
                ins.then_inc(sem("sampled"), 1)
            pe.wait_ge(sem("kv"), 1)
            kflat = kv[:].rearrange("p b k -> p (b k)")
            pe.matmul(PS[:, 6, 0:NB * KEYS], W["kw"], kflat, start=True, stop=True)
            pe.matmul(PS[:, 7, 0:NB * KEYS], W["vw"], kflat, start=True, stop=True).then_inc(sem("k"), 1)
            pe.wait_ge(sem("f"), 1)
            for n in range(NB * HEADS):
                b, g = divmod(n, HEADS)
                if n >= 2:
                    pe.wait_ge(sem("a_out"), n - 1)
                    pe.wait_ge(sem("b_out"), n - 1)
                for c in range(2):
                    r = 64 * c + 32 * b
                    ins = pe.matmul(PS[:, 2 * (n % 2) + c], W["cpb_w1"][r:r + 32, g * P:(g + 1) * P], F[r:r + 32, :],
                                    start=True, stop=True, tile_position=(r, 0))
                ins.then_inc(sem("ab"), 1)
            pe.wait_ge(sem("vm"), NB)
            for n in range(NB * PAIRS):
                ins = pe.transpose(PS[:, 4 + n // 4, (n % 4) * P:(n % 4 + 1) * P],
                                   vm[:, n // 4, 2 * (n % 4):2 * (n % 4) + 2].rearrange("p g k -> p (g k)"), W["ident"])
                if n % 4 == 3:
                    ins.then_inc(sem("vt"), 1)


def reg_wait(eng, sem, value, passed):
    eng.wait_ge(sem, value)
    eng.sem_inc(passed, 1)


def l0_scores(nc, PS, W, KM, Q, A, B, SALL):
    with ExitStack() as ctx:
        st = Stage(nc, ctx)
        sb, sem = st.sb, st.sem
        kcur = sb("sc_k", [P, P])
        H1 = sb("sc_h1", [P, 2, 4, HALF])
        H2 = sb("sc_h2", [P, 8, HALF])
        NBT = 2 * BATCHES
        STEPS = NB * PAIRS
        Z2, H1N, QK, TILE, BIASED = 8, 4, 1, 2, 2
        block = ctx.enter_context(nc.Block())

        @block.gpsimd
        def _(pool):
            with pool.Fori(0, STEPS) as n:
                reg_wait(pool, sem("qk"), n + 1, sem("pool_passed"))
                pool.tensor_copy(kcur[:].rearrange("p (g k) -> p g k", g=2),
                                 KM[:].rearrange("p b (q g) k -> p (b q) g k", g=2)[:, bass.ds(n, 1)].squeeze(1)
                                 ).then_inc(sem("kcur"), 1)
                for m in range(NBT):
                    half, bt = divmod(m, BATCHES)
                    reg_wait(pool, sem("z2"), (n * NBT + m) * 4 + Z2 - 4, sem("pool_passed"))
                    a = A[:, bass.ds(n, 1), bt:32:BATCHES, :].squeeze(1)
                    b = B[:, bass.ds(n, 1), bt:32:BATCHES, 16 * half:16 * half + 16].squeeze(1)
                    pool.tensor_tensor(H1[:, m % 2].rearrange("p u (y x) -> p u y x", x=HW), bc(a, 2, 16),
                                       bc(b, 3, HW), ALU.add).then_inc(sem("z1"), 1)

        @block.vector
        def _(dve):
            with dve.Fori(0, STEPS) as n:
                for m in range(NBT):
                    dve.wait_ge(sem("z1"), n * NBT + m + 1)
                    h = H1[:, m % 2].rearrange("p u q -> p (u q)")
                    dve.tensor_scalar(h, h, 0.0, None, ALU.max).then_inc(sem("h1"), 1)

        @block.tensor
        def _(pe):
            pe.sem_inc(sem("qk"), QK)
            pe.sem_inc(sem("z2"), Z2)
            pe.sem_inc(sem("biased"), BIASED)

            def scores(n, half):
                pe.wait_ge(sem("tile_out"), n * 2 + half + 1)
                ins = pe.matmul(PS[:, half], kcur[:], Q[:, bass.ds((n // PAIRS) * PIX + half * HALF, HALF)],
                                start=True, stop=False, skip_group_check=True)
                if half:
                    ins.then_inc(sem("qk"), 1)

            def layer2(n, m):
                pe.wait_ge(sem("h1"), n * NBT + m + 1)
                for i in range(4):
                    pe.wait_ge(sem("h2"), (n * NBT + m) * 4 + i + 1)
                    pe.matmul(PS[:, 2 + i], W["cpb_w2"], H1[:, m % 2, i], start=True, stop=True).then_inc(sem("z2"), 1)

            def layer3(n, m):
                half, bt = divmod(m, BATCHES)
                pe.wait_ge(sem("h2"), (n * NBT + m) * 4 + 4 + H1N)
                for i in range(4):
                    ins = pe.matmul(PS[32 * i:32 * i + 32, half], W["cpb_w3"][:, bt * HID:(bt + 1) * HID],
                                    H2[:, 4 * (m % 2) + i], start=False, stop=(bt == BATCHES - 1),
                                    tile_position=(0, 32 * i), skip_group_check=True)
                ins.then_inc(sem("biased"), 1)

            with pe.Fori(0, STEPS) as n:
                pe.wait_ge(sem("kcur"), n + 1)
                scores(n, 0)
                for m in range(NBT):
                    layer2(n, m)
                    if m:
                        layer3(n, m - 1)
                    if m == BATCHES - 1:
                        scores(n, 1)
                layer3(n, NBT - 1)

        @block.scalar
        def _(act):
            act.sem_inc(sem("h2"), H1N)
            act.sem_inc(sem("tile_out"), TILE)

            def tile_out(n, half):
                reg_wait(act, sem("biased"), n * NBT + (half + 1) * BATCHES + BIASED, sem("act_passed"))
                act.activation(SALL[:, bass.ds(n * 2 + half, 1)].squeeze(1), PS[:, half], ACT.Identity,
                               bias=W["cpb_b3"]).then_inc(sem("tile_out"), 1)

            with act.Fori(0, STEPS) as n:
                for m in range(NBT):
                    for i in range(4):
                        act.wait_ge(sem("z2"), (n * NBT + m) * 4 + i + 1 + Z2)
                        if i == 0:
                            act.wait_ge(sem("biased"), n * NBT + m - 1 + BIASED)
                        act.activation(H2[:, 4 * (m % 2) + i], PS[:, 2 + i], ACT.Relu,
                                       bias=W["cpb_b2"]).then_inc(sem("h2"), 1)
                    if m == BATCHES + 1:
                        tile_out(n, 0)
                tile_out(n, 1)


def l0_attend(nc, X, PS, W, SALL, VT):
    with ExitStack() as ctx:
        st = Stage(nc, ctx)
        sb, sem = st.sb, st.sem
        mx = sb("at_max", [P, 8])
        E = sb("at_e", [P, 2, 8, KEYS])
        den = sb("at_den", [P, 8])
        rden = sb("at_rden", [P, 8])
        PT = sb("at_pt", [P, 2, HALF])
        ATT = sb("at_att", [P, T])
        TILES = NB * PAIRS * 2
        block = ctx.enter_context(nc.Block())

        @block.tensor
        def _(pe):
            def turn(s):
                if s >= 2:
                    pe.wait_ge(sem("shifted"), s - 1)
                for t in range(4):
                    ins = pe.transpose(PS[:, s % 2, t * P:(t + 1) * P], SALL[:, s, t * P:(t + 1) * P], W["ident"])
                ins.then_inc(sem("turned"), 1)

            def back(s):
                pe.wait_ge(sem("probs"), s + 1)
                if s >= 2:
                    pe.wait_ge(sem("pt"), s - 1)
                for t in range(4):
                    ins = pe.transpose(PS[:, 2 + s % 2, t * P:(t + 1) * P],
                                       E[:, s % 2, 2 * t:2 * t + 2].rearrange("p g k -> p (g k)"), W["ident"])
                ins.then_inc(sem("back"), 1)

            def values(s):
                b, pair, half = s // 8, s // 2 % 4, s % 2
                pe.wait_ge(sem("pt"), s + 1)
                pe.matmul(PS[:, 4 + 2 * b + half], VT[:, b * PAIRS + pair], PT[:, s % 2], start=(pair == 0),
                          stop=(pair == PAIRS - 1)).then_inc(sem("valued"), 1)

            for s in range(TILES + 2):
                if s < TILES:
                    turn(s)
                if 1 <= s <= TILES:
                    back(s - 1)
                if s >= 2:
                    values(s - 2)
            for n in range(NCH):
                pe.wait_ge(sem("att"), n + 1)
                pe.matmul(PS[:, n], W["out_w"], ATT[:, n * CH:(n + 1) * CH], start=True,
                          stop=True).then_inc(sem("proj"), 1)

        @block.vector
        def _(dve):
            link = Chain(dve, sem("dve_chain"))

            def shift(s):
                dve.wait_ge(sem("turned"), s + 1)
                t = PS[:, s % 2].rearrange("p (g k) -> p g k", k=KEYS)
                link(dve.tensor_reduce(mx[:], t, AX.X, ALU.max))
                if s >= 2:
                    dve.wait_ge(sem("back"), s - 1)
                dve.tensor_tensor(E[:, s % 2], t, bc(mx[:], 2, KEYS), ALU.subtract).then_inc(sem("shifted"), 1)
                dve.wait_ge(sem("shifted"), s + 1)

            def norm(s):
                dve.wait_ge(sem("exp"), s + 1)
                link(dve.tensor_reduce(den[:], E[:, s % 2], AX.X, ALU.add))
                link(dve.reciprocal(rden[:], den[:]))
                dve.tensor_tensor(E[:, s % 2], E[:, s % 2], bc(rden[:], 2, KEYS), ALU.mult).then_inc(sem("probs"), 1)
                dve.wait_ge(sem("probs"), s + 1)

            for s in range(TILES + 1):
                if s < TILES:
                    shift(s)
                if s >= 1:
                    norm(s - 1)
            for n in range(NCH):
                dve.wait_ge(sem("proj"), n + 1)
                x = X[:, n * CH:(n + 1) * CH]
                dve.scalar_tensor_tensor(x, PS[:, n], W["out_b"], x, ALU.add, ALU.add)

        @block.scalar
        def _(act):
            for s in range(TILES + 1):
                if s < TILES:
                    act.wait_ge(sem("shifted"), s + 1)
                    e = E[:, s % 2].rearrange("p g k -> p (g k)")
                    act.activation(e, e, ACT.Exp).then_inc(sem("exp"), 1)
                if s >= 1:
                    act.wait_ge(sem("back"), s)
                    if s >= 3:
                        act.wait_ge(sem("valued"), s - 2)
                    act.activation(PT[:, (s - 1) % 2], PS[:, 2 + (s - 1) % 2], ACT.Copy).then_inc(sem("pt"), 1)
            for n in range(NCH):
                act.wait_ge(sem("valued"), 16 if n >= 2 else 8)
                act.activation(ATT[:, n * CH:(n + 1) * CH], PS[:, 4 + n], ACT.Copy).then_inc(sem("att"), 1)


def l0_mlp(nc, X, PS, W):
    with ExitStack() as ctx:
        st = Stage(nc, ctx)
        sb, sem = st.sb, st.sem
        s2 = sb("ml_s2", [P, 1])
        XN = sb("ml_xn", [P, T])
        H = sb("ml_h", [P, 2, 4, CH])
        block = ctx.enter_context(nc.Block())

        @block.vector
        def _(dve):
            link = Chain(dve, sem("dve_chain"))
            link(dve.tensor_scalar(s2[:], W["bn2_g"], BN_SCALE, None, ALU.mult))
            for n in range(NCH):
                c = slice(n * CH, (n + 1) * CH)
                dve.tensor_scalar(XN[:, c], X[:, c], s2[:, 0:1], W["bn2_b"], ALU.mult, ALU.add).then_inc(sem("xn"), 1)
            for n in range(NCH):
                dve.wait_ge(sem("down"), n + 1)
                x = X[:, n * CH:(n + 1) * CH]
                dve.scalar_tensor_tensor(x, PS[:, 6 + n % 2], W["mlp_b2"], x, ALU.add, ALU.add).then_inc(sem("added"), 1)

        @block.tensor
        def _(pe):
            def up(n):
                pe.wait_ge(sem("xn"), n + 1)
                for k in range(4):
                    g = 4 * n + k
                    if g >= 6:
                        pe.wait_ge(sem("gelu"), g - 5)
                    pe.matmul(PS[:, g % 6], W["mlp_w1"][:, k * P:(k + 1) * P], XN[:, n * CH:(n + 1) * CH], start=True,
                              stop=True).then_inc(sem("up"), 1)

            def down(n):
                pe.wait_ge(sem("gelu"), 4 * n + 4)
                if n >= 2:
                    pe.wait_ge(sem("added"), n - 1)
                for k in range(4):
                    ins = pe.matmul(PS[:, 6 + n % 2], W["mlp_w2"][:, k * P:(k + 1) * P], H[:, n % 2, k],
                                    start=(k == 0), stop=(k == 3))
                ins.then_inc(sem("down"), 1)

            for n in range(NCH + 1):
                if n < NCH:
                    up(n)
                if n >= 1:
                    down(n - 1)

        @block.scalar
        def _(act):
            for g in range(4 * NCH):
                n, k = divmod(g, 4)
                act.wait_ge(sem("up"), g + 1)
                if n >= 2:
                    act.wait_ge(sem("down"), n - 1)
                act.activation(H[:, n % 2, k], PS[:, g % 6], ACT.Gelu, bias=W["mlp_b1"][:, k:k + 1]
                               ).then_inc(sem("gelu"), 1)


ITILES = PIX // P


def l1_pack(w):
    p = Pack()
    L = lambda n: w["L1_conv_" + n]
    for n in ("gn_w", "gn_b", "bq", "bk", "bv", "bo"):
        p.add(n, L(n).reshape(P, 1))
    for n in ("wq", "wk", "wv", "wo"):
        p.add(n, L(n).T)
    p.add("ident", np.eye(P, dtype=np.float32))
    p.add("group", np.kron(np.eye(32), np.full((4, 4), 0.25)).astype(np.float32))
    return p


def l1_attention(nc, X, PS, W):
    with ExitStack() as ctx:
        st = Stage(nc, ctx)
        sb, sem = st.sb, st.sem
        stats = sb("gn_stats", [P, NB, 2, 6])
        mv = sb("gn_mv", [P, NB, 2])
        mom = sb("gn_mom", [P, 2, NB])
        mu = sb("gn_mu", [P, NB])
        dev = sb("gn_dev", [P, NB])
        rstd = sb("gn_rstd", [P, NB])
        gain = sb("gn_gain", [P, NB])
        shift = sb("gn_shift", [P, NB])
        HF = sb("a1_hf", [P, T])
        Qm = sb("a1_q", [P, T])
        Km = sb("a1_k", [P, T])
        Vt = sb("a1_vt", [P, NB * ITILES, P])
        mx = sb("a1_max", [P, 2])
        nmx = sb("a1_nmax", [P, 2])
        den = sb("a1_den", [P, 2])
        rden = sb("a1_rden", [P, 2])
        E = sb("a1_e", [P, 2, PIX])
        PT = sb("a1_pt", [P, 2, ITILES, P])
        AO = sb("a1_ao", [P, T])
        SCALE = float(P) ** -0.5
        TILES = NB * ITILES
        block = ctx.enter_context(nc.Block())

        @block.vector
        def _(dve):
            link = Chain(dve, sem("dve_chain"))
            for b in range(NB):
                for h in range(2):
                    c = (b * 2 + h) * CH
                    ins = dve.bn_stats(stats[:, b, h], X[:, c:c + CH])
            link(ins)
            for b in range(NB):
                link(dve.bn_aggr(mv[:, b], stats[:, b]))
            dve.tensor_copy(mom[:, 0], mv[:, :, 0]).then_inc(sem("means"), 1)
            dve.wait_ge(sem("group_mean"), 1)
            link(dve.tensor_copy(mu[:], PS[:, 0, 0:NB]))
            link(dve.tensor_tensor(dev[:], mv[:, :, 0], mu[:], ALU.subtract))
            link(dve.tensor_tensor(dev[:], dev[:], dev[:], ALU.mult))
            dve.tensor_tensor(mom[:, 1], dev[:], mv[:, :, 1], ALU.add).then_inc(sem("vars"), 1)
            dve.wait_ge(sem("group_var"), 1)
            link(dve.tensor_scalar(rstd[:], PS[:, 1, 0:NB], 1e-6, None, ALU.add))
            link(dve.reciprocal(rstd[:], rstd[:]))
            dve.sem_inc(sem("inverse"), 1)
            dve.wait_ge(sem("root"), 1)
            link(dve.tensor_scalar(gain[:], rstd[:], W["gn_w"], None, ALU.mult))
            link(dve.tensor_tensor(shift[:], mu[:], gain[:], ALU.mult))
            link(dve.tensor_scalar(shift[:], shift[:], -1.0, W["gn_b"], ALU.mult, ALU.add))
            for b in range(NB):
                c = slice(b * PIX, (b + 1) * PIX)
                dve.tensor_scalar(HF[:, c], X[:, c], gain[:, b:b + 1], shift[:, b:b + 1], ALU.mult,
                                  ALU.add).then_inc(sem("hf"), 1)
            for n in range(NCH):
                dve.wait_ge(sem("k"), n + 1)
                dve.tensor_scalar(Km[:, n * CH:(n + 1) * CH], PS[:, 4 + n], W["bk"], None,
                                  ALU.add).then_inc(sem("k_out"), 1)

            def top(s):
                dve.wait_ge(sem("scores"), s + 1)
                if s >= 2:
                    dve.wait_ge(sem("exp"), s - 1)
                v = PS[:, 2 * (s % 2):2 * (s % 2) + 2].rearrange("p a n -> p (a n)")
                link(dve.tensor_reduce(mx[:, s % 2:s % 2 + 1], v, AX.X, ALU.max))
                dve.tensor_scalar(nmx[:, s % 2:s % 2 + 1], mx[:, s % 2:s % 2 + 1], -SCALE, None,
                                  ALU.mult).then_inc(sem("top"), 1)

            def norm(s):
                dve.wait_ge(sem("exp"), s + 1)
                link(dve.reciprocal(rden[:, s % 2:s % 2 + 1], den[:, s % 2:s % 2 + 1]))
                dve.tensor_scalar(E[:, s % 2], E[:, s % 2], rden[:, s % 2:s % 2 + 1], None,
                                  ALU.mult).then_inc(sem("probs"), 1)

            def back_out(s):
                dve.wait_ge(sem("back"), 2 * s + 2)
                if s >= 2:
                    dve.wait_ge(sem("valued"), s - 1)
                dve.tensor_copy(PT[:, s % 2, 4:8].rearrange("p j i -> p (j i)"), PS[:, 5]).then_inc(sem("pt_dve"), 1)

            for s in range(TILES + 2):
                if s < TILES:
                    top(s)
                if 1 <= s <= TILES:
                    norm(s - 1)
                if s >= 2:
                    back_out(s - 2)
            for n in range(NCH):
                dve.wait_ge(sem("proj"), n + 1)
                x = X[:, n * CH:(n + 1) * CH]
                dve.scalar_tensor_tensor(x, PS[:, n], W["bo"], x, ALU.add, ALU.add)

        @block.scalar
        def _(act):
            act.wait_ge(sem("inverse"), 1)
            act.activation(rstd[:], rstd[:], ACT.Sqrt).then_inc(sem("root"), 1)
            for n in range(NCH):
                act.wait_ge(sem("q"), n + 1)
                act.activation(Qm[:, n * CH:(n + 1) * CH], PS[:, n], ACT.Identity, bias=W["bq"]).then_inc(sem("q_out"), 1)
            for n in range(4):
                act.wait_ge(sem("vt"), n + 1)
                act.activation(Vt[:, 4 * n:4 * n + 4].rearrange("p c k -> p (c k)"), PS[:, n],
                               ACT.Copy).then_inc(sem("vt_out"), 1)

            def exp(s):
                act.wait_ge(sem("top"), s + 1)
                if s >= 2:
                    act.wait_ge(sem("back"), 2 * (s - 2) + 2)
                v = PS[:, 2 * (s % 2):2 * (s % 2) + 2].rearrange("p a n -> p (a n)")
                act.activation(E[:, s % 2], v, ACT.Exp, bias=nmx[:, s % 2:s % 2 + 1], scale=SCALE,
                               accum_out=den[:, s % 2:s % 2 + 1]).then_inc(sem("exp"), 1)

            def back_out(s):
                act.wait_ge(sem("back"), 2 * s + 1)
                if s >= 2:
                    act.wait_ge(sem("valued"), s - 1)
                act.activation(PT[:, s % 2, 0:4].rearrange("p j i -> p (j i)"), PS[:, 4],
                               ACT.Copy).then_inc(sem("pt_act"), 1)

            def out(n):
                act.wait_ge(sem("valued"), 4 * n + 4)
                act.activation(AO[:, n * CH:(n + 1) * CH], PS[:, 6 + n % 2], ACT.Identity,
                               bias=W["bv"]).then_inc(sem("ao"), 1)

            for s in range(TILES + 2):
                if s < TILES:
                    exp(s)
                if s >= 2:
                    back_out(s - 2)
                if s >= 6 and (s - 6) % 4 == 0:
                    out((s - 6) // 4)
            out(NCH - 1)

        @block.tensor
        def _(pe):
            pe.wait_ge(sem("means"), 1)
            pe.matmul(PS[:, 0, 0:NB], W["group"], mom[:, 0], start=True, stop=True).then_inc(sem("group_mean"), 1)
            pe.wait_ge(sem("vars"), 1)
            pe.matmul(PS[:, 1, 0:NB], W["group"], mom[:, 1], start=True, stop=True).then_inc(sem("group_var"), 1)
            for n in range(NCH):
                pe.wait_ge(sem("hf"), n // 2 + 1)
                pe.matmul(PS[:, n], W["wq"], HF[:, n * CH:(n + 1) * CH], start=True, stop=True).then_inc(sem("q"), 1)
            for n in range(NCH):
                pe.matmul(PS[:, 4 + n], W["wk"], HF[:, n * CH:(n + 1) * CH], start=True, stop=True).then_inc(sem("k"), 1)
            for n in range(4):
                pe.wait_ge(sem("q_out"), n + 1)
                for j in range(4):
                    t = 4 * n + j
                    ins = pe.matmul(PS[:, n, j * P:(j + 1) * P], HF[:, t * P:(t + 1) * P], W["wv"], start=True, stop=True)
                ins.then_inc(sem("vt"), 1)
            pe.wait_ge(sem("k_out"), NCH)
            pe.wait_ge(sem("vt_out"), 4)

            def scores(s):
                b = s // ITILES
                if s >= 2:
                    pe.wait_ge(sem("exp"), s - 1)
                for h in range(2):
                    c = b * PIX + h * CH
                    ins = pe.matmul(PS[:, 2 * (s % 2) + h], Qm[:, s * P:(s + 1) * P], Km[:, c:c + CH], start=True,
                                    stop=True)
                ins.then_inc(sem("scores"), 1)

            def back(s):
                pe.wait_ge(sem("probs"), s + 1)
                for h in range(2):
                    if s >= 1:
                        pe.wait_ge(sem("pt_dve" if h else "pt_act"), s)
                    for j in range(4):
                        t = 4 * h + j
                        ins = pe.transpose(PS[:, 4 + h, j * P:(j + 1) * P], E[:, s % 2, t * P:(t + 1) * P], W["ident"])
                    ins.then_inc(sem("back"), 1)

            def values(s):
                b, n = s // ITILES, s // 4
                pe.wait_ge(sem("pt_act"), s + 1)
                pe.wait_ge(sem("pt_dve"), s + 1)
                if n >= 2 and s % 4 == 0:
                    pe.wait_ge(sem("ao"), n - 1)
                for j in range(ITILES):
                    ins = pe.matmul(PS[:, 6 + n % 2, (s % 4) * P:(s % 4 + 1) * P], Vt[:, b * ITILES + j],
                                    PT[:, s % 2, j], start=(j == 0), stop=(j == ITILES - 1))
                ins.then_inc(sem("valued"), 1)

            for s in range(TILES + 3):
                if s < TILES:
                    scores(s)
                if 1 <= s <= TILES:
                    back(s - 1)
                if s >= 3:
                    values(s - 3)
            for n in range(NCH):
                pe.wait_ge(sem("ao"), n + 1)
                if n == 0:
                    pe.wait_ge(sem("exp"), TILES)
                pe.matmul(PS[:, n], W["wo"], AO[:, n * CH:(n + 1) * CH], start=True, stop=True).then_inc(sem("proj"), 1)


def layer_norm(nc, name, X, XN, PS, mean):
    with ExitStack() as ctx:
        st = Stage(nc, ctx)
        sb, sem = st.sb, st.sem
        SQ = sb(name + "_sq", [P, 2, CH])
        R = sb(name + "_r", [P, T])
        block = ctx.enter_context(nc.Block())

        @block.tensor
        def _(pe):
            for n in range(NCH):
                pe.matmul(PS[:, n], mean, X[:, n * CH:(n + 1) * CH], start=True, stop=True).then_inc(sem("mean"), 1)
            for n in range(NCH):
                pe.wait_ge(sem("square"), n + 1)
                pe.matmul(PS[:, 4 + n], mean, SQ[:, n % 2], start=True, stop=True).then_inc(sem("var"), 1)

        @block.vector
        def _(dve):
            for n in range(NCH):
                c = slice(n * CH, (n + 1) * CH)
                dve.wait_ge(sem("mean"), n + 1)
                dve.tensor_tensor(XN[:, c], X[:, c], PS[:, n], ALU.subtract).then_inc(sem("centred"), 1)
            for n in range(NCH):
                c = slice(n * CH, (n + 1) * CH)
                dve.wait_ge(sem("var"), n + 1)
                dve.tensor_scalar(R[:, c], PS[:, 4 + n], 1e-5, None, ALU.add).then_inc(sem("eps"), 1)
                dve.wait_ge(sem("eps"), n + 1)
                dve.reciprocal(R[:, c], R[:, c]).then_inc(sem("inverse"), 1)
            for n in range(NCH):
                c = slice(n * CH, (n + 1) * CH)
                dve.wait_ge(sem("root"), n + 1)
                dve.tensor_tensor(XN[:, c], XN[:, c], R[:, c], ALU.mult)

        @block.scalar
        def _(act):
            for n in range(NCH):
                act.wait_ge(sem("centred"), n + 1)
                if n >= 2:
                    act.wait_ge(sem("var"), n - 1)
                act.activation(SQ[:, n % 2], XN[:, n * CH:(n + 1) * CH], ACT.Square).then_inc(sem("square"), 1)
            for n in range(NCH):
                c = slice(n * CH, (n + 1) * CH)
                act.wait_ge(sem("inverse"), n + 1)
                act.activation(R[:, c], R[:, c], ACT.Sqrt).then_inc(sem("root"), 1)


REL = 257
WIN = 3 * P
ROW = 512


def l2a_pack(w):
    p = Pack()
    L = lambda n: w["L2_attn_" + n]
    p.add("b_out", L("b_out").reshape(P, 1))
    for n, name in enumerate(("wq", "wk", "wv")):
        p.add(name, L("W_qkv")[:, n * P:(n + 1) * P])
    p.add("w_out", L("W_out"))
    p.add("rel", np.tile(L("rel_table").T[:, ::-1], (HEADS, 1)))
    p.add("ident", np.eye(P, dtype=np.float32))
    p.add("mean", np.full((P, P), 1.0 / P, np.float32))
    hm = np.zeros((P, HEADS + 1), np.float32)
    hm[:, :HEADS] = np.repeat(np.eye(HEADS, dtype=np.float32), DH, axis=0)
    p.add("hmask", hm)
    return p


def l2_attention(nc, X, XN, PS, W, scratch):
    with ExitStack() as ctx:
        st = Stage(nc, ctx)
        sb, sem = st.sb, st.sem
        Qm = sb("r_q", [P, T])
        K = sb("r_k", [P, 3, T])
        V = sb("r_v", [P, NB, ITILES, P])
        VH = sb("r_vh", [P, NB, ITILES, DH])
        qh = sb("r_qh", [P, NB, PIX])
        qd = sb("r_qd", [P, NB, PIX])
        RD = sb("r_rd", [P, NB, ITILES, ROW])
        band = sb("r_band", [P, NB, ITILES, WIN])
        raw = sb("r_raw", [P, 2])
        mx = sb("r_max", [P, 2])
        den = sb("r_den", [P, NB, ITILES])
        rden = sb("r_rden", [P, NB, ITILES])
        E = sb("r_e", [P, 2, PIX])
        PT = sb("r_pt", [P, 2, ITILES, P])
        O = XN[:].rearrange("p (t c) -> p t c", c=P)
        AO = Qm
        SCALE = float(DH) ** -0.5
        l2_project(nc, st, PS, W, XN, Qm, K, V, RD)
        with nc.Block() as block:
            l2_heads(nc, st, block, PS, W, scratch, Qm, K, V, VH, qh, qd, RD, band, raw, mx, den, rden, E, PT, O, SCALE)
        l2_output(nc, st, X, PS, W, O, AO)


def l2_project(nc, st, PS, W, XN, Qm, K, V, RD):
    sem = st.sem
    with nc.Block() as block:
        @block.tensor
        def _(pe):
            for k, name in enumerate(("wq", "wk")):
                for n in range(NCH):
                    pe.matmul(PS[:, 4 * k + n], W[name], XN[:, n * CH:(n + 1) * CH], start=True,
                              stop=True).then_inc(sem(name), 1)
            for n in range(4):
                pe.wait_ge(sem("q_out"), n + 1)
                for j in range(4):
                    t = 4 * n + j
                    ins = pe.matmul(PS[:, n, j * P:(j + 1) * P], XN[:, t * P:(t + 1) * P], W["wv"], start=True, stop=True)
                ins.then_inc(sem("v"), 1)

        @block.scalar
        def _(act):
            for n in range(NCH):
                act.wait_ge(sem("wq"), n + 1)
                act.activation(Qm[:, n * CH:(n + 1) * CH], PS[:, n], ACT.Copy).then_inc(sem("q_out"), 1)
            for n in range(4):
                act.wait_ge(sem("v"), n + 1)
                act.activation(V[:, n // 2, 4 * (n % 2):4 * (n % 2) + 4].rearrange("p c k -> p (c k)"), PS[:, n], ACT.Copy)

        @block.vector
        def _(dve):
            for n in range(NCH):
                dve.wait_ge(sem("wk"), n + 1)
                dve.tensor_copy(K[:, 0, n * CH:(n + 1) * CH], PS[:, 4 + n]).then_inc(sem("k_out"), 1)
            dve.wait_ge(sem("k_out"), NCH)
            dve.tensor_scalar(K[:, 1], K[:, 0], W["rel"][:, 0:1], None, ALU.add)
            dve.tensor_scalar(K[:, 2], K[:, 0], W["rel"][:, REL - 1:REL], None, ALU.add)

        @block.gpsimd
        def _(pool):
            pool.memset(RD[:, :, :, ROW - 1:ROW], 0.0)


def l2_heads(nc, st, block, PS, W, scratch, Qm, K, V, VH, qh, qd, RD, band, raw, mx, den, rden, E, PT, O, SCALE):
    sem = st.sem
    SCORES, EXP, BACK, PTS, RDS, SENT, ADDED, VALUED, OUT = 16, 2, 4, 1, 1, 32, 16, 9, 1
    tiles = lambda i, t: i * ITILES + t
    LEFT = P - 1

    def wide(t):
        return PS[:, 2 * (t % 2):2 * (t % 2) + 2].rearrange("p a n -> p (a n)")

    @block.tensor
    def _(pe):
        pe.sem_inc(sem("scores"), SCORES)
        pe.sem_inc(sem("backs"), BACK)
        pe.sem_inc(sem("valued"), VALUED)

        def distances(f, b, t):
            if t == 0:
                pe.wait_ge(sem("qd"), f + 1)
            pe.wait_ge(sem("rd"), tiles(f, t) + RDS)
            pe.matmul(PS[:, 6, 0:REL], qd[:, b, t * P:(t + 1) * P], W["rel"], start=True, stop=True).then_inc(sem("qr"), 1)

        def scores(i, b, t):
            if t == 0:
                pe.wait_ge(sem("qh"), i + 1)
            pe.wait_ge(sem("exp"), tiles(i, t) - 1 + EXP)
            edges = sorted({0, max(0, (t - 1) * P), CH, min(PIX, (t + 2) * P), PIX})
            for lo, hi in zip(edges, edges[1:]):
                kind = 1 if hi <= (t - 1) * P else 2 if lo >= (t + 2) * P else 0
                ins = pe.matmul(PS[:, 2 * (t % 2) + lo // CH, lo % CH:lo % CH + hi - lo], qh[:, b, t * P:(t + 1) * P],
                                K[:, kind, b * PIX + lo:b * PIX + hi], start=True, stop=True, skip_group_check=True)
            ins.then_inc(sem("scores"), 1)

        def back(i, b, t):
            pe.wait_ge(sem("exp"), tiles(i, t) + 1 + EXP)
            for h in range(2):
                pe.wait_ge(sem("pt_dve" if h else "pt_act"), tiles(i, t) + PTS)
                for j in range(4):
                    c = (4 * h + j) * P
                    ins = pe.transpose(PS[:, 4 + h, j * P:(j + 1) * P], E[:, t % 2, c:c + P], W["ident"])
                ins.then_inc(sem("backs"), 1)

        def values(i, b, t):
            if t == 0:
                pe.wait_ge(sem("vh"), i + 1)
                pe.wait_ge(sem("o_out"), i + OUT)
            pe.wait_ge(sem("pt_act"), tiles(i, t) + 1 + PTS)
            pe.wait_ge(sem("pt_dve"), tiles(i, t) + 1 + PTS)
            for j in range(ITILES):
                ins = pe.matmul(PS[:, 7, t * DH:(t + 1) * DH], PT[:, t % 2, j], VH[:, b, j],
                                start=(j == 0), stop=(j == ITILES - 1), skip_group_check=True)
            ins.then_inc(sem("valued"), 1)

        for f in range(NB):
            for t in range(ITILES):
                distances(f, f, t)
        with pe.Fori(0, HEADS) as n:
            for s in range(NB * ITILES + 2):
                at = lambda lag: (n * 2 + (s - lag) // ITILES, (s - lag) // ITILES, (s - lag) % ITILES)
                if s < NB * ITILES:
                    i, b, t = at(0)
                    scores(i, b, t)
                    distances(i + 2, b, t)
                if 1 <= s <= NB * ITILES:
                    back(*at(1))
                if s >= 2:
                    values(*at(2))

    @block.scalar
    def _(act):
        act.sem_inc(sem("rd"), RDS)
        act.sem_inc(sem("exp"), EXP)
        act.sem_inc(sem("pt_act"), PTS)

        def distances_out(f, b, t):
            if t == 0:
                act.wait_ge(sem("rd_sent"), (f + 1) * 16)
            act.wait_ge(sem("qr"), tiles(f, t) + 1)
            act.activation(RD[:, b, t, LEFT:LEFT + REL], PS[:, 6, 0:REL], ACT.Copy).then_inc(sem("rd"), 1)

        def exp(i, b, t):
            act.wait_ge(sem("top"), tiles(i, t) + 1)
            act.wait_ge(sem("backs"), tiles(i, t) * 2 - 2 + BACK)
            act.activation(E[:, t % 2], wide(t), ACT.Exp, bias=mx[:, t % 2:t % 2 + 1], scale=SCALE,
                           accum_out=den[:, b, t:t + 1]).then_inc(sem("exp"), 1)

        def back_out(i, b, t):
            act.wait_ge(sem("backs"), tiles(i, t) * 2 + 1 + BACK)
            act.wait_ge(sem("valued"), tiles(i, t) - 1 + VALUED)
            act.activation(PT[:, t % 2, 0:4].rearrange("p j i -> p (j i)"), PS[:, 4], ACT.Copy).then_inc(sem("pt_act"), 1)

        for f in range(NB):
            for t in range(ITILES):
                distances_out(f, f, t)
        with act.Fori(0, HEADS) as n:
            for s in range(NB * ITILES + 1):
                at = lambda lag: (n * 2 + (s - lag) // ITILES, (s - lag) // ITILES, (s - lag) % ITILES)
                if s < NB * ITILES:
                    i, b, t = at(0)
                    distances_out(i + 2, b, t)
                if s >= 1:
                    back_out(*at(1))
                if s < NB * ITILES:
                    exp(i, b, t)

    @block.vector
    def _(dve):
        dve.sem_inc(sem("pt_dve"), PTS)
        dve.sem_inc(sem("added"), ADDED)
        dve.sem_inc(sem("o_out"), OUT)

        def top(i, b, t):
            dve.wait_ge(sem("scores"), tiles(i, t) + 1 + SCORES)
            if t == 0:
                dve.wait_ge(sem("band_in"), (i + 1) * 16)
            lo, hi = max(0, (t - 1) * P), min(PIX, (t + 2) * P)
            u = lo - (t - 1) * P
            v = wide(t)
            dve.tensor_tensor(v[:, lo:hi], v[:, lo:hi], band[:, b, t, u:u + hi - lo], ALU.add).then_inc(sem("added"), 1)
            dve.wait_ge(sem("added"), tiles(i, t) + 1 + ADDED)
            dve.tensor_reduce(raw[:, t % 2:t % 2 + 1], v, AX.X, ALU.max).then_inc(sem("maxed"), 1)
            dve.wait_ge(sem("maxed"), tiles(i, t) + 1)
            dve.tensor_scalar(mx[:, t % 2:t % 2 + 1], raw[:, t % 2:t % 2 + 1], -SCALE, None, ALU.mult).then_inc(sem("top"), 1)

        def back_out(i, b, t):
            dve.wait_ge(sem("backs"), tiles(i, t) * 2 + 2 + BACK)
            dve.wait_ge(sem("valued"), tiles(i, t) - 1 + VALUED)
            dve.tensor_copy(PT[:, t % 2, 4:8].rearrange("p j i -> p (j i)"), PS[:, 5]).then_inc(sem("pt_dve"), 1)

        def outputs(i, n, b):
            dve.wait_ge(sem("exp"), tiles(i, ITILES) + EXP)
            dve.reciprocal(rden[:, b], den[:, b]).then_inc(sem("inverse"), 1)
            dve.wait_ge(sem("inverse"), i + 1)
            dve.wait_ge(sem("valued"), tiles(i, ITILES) + VALUED)
            dve.tensor_tensor(O[:, b * ITILES:(b + 1) * ITILES, bass.ds(n * DH, DH)],
                              PS[:, 7, 0:P].rearrange("p (t d) -> p t d", d=DH), bc(rden[:, b], 2, DH),
                              ALU.mult).then_inc(sem("o_out"), 1)

        with dve.Fori(0, HEADS) as n:
            for s in range(NB * ITILES + 2):
                at = lambda lag: (n * 2 + (s - lag) // ITILES, (s - lag) // ITILES, (s - lag) % ITILES)
                if s >= 2:
                    back_out(*at(2))
                if s < NB * ITILES:
                    top(*at(0))
                if s == ITILES + 1:
                    outputs(n * 2, n, 0)
            outputs(n * 2 + 1, n, 1)

    @block.gpsimd
    def _(pool):
        def repeat_ends(f, b):
            reg_wait(pool, sem("rd"), tiles(f, ITILES) + RDS, sem("pool_passed"))
            pool.tensor_copy(RD[:, b, :, 0:LEFT], RD[:, b, :, LEFT:LEFT + 1].broadcast_to([P, ITILES, LEFT])
                             ).then_inc(sem("ends"), 1)
            r = LEFT + REL
            pool.tensor_copy(RD[:, b, :, r:r + LEFT], RD[:, b, :, r - 1:r].broadcast_to([P, ITILES, LEFT])
                             ).then_inc(sem("ends"), 1)

        def head_queries(q, name, f, head, b):
            pool.tensor_tensor(q[:, b], Qm[:, b * PIX:(b + 1) * PIX],
                               W["hmask"][:, bass.ds(head, 1)].broadcast_to([P, PIX]), ALU.mult).then_inc(sem(name), 1)

        for f in range(NB):
            head_queries(qd, "qd", f, 0, f)
        for f in range(NB):
            head_queries(qh, "qh", f, 0, f)
        for f in range(NB):
            repeat_ends(f, f)
        with pool.Fori(0, HEADS) as n:
            for b in range(NB):
                i = n * 2 + b
                reg_wait(pool, sem("valued"), tiles(i - 1, 0) + VALUED, sem("pool_passed"))
                pool.tensor_copy(VH[:, b], V[:, b, :, bass.ds(n * DH, DH)]).then_inc(sem("vh"), 1)
                head_queries(qd, "qd", i + 2, n + 1, b)
                repeat_ends(i + 2, b)
                reg_wait(pool, sem("added"), tiles(i, ITILES) + ADDED, sem("pool_passed"))
                head_queries(qh, "qh", i + 2, n + 1, b)

    @block.sync
    def _(sp):
        sp.sem_inc(sem("rd_sent"), SENT)

        def skew(f, b):
            sp.wait_ge(sem("ends"), f * 2 + 2)
            sp.dma_start(scratch[b], RD[:, b]).then_inc(sem("rd_sent"), 16)
            sp.wait_ge(sem("rd_sent"), (f + 1) * 16 + SENT)
            sp.wait_ge(sem("added"), tiles(f, 0) - ITILES + ADDED)
            rows = bass.AP(tensor=scratch.tensor, offset=b * P * ITILES * ROW + LEFT,
                           ap=[[ITILES * ROW - 1, P], [ROW, ITILES], [1, WIN]])
            sp.dma_start(band[:, b], rows).then_inc(sem("band_in"), 16)

        for f in range(NB):
            skew(f, f)
        with sp.Fori(0, HEADS) as n:
            for b in range(NB):
                skew(n * 2 + b + 2, b)
        sp.wait_ge(sem("band_in"), (HEADS * NB + 2) * 16)


def l2_output(nc, st, X, PS, W, O, AO):
    sem = st.sem
    with nc.Block() as block:
        @block.tensor
        def _(pe):
            for n in range(NCH):
                for j in range(4):
                    ins = pe.transpose(PS[:, n, j * P:(j + 1) * P], O[:, 4 * n + j], W["ident"])
                ins.then_inc(sem("o_turned"), 1)
            for n in range(NCH):
                pe.wait_ge(sem("ao"), n + 1)
                pe.matmul(PS[:, 4 + n], W["w_out"], AO[:, n * CH:(n + 1) * CH], start=True, stop=True).then_inc(sem("out"), 1)

        @block.scalar
        def _(act):
            for n in range(NCH):
                act.wait_ge(sem("o_turned"), n + 1)
                act.activation(AO[:, n * CH:(n + 1) * CH], PS[:, n], ACT.Copy).then_inc(sem("ao"), 1)

        @block.vector
        def _(dve):
            for n in range(NCH):
                dve.wait_ge(sem("out"), n + 1)
                x = X[:, n * CH:(n + 1) * CH]
                dve.scalar_tensor_tensor(x, PS[:, 4 + n], W["b_out"], x, ALU.add, ALU.add)


HB = 4
NODES = 32
GUESSES = 12
STEPS_N = PIX - 1
DT = 1.0 / (PIX - 1)
CLOSE = 2.0 ** -18


def integration(nodes, times):
    x = np.cos(np.pi * (np.arange(nodes) + 0.5) / nodes)
    k = np.arange(nodes)
    to_coef = 2.0 / nodes * np.cos(np.outer(k, np.arccos(x)))
    to_coef[0] *= 0.5
    t = lambda z: np.cos(np.outer(np.arange(nodes + 2), np.arccos(np.clip(z, -1.0, 1.0))))
    z = 2.0 * times - 1.0
    tz, t0 = t(z), t(np.array([-1.0]))
    anti = np.zeros((nodes, len(times)))
    for n in range(nodes):
        if n == 0:
            a = lambda v: v[1]
        elif n == 1:
            a = lambda v: v[2] / 4.0
        else:
            a = lambda v, n=n: v[n + 1] / (2.0 * (n + 1)) - v[n - 1] / (2.0 * (n - 1))
        anti[n] = a(tz) - a(t0)
    return (0.5 * to_coef.T @ anti).astype(np.float32)


def l2f_pack(w):
    p = Pack()
    L = lambda n: w["L2_ffn_" + n]
    p.add("w1", L("W1").T)
    p.add("w2", L("W2").T.reshape(HB, P, HB * P).transpose(1, 0, 2))
    p.add("w3", L("W3").T.reshape(HB, P, P).transpose(1, 0, 2))
    p.add("b1", L("b1").reshape(HB, P).T)
    p.add("b2", L("b2").reshape(HB, P).T)
    p.add("b3", L("b3").reshape(P, 1))
    p.add("b3_row", np.tile(L("b3").reshape(1, P), (NB * NODES, 1)))
    p.add("mean", np.full((P, P), 1.0 / P, np.float32))
    x = 0.5 + 0.5 * np.cos(np.pi * (np.arange(NODES) + 0.5) / NODES)
    p.add("to_nodes", np.kron(np.eye(NB, dtype=np.float32), integration(NODES, x)))
    p.add("to_steps", np.kron(np.eye(NB, dtype=np.float32), integration(NODES, np.arange(PIX) * DT)))
    return p


def l2_guess(nc, PS, W, Y0, Y):
    with ExitStack() as ctx:
        st = Stage(nc, ctx)
        sb, sem = st.sb, st.sem
        N = NB * NODES
        YN = sb("g_y", [P, N])
        H1 = sb("g_h1", [P, HB, N])
        H2 = sb("g_h2", [P, HB, N])
        F = sb("g_f", [N, P])
        block = ctx.enter_context(nc.Block())

        @block.vector
        def _(dve):
            dve.tensor_copy(YN[:].rearrange("p (b n) -> p b n", b=NB), bc(Y0[:], 2, NODES)).then_inc(sem("y"), 1)
            with dve.Fori(0, GUESSES) as g:
                dve.wait_ge(sem("f"), g + 1)
                dve.tensor_tensor(F[:], PS[0:N, 2, 0:P], W["b3_row"], ALU.add).then_inc(sem("f_out"), 1)
                dve.wait_ge(sem("moved"), g + 1)
                dve.tensor_tensor(YN[:].rearrange("p (b n) -> p b n", b=NB),
                                  PS[:, 3, 0:N].rearrange("p (b n) -> p b n", b=NB), bc(Y0[:], 2, NODES),
                                  ALU.add).then_inc(sem("y"), 1)
            for n in range(NCH):
                dve.wait_ge(sem("steps"), n + 1)
                dve.tensor_scalar(Y[:, n * CH:(n + 1) * CH], PS[:, 4 + n], Y0[:, n // 2:n // 2 + 1], None, ALU.add)

        @block.scalar
        def _(act):
            with act.Fori(0, GUESSES) as g:
                for k in range(HB):
                    act.wait_ge(sem("z1"), g + 1)
                    act.activation(H1[:, k], PS[:, 0, k * N:(k + 1) * N], ACT.Tanh, bias=W["b1"][:, k:k + 1]
                                   ).then_inc(sem("h1"), 1)
                for k in range(HB):
                    act.wait_ge(sem("z2"), g + 1)
                    act.activation(H2[:, k], PS[:, 1, k * N:(k + 1) * N], ACT.Tanh, bias=W["b2"][:, k:k + 1]
                                   ).then_inc(sem("h2"), 1)

        @block.tensor
        def _(pe):
            with pe.Fori(0, GUESSES) as g:
                pe.wait_ge(sem("y"), g + 1)
                for k in range(HB):
                    ins = pe.matmul(PS[:, 0, k * N:(k + 1) * N], W["w1"][:, k * P:(k + 1) * P], YN[:], start=True, stop=True)
                ins.then_inc(sem("z1"), 1)
                pe.wait_ge(sem("h1"), g * HB + HB)
                for k in range(HB):
                    for m in range(HB):
                        c = (m * HB + k) * P
                        ins = pe.matmul(PS[:, 1, k * N:(k + 1) * N], W["w2"][:, c:c + P], H1[:, m], start=(m == 0),
                                        stop=(m == HB - 1))
                ins.then_inc(sem("z2"), 1)
                pe.wait_ge(sem("h2"), g * HB + HB)
                for m in range(HB):
                    ins = pe.matmul(PS[0:N, 2, 0:P], H2[:, m], W["w3"][:, m * P:(m + 1) * P], start=(m == 0),
                                    stop=(m == HB - 1))
                ins.then_inc(sem("f"), 1)
                reg_wait(pe, sem("f_out"), g + 1, sem("pe_passed"))
                pe.matmul(PS[:, 3, 0:N], F[:], W["to_nodes"], start=True, stop=True).then_inc(sem("moved"), 1)
            for n in range(NCH):
                pe.matmul(PS[:, 4 + n], F[:], W["to_steps"][:, n * CH:(n + 1) * CH], start=True,
                          stop=True).then_inc(sem("steps"), 1)


def l2_sweeps(nc, PS, W, Y0, Y):
    with ExitStack() as ctx:
        st = Stage(nc, ctx)
        sb, sem = st.sb, st.sem
        Z = sb("s_z", [P, 2, CH])
        KS = sb("s_k", [P, 2, CH])
        S = sb("s_sum", [P, T])
        H1 = sb("s_h1", [P, 2, HB, CH])
        H2 = sb("s_h2", [P, 2, HB, CH])
        NEW = sb("s_new", [P, T])
        ones = sb("s_ones", [P, PIX])
        gap = sb("s_gap", [P, 2])
        size = sb("s_size", [P, 1])
        off = sb("s_off", [P, 1])
        flag = sb("s_flag", [1, 1], I32)
        EV = 4
        GROUPS = EV * 2 * (2 * HB + 1)
        block = ctx.enter_context(nc.Block())

        def schedule():
            out = []
            for e in range(EV):
                for layer in range(3):
                    for c in range(2):
                        for k in range(HB if layer < 2 else 1):
                            out.append((e, layer, c, k))
            return out

        GR = schedule()
        acts = [g for g, x in enumerate(GR) if x[1] < 2]
        dves = [g for g, x in enumerate(GR) if x[1] == 2]
        NA, ND = len(acts), len(dves)

        @block.tensor
        def _(pe):
            end = pe.alloc_register("pe_end")
            pe.reg_mov(end, STEPS_N)
            with pe.Fori(0, end) as sweep:
                with pe.Fori(0, NB) as b:
                    it = sweep * 2 + b
                    for g, (e, layer, c, k) in enumerate(GR):
                        if g >= 8:
                            before = g - 8
                            if before in acts:
                                pe.wait_ge(sem("tanh"), it * NA + acts.index(before) + 1)
                            else:
                                pe.wait_ge(sem("taken"), it * ND + dves.index(before) + 1)
                        elif g == 0:
                            pe.wait_ge(sem("free"), it + 1)
                        bank = PS[:, g % 8]
                        if layer == 0:
                            if e == 0:
                                if c == 0 and k == 0:
                                    pe.wait_ge(sem("y"), sweep + 1)
                                x = Y[:, bass.ds(b * PIX + c * CH, CH)]
                            else:
                                if k == 0:
                                    pe.wait_ge(sem("z"), (it * (EV - 1) + e - 1) * 2 + c + 1)
                                x = Z[:, c]
                            pe.matmul(bank, W["w1"][:, k * P:(k + 1) * P], x, start=True, stop=True).then_inc(sem("filled"), 1)
                        elif layer == 1:
                            if k == 0:
                                pe.wait_ge(sem("tanh"), it * NA + (e * 2 * 2 + c) * HB + HB)
                            for m in range(HB):
                                col = (m * HB + k) * P
                                ins = pe.matmul(bank, W["w2"][:, col:col + P], H1[:, c, m], start=(m == 0), stop=(m == HB - 1))
                            ins.then_inc(sem("filled"), 1)
                        else:
                            pe.wait_ge(sem("tanh"), it * NA + ((e * 2 + 1) * 2 + c) * HB + HB)
                            for m in range(HB):
                                ins = pe.matmul(bank, W["w3"][:, m * P:(m + 1) * P], H2[:, c, m], start=(m == 0),
                                                stop=(m == HB - 1))
                            ins.then_inc(sem("filled"), 1)
                reg_wait(pe, sem("off"), sweep + 1, sem("pe_passed"))
                pe.matmul(PS[0:1, 0, 0:1], off[:], ones[:, 0:1], start=True, stop=True).then_inc(sem("count"), 1)
                reg_wait(pe, sem("flag"), sweep + 1, sem("pe_passed"))
                pe.reg_load(end, flag[0:1, 0:1])

        @block.scalar
        def _(act):
            end = act.alloc_register("act_end")
            act.reg_mov(end, STEPS_N)
            with act.Fori(0, end) as sweep:
                with act.Fori(0, NB) as b:
                    it = sweep * 2 + b
                    for g in acts:
                        e, layer, c, k = GR[g]
                        act.wait_ge(sem("filled"), it * GROUPS + g + 1)
                        H = H1 if layer == 0 else H2
                        bias = W["b1" if layer == 0 else "b2"][:, k:k + 1]
                        act.activation(H[:, c, k], PS[:, g % 8], ACT.Tanh, bias=bias).then_inc(sem("tanh"), 1)
                reg_wait(act, sem("flag"), sweep + 1, sem("act_passed"))
                act.reg_load(end, flag[0:1, 0:1])

        @block.vector
        def _(dve):
            end = dve.alloc_register("dve_end")
            dve.reg_mov(end, STEPS_N)
            dve.memset(ones[:], 1.0)
            dve.sem_inc(sem("y"), 1)
            dve.sem_inc(sem("free"), 1)
            with dve.Fori(0, end) as sweep:
                with dve.Fori(0, NB) as b:
                    it = sweep * 2 + b
                    for d, g in enumerate(dves):
                        e, _, c, _ = GR[g]
                        dve.wait_ge(sem("filled"), it * GROUPS + g + 1)
                        s = S[:, bass.ds(b * PIX + c * CH, CH)]
                        y = Y[:, bass.ds(b * PIX + c * CH, CH)]
                        if e < EV - 1:
                            dve.tensor_scalar(KS[:, c], PS[:, g % 8], W["b3"], None, ALU.add).then_inc(sem("k"), 1)
                            dve.wait_ge(sem("k"), (it * (EV - 1) + e) * 2 + c + 1)
                            dve.scalar_tensor_tensor(Z[:, c], KS[:, c], DT / 2.0 if e < 2 else DT, y, ALU.mult,
                                                     ALU.add).then_inc(sem("z"), 1)
                            if e == 0:
                                dve.tensor_copy(s, KS[:, c]).then_inc(sem("taken"), 1)
                            else:
                                dve.scalar_tensor_tensor(s, KS[:, c], 2.0, s, ALU.mult, ALU.add).then_inc(sem("taken"), 1)
                            dve.wait_ge(sem("taken"), it * ND + d + 1)
                        else:
                            dve.scalar_tensor_tensor(s, PS[:, g % 8], W["b3"], s, ALU.add, ALU.add).then_inc(sem("taken"), 1)
                    dve.wait_ge(sem("taken"), it * ND + ND)
                    dve.sem_inc(sem("free"), 1)
                dve.tensor_scalar(S[:], S[:], DT / 6.0, None, ALU.mult).then_inc(sem("scaled"), 1)
                dve.wait_ge(sem("scaled"), sweep + 1)
                for b in range(NB):
                    c = b * PIX
                    dve.tensor_copy(NEW[:, c:c + 1], Y0[:, b:b + 1]).then_inc(sem("new"), 1)
                    dve.tensor_tensor_scan(NEW[:, c + 1:c + PIX], ones[:, 0:PIX - 1], S[:, c:c + PIX - 1],
                                           Y0[:, b:b + 1], ALU.mult, ALU.add).then_inc(sem("new"), 1)
                dve.wait_ge(sem("new"), sweep * 4 + 4)
                dve.tensor_tensor(S[:], NEW[:], Y[:], ALU.subtract).then_inc(sem("gap"), 1)
                dve.wait_ge(sem("gap"), sweep * 3 + 1)
                dve.tensor_reduce(gap[:, 0:1], S[:], AX.X, ALU.max, apply_absolute_value=True)
                dve.tensor_reduce(size[:], NEW[:], AX.X, ALU.max, apply_absolute_value=True).then_inc(sem("gap"), 1)
                dve.wait_ge(sem("gap"), sweep * 3 + 2)
                dve.tensor_scalar(size[:], size[:], 1.0, CLOSE, ALU.add, ALU.mult).then_inc(sem("gap"), 1)
                dve.wait_ge(sem("gap"), sweep * 3 + 3)
                dve.tensor_tensor(off[:], gap[:, 0:1], size[:], ALU.is_gt).then_inc(sem("off"), 1)
                dve.tensor_copy(Y[:], NEW[:]).then_inc(sem("y"), 1)
                dve.wait_ge(sem("count"), sweep + 1)
                dve.tensor_scalar(flag[:], PS[0:1, 0, 0:1], 0.5, float(STEPS_N), ALU.is_gt, ALU.mult).then_inc(sem("flag"), 1)
                dve.wait_ge(sem("y"), sweep + 2)
                reg_wait(dve, sem("flag"), sweep + 1, sem("dve_passed"))
                dve.reg_load(end, flag[0:1, 0:1])


def l2_trajectory(nc, X, XN, PS, W):
    with ExitStack() as ctx:
        Y0 = ctx.enter_context(nc.sbuf_tensor("t_y0", [P, NB], F32))
        Y = ctx.enter_context(nc.sbuf_tensor("t_y", [P, T], F32))
        with nc.Block() as block:
            @block.vector
            def _(dve):
                dve.tensor_copy(Y0[:], XN[:, 0:T:PIX])
        l2_guess(nc, PS, W, Y0, Y)
        l2_sweeps(nc, PS, W, Y0, Y)
        with nc.Block() as block:
            @block.vector
            def _(dve):
                dve.tensor_tensor(X[:], X[:], Y[:], ALU.add)


GH = 4
GK = 16
GV = 32
GC = 16
GLOW = 16
CPT = P // GC
GD = GH * GK


def l3a_pack(w):
    p = Pack()
    L = lambda n: w["L3_attn_" + n]
    p.add("wq", L("Wq").T)
    p.add("wk", L("Wk").T)
    p.add("wv", L("Wv").T)
    p.add("wg", L("Wg").T)
    p.add("wo", L("Wo").T)
    p.add("wgk1", L("Wgk1").T)
    p.add("wgk2", L("Wgk2").T)
    p.add("bgk2", np.tile(L("bgk2"), NB).reshape(P, 1))
    p.add("g_norm", np.tile(L("g_norm_w"), GH).reshape(P, 1))
    p.add("ident", np.eye(P, dtype=np.float32))
    p.add("mean", np.full((P, P), 1.0 / P, np.float32))
    p.add("head_mean", np.kron(np.eye(GH), np.full((GV, GV), 1.0 / GV)).astype(np.float32))
    p.add("hmask", np.kron(np.eye(NB * GH), np.ones((GK, 1))).astype(np.float32))
    p.add("cmask", np.kron(np.eye(CPT), np.ones((GC, 1))).astype(np.float32))
    p.add("causal", np.kron(np.eye(CPT), np.triu(np.ones((GC, GC)))).astype(np.float32))
    return p


def l3_gates(nc, PS, W, XN, QE, KE, KD, V, QM, decay):
    with ExitStack() as ctx:
        st = Stage(nc, ctx)
        sb, sem = st.sb, st.sem
        low = sb("ga_low", [GLOW, T])
        KP = sb("ga_k", [P, PIX])
        z = sb("ga_z", [P, PIX])
        mag = sb("ga_mag", [P, PIX])
        gk = sb("ga_gk", [P, PIX])
        keep = sb("ga_keep", [P, PIX])
        cum = sb("ga_cum", [P, PIX])
        ex = sb("ga_ex", [P, 3, PIX])
        rest = sb("ga_rest", [P, PIX])
        block = ctx.enter_context(nc.Block())
        chunks = lambda v: v.rearrange("p (n c) -> p n c", c=GC)

        @block.tensor
        def _(pe):
            for k, name in enumerate(("wq", "wk")):
                for h in range(2):
                    for b in range(NB):
                        c = b * PIX + h * CH
                        ins = pe.matmul(PS[GD * b:GD * b + GD, 2 * k + h], W[name], XN[:, c:c + CH], start=True, stop=True,
                                        skip_group_check=True)
                    ins.then_inc(sem("qk"), 1)
            for n in range(NCH):
                pe.matmul(PS[0:GLOW, 4 + n], W["wgk1"], XN[:, n * CH:(n + 1) * CH], start=True,
                          stop=True).then_inc(sem("low"), 1)
            pe.wait_ge(sem("low_out"), NCH)
            for h in range(2):
                for b in range(NB):
                    c = b * PIX + h * CH
                    ins = pe.matmul(PS[GD * b:GD * b + GD, 4 + h], W["wgk2"], low[:, c:c + CH], start=True, stop=True,
                                    skip_group_check=True)
            ins.then_inc(sem("gate"), 1)
            pe.wait_ge(sem("qk_out"), 4)
            for n in range(4):
                for j in range(4):
                    t = 4 * n + j
                    ins = pe.matmul(PS[:, n, j * P:(j + 1) * P], XN[:, t * P:(t + 1) * P], W["wv"], start=True, stop=True)
                ins.then_inc(sem("v"), 1)

        @block.scalar
        def _(act):
            for n in range(NCH):
                act.wait_ge(sem("low"), n + 1)
                act.activation(low[:, n * CH:(n + 1) * CH], PS[0:GLOW, 4 + n], ACT.Copy).then_inc(sem("low_out"), 1)
            link = Chain(act, sem("act_chain"))
            act.wait_ge(sem("gate"), 1)
            link(act.activation(z[:], PS[:, 4:6].rearrange("p a n -> p (a n)"), ACT.Identity, bias=W["bgk2"]))
            act.sem_inc(sem("z"), 1)
            link(act.activation(mag[:], z[:], ACT.Abs))
            link(act.activation(mag[:], mag[:], ACT.Exp, scale=-1.0))
            act.activation(mag[:], mag[:], ACT.Ln, bias=1.0).then_inc(sem("log"), 1)
            for n in range(4):
                act.wait_ge(sem("v"), n + 1)
                act.activation(V[:, n // 2, 4 * (n % 2):4 * (n % 2) + 4].rearrange("p c k -> p (c k)"), PS[:, n], ACT.Copy)
            act.wait_ge(sem("cum"), 1)
            act.activation(ex[:, 0], cum[:], ACT.Exp).then_inc(sem("ex"), 1)
            act.activation(ex[:, 1], cum[:], ACT.Exp, scale=-1.0).then_inc(sem("ex"), 1)
            act.activation(decay[:], cum[:, GC - 1::GC], ACT.Exp)
            act.wait_ge(sem("rest"), 1)
            act.activation(ex[:, 2], rest[:], ACT.Exp).then_inc(sem("ex"), 1)

        @block.gpsimd
        def _(pool):
            pool.memset(keep[:], 1.0).then_inc(sem("ones"), 1)
            pool.wait_ge(sem("ones"), 1)
            pool.memset(chunks(keep[:])[:, :, 0:1], 0.0).then_inc(sem("keep"), 1)
            for n in range(NB * GH):
                pool.wait_ge(sem("qe"), 1)
                pool.tensor_tensor(QM[:, n], QE[:], W["hmask"][:, n:n + 1].broadcast_to([P, PIX]), ALU.mult)

        @block.vector
        def _(dve):
            link = Chain(dve, sem("dve_chain"))
            for h in range(2):
                dve.wait_ge(sem("qk"), h + 1)
                dve.tensor_scalar(QE[:, h * CH:(h + 1) * CH], PS[:, h], GK ** -0.5, None, ALU.mult).then_inc(sem("qk_out"), 1)
            for h in range(2):
                dve.wait_ge(sem("qk"), h + 3)
                dve.tensor_copy(KP[:, h * CH:(h + 1) * CH], PS[:, 2 + h]).then_inc(sem("qk_out"), 1)
            dve.wait_ge(sem("z"), 1)
            link(dve.tensor_scalar(gk[:], z[:], 0.0, None, ALU.min))
            dve.wait_ge(sem("log"), 1)
            link(dve.tensor_tensor(gk[:], gk[:], mag[:], ALU.subtract))
            link(dve.tensor_scalar(gk[:], gk[:], 1.0 / 16.0, None, ALU.mult))
            dve.wait_ge(sem("keep"), 1)
            link(dve.tensor_tensor_scan(cum[:], keep[:], gk[:], 0.0, ALU.mult, ALU.add))
            dve.sem_inc(sem("cum"), 1)
            c3 = chunks(cum[:])
            dve.tensor_tensor(chunks(rest[:]), c3[:, :, GC - 1:GC].broadcast_to([P, PIX // GC, GC]), c3,
                              ALU.subtract).then_inc(sem("rest"), 1)
            dve.wait_ge(sem("ex"), 1)
            dve.wait_ge(sem("qk_out"), 4)
            dve.tensor_tensor(QE[:], QE[:], ex[:, 0], ALU.mult).then_inc(sem("qe"), 1)
            dve.wait_ge(sem("ex"), 2)
            dve.tensor_tensor(KE[:], KP[:], ex[:, 1], ALU.mult)
            dve.wait_ge(sem("ex"), 3)
            dve.tensor_tensor(KD[:], KP[:], ex[:, 2], ALU.mult)


def l3_chunks(nc, PS, W, KE, KD, V, QM, decay, OT):
    with ExitStack() as ctx:
        st = Stage(nc, ctx)
        sb, sem = st.sb, st.sem
        KDM = sb("gb_kdm", [P, 2, CPT, P])
        S = sb("gb_s", [P, PIX // GC + 1, P])
        AM = sb("gb_a", [P, NB, GH, P])
        block = ctx.enter_context(nc.Block())

        @block.vector
        def _(dve):
            dve.memset(S[:, 0], 0.0).then_inc(sem("state"), 1)

            def keys(t):
                dve.wait_ge(sem("turned"), t + 1)
                if t >= 2:
                    dve.wait_ge(sem("kv"), t - 1)
                dve.tensor_tensor(KDM[:, t % 2], bc(PS[:, t % 2, 0:P], 1, CPT), bc(W["cmask"], 2, P),
                                  ALU.mult).then_inc(sem("kdm"), 1)

            def states(t):
                dve.wait_ge(sem("kv"), t + 1)
                for j in range(CPT):
                    n = t * CPT + j
                    dve.wait_ge(sem("state"), n + 1)
                    dve.scalar_tensor_tensor(S[:, n + 1], S[:, n], decay[:, n:n + 1],
                                             PS[:, 2 + j // 4, (j % 4) * P:(j % 4 + 1) * P], ALU.mult,
                                             ALU.add).then_inc(sem("state"), 1)

            def masked(t):
                for b in range(NB):
                    dve.wait_ge(sem("scores"), NB * t + b + 1)
                    if t >= 1:
                        dve.wait_ge(sem("outs"), NB * (t - 1) + b + 1)
                    dve.tensor_tensor(AM[:, b], PS[:, 4 + b].rearrange("p (h c) -> p h c", h=GH), bc(W["causal"], 1, GH),
                                      ALU.mult).then_inc(sem("am"), 1)

            keys(0)
            for t in range(ITILES):
                if t + 1 < ITILES:
                    keys(t + 1)
                masked(t)
                states(t)

        @block.scalar
        def _(act):
            for t in range(ITILES):
                for b in range(NB):
                    act.wait_ge(sem("outs"), NB * t + b + 1)
                    c = b * PIX + t * P
                    act.activation(OT[:, c:c + P], PS[:, 6 + b, 0:P], ACT.Copy).then_inc(sem("ot"), 1)

        @block.tensor
        def _(pe):
            def turn(t):
                if t >= 2:
                    pe.wait_ge(sem("kdm"), t - 1)
                pe.transpose(PS[:, t % 2, 0:P], KD[:, t * P:(t + 1) * P], W["ident"]).then_inc(sem("turned"), 1)

            def key_values(t):
                pe.wait_ge(sem("kdm"), t + 1)
                pe.wait_ge(sem("state"), t * CPT + 1)
                for j in range(CPT):
                    for b in range(NB):
                        ins = pe.matmul(PS[GD * b:GD * b + GD, 2 + j // 4, (j % 4) * P:(j % 4 + 1) * P],
                                        KDM[:, t % 2, j, GD * b:GD * b + GD], V[:, b, t], start=True, stop=True,
                                        skip_group_check=True)
                ins.then_inc(sem("kv"), 1)

            def scores(t):
                for b in range(NB):
                    if t >= 1:
                        pe.wait_ge(sem("am"), NB * (t - 1) + b + 1)
                    pe.matmul(PS[:, 4 + b], KE[:, t * P:(t + 1) * P], QM[:, GH * b:GH * b + GH, t * P:(t + 1) * P],
                              start=True, stop=True).then_inc(sem("scores"), 1)

            def outputs(t):
                for b in range(NB):
                    pe.wait_ge(sem("am"), NB * t + b + 1)
                    if t >= 1:
                        pe.wait_ge(sem("ot"), NB * (t - 1) + b + 1)
                    for h in range(GH):
                        pe.matmul(PS[GV * h:GV * h + GV, 6 + b, 0:P], V[:, b, t, GV * h:GV * h + GV], AM[:, b, h],
                                  start=True, stop=False, skip_group_check=True)
                    pe.wait_ge(sem("state"), (t + 1) * CPT)
                    for j in range(CPT):
                        c = t * P + j * GC
                        for h in range(GH):
                            ins = pe.matmul(PS[GV * h:GV * h + GV, 6 + b, j * GC:(j + 1) * GC],
                                            S[:, t * CPT + j, GV * h:GV * h + GV], QM[:, GH * b + h, c:c + GC],
                                            start=False, stop=(j == CPT - 1), skip_group_check=True)
                    ins.then_inc(sem("outs"), 1)

            turn(0)
            for t in range(ITILES):
                if t + 1 < ITILES:
                    turn(t + 1)
                scores(t)
                key_values(t)
                outputs(t)


def l3_gated_output(nc, X, PS, W, XN, OT):
    with ExitStack() as ctx:
        st = Stage(nc, ctx)
        sb, sem = st.sb, st.sem
        SQ = sb("go_sq", [P, 2, CH])
        R = sb("go_r", [P, T])
        G = sb("go_g", [P, T])
        block = ctx.enter_context(nc.Block())
        col = lambda n: slice(n * CH, (n + 1) * CH)

        @block.tensor
        def _(pe):
            for n in range(NCH):
                pe.matmul(PS[:, n], W["wg"], XN[:, col(n)], start=True, stop=True).then_inc(sem("g"), 1)
            for n in range(NCH):
                pe.wait_ge(sem("square"), n + 1)
                pe.matmul(PS[:, 4 + n], W["head_mean"], SQ[:, n % 2], start=True, stop=True).then_inc(sem("ms"), 1)
            for n in range(NCH):
                pe.wait_ge(sem("gated"), n + 1)
                pe.matmul(PS[:, n], W["wo"], OT[:, col(n)], start=True, stop=True).then_inc(sem("out"), 1)

        @block.scalar
        def _(act):
            for n in range(NCH):
                if n >= 2:
                    act.wait_ge(sem("ms"), n - 1)
                act.activation(SQ[:, n % 2], OT[:, col(n)], ACT.Square).then_inc(sem("square"), 1)
            for n in range(NCH):
                act.wait_ge(sem("g"), n + 1)
                act.activation(G[:, col(n)], PS[:, n], ACT.Silu).then_inc(sem("silu"), 1)
            for n in range(NCH):
                act.wait_ge(sem("inverse"), n + 1)
                act.activation(R[:, col(n)], R[:, col(n)], ACT.Sqrt).then_inc(sem("root"), 1)

        @block.vector
        def _(dve):
            for n in range(NCH):
                dve.wait_ge(sem("ms"), n + 1)
                dve.tensor_scalar(R[:, col(n)], PS[:, 4 + n], 1e-5, None, ALU.add).then_inc(sem("eps"), 1)
                dve.wait_ge(sem("eps"), n + 1)
                dve.reciprocal(R[:, col(n)], R[:, col(n)]).then_inc(sem("inverse"), 1)
            for n in range(NCH):
                dve.wait_ge(sem("silu"), n + 1)
                dve.scalar_tensor_tensor(G[:, col(n)], G[:, col(n)], W["g_norm"], OT[:, col(n)], ALU.mult,
                                         ALU.mult).then_inc(sem("weighted"), 1)
                dve.wait_ge(sem("root"), n + 1)
                dve.wait_ge(sem("weighted"), n + 1)
                dve.tensor_tensor(OT[:, col(n)], G[:, col(n)], R[:, col(n)], ALU.mult).then_inc(sem("gated"), 1)
            for n in range(NCH):
                dve.wait_ge(sem("out"), n + 1)
                dve.tensor_tensor(X[:, col(n)], PS[:, n], X[:, col(n)], ALU.add)


def l3_attention(nc, X, XN, PS, W):
    with ExitStack() as ctx:
        sb = lambda name, shape: ctx.enter_context(nc.sbuf_tensor(name, shape, F32))
        OT = sb("gl_o", [P, T])
        with ExitStack() as inner:
            own = lambda name, shape: inner.enter_context(nc.sbuf_tensor(name, shape, F32))
            QE = own("gl_qe", [P, PIX])
            KE = own("gl_ke", [P, PIX])
            KD = own("gl_kd", [P, PIX])
            V = own("gl_v", [P, NB, ITILES, P])
            QM = own("gl_qm", [P, NB * GH, PIX])
            decay = own("gl_decay", [P, PIX // GC])
            l3_gates(nc, PS, W, XN, QE, KE, KD, V, QM, decay)
            l3_chunks(nc, PS, W, KE, KD, V, QM, decay, OT)
        l3_gated_output(nc, X, PS, W, XN, OT)


EXPERTS = 32
EH = 32
EB = EXPERTS * EH // P
TT = T // P


def l3f_pack(w):
    p = Pack()
    L = lambda n: w["L3_ffn_" + n]
    p.add("select", L("expert_sel").T)
    p.add("keys", L("keys").transpose(1, 0, 2))
    p.add("values", L("values").reshape(EB, P, P).transpose(1, 0, 2))
    p.add("ident", np.eye(P, dtype=np.float32))
    p.add("mean", np.full((P, P), 1.0 / P, np.float32))
    p.add("index", np.tile(np.arange(EXPERTS, dtype=np.float32), (P, 1)))
    return p


def l3_experts(nc, X, XN, PS, W):
    with ExitStack() as ctx:
        st = Stage(nc, ctx)
        sb, sem = st.sb, st.sem
        SEL = sb("ex_sel", [P, TT, EXPERTS])
        best = sb("ex_best", [P, TT, 8])
        which = sb("ex_which", [P, TT, 8], mybir.dt.uint32)
        at = sb("ex_at", [P, TT, 8])
        hit = sb("ex_hit", [P, 2, TT, EXPERTS])
        GW = sb("ex_w", [P, TT, EXPERTS])
        H = sb("ex_h", [P, 2, EXPERTS, EH])
        HT = sb("ex_ht", [P, 2, EB, CH])
        block = ctx.enter_context(nc.Block())

        @block.tensor
        def _(pe):
            for t in range(TT):
                ins = pe.matmul(PS[:, 6, t * EXPERTS:(t + 1) * EXPERTS], XN[:, t * P:(t + 1) * P], W["select"],
                                start=True, stop=True)
            ins.then_inc(sem("select"), 1)

            def hidden(t):
                if t >= 2:
                    pe.wait_ge(sem("weighted"), 2 * (t - 1))
                for k in range(2):
                    ins = pe.matmul(PS[:, 2 * (t % 2) + k], XN[:, t * P:(t + 1) * P], W["keys"][:, k * CH:(k + 1) * CH],
                                    start=True, stop=True)
                ins.then_inc(sem("hidden"), 1)

            def turn(t):
                pe.wait_ge(sem("weighted"), 2 * (t + 1))
                for k in range(2):
                    if t >= 1:
                        pe.wait_ge(sem("ht"), 2 * (t - 1) + k + 1)
                    for j in range(4):
                        ins = pe.transpose(PS[:, 4 + k, j * P:(j + 1) * P],
                                           H[:, t % 2, 4 * (4 * k + j):4 * (4 * k + j) + 4].rearrange("p e h -> p (e h)"),
                                           W["ident"])
                    ins.then_inc(sem("turned"), 1)

            def values(n):
                pe.wait_ge(sem("ht"), 2 * 4 * (n + 1))
                if n >= 2:
                    pe.wait_ge(sem("added"), n - 1)
                if n == 0:
                    pe.wait_ge(sem("scores"), 1)
                for j in range(EB):
                    ins = pe.matmul(PS[:, 6 + n % 2], W["values"][:, j * P:(j + 1) * P], HT[:, n % 2, j],
                                    start=(j == 0), stop=(j == EB - 1))
                ins.then_inc(sem("out"), 1)

            for t in range(TT + 1):
                if t < TT:
                    hidden(t)
                if t >= 1:
                    turn(t - 1)
                if t >= 5 and (t - 5) % 4 == 0:
                    values((t - 5) // 4)
            values(NCH - 1)

        @block.scalar
        def _(act):
            act.wait_ge(sem("select"), 1)
            act.activation(SEL[:].rearrange("p t e -> p (t e)"), PS[:, 6], ACT.Sigmoid).then_inc(sem("scores"), 1)
            for t in range(TT):
                n = t // 4
                for k in range(2):
                    act.wait_ge(sem("turned"), 2 * t + k + 1)
                    if n >= 2 and t % 4 == 0:
                        act.wait_ge(sem("out"), n - 1)
                    act.activation(HT[:, n % 2, 4 * k:4 * k + 4, (t % 4) * P:(t % 4 + 1) * P],
                                   PS[:, 4 + k].rearrange("p (j c) -> p j c", j=4), ACT.Copy).then_inc(sem("ht"), 1)

        @block.vector
        def _(dve):
            link = Chain(dve, sem("dve_chain"))
            dve.wait_ge(sem("scores"), 1)
            for t in range(TT):
                ins = dve.max(best[:, t], SEL[:, t])
            link(ins)
            for t in range(TT):
                ins = dve.max_index(which[:, t], best[:, t], SEL[:, t])
            link(ins)
            link(dve.tensor_copy(at[:], which[:]))
            index = bc(W["index"], 1, TT)
            for k in range(2):
                link(dve.tensor_tensor(hit[:, k], index, at[:, :, k:k + 1].broadcast_to([P, TT, EXPERTS]), ALU.is_equal))
            link(dve.tensor_tensor(hit[:, 0], hit[:, 0], hit[:, 1], ALU.add))
            link(dve.tensor_tensor(GW[:], SEL[:], hit[:, 0], ALU.mult))

            def added(n):
                dve.wait_ge(sem("out"), n + 1)
                x = X[:, n * CH:(n + 1) * CH]
                dve.tensor_tensor(x, PS[:, 6 + n % 2], x, ALU.add).then_inc(sem("added"), 1)

            for t in range(TT):
                dve.wait_ge(sem("hidden"), t + 1)
                if t >= 2:
                    dve.wait_ge(sem("turned"), 2 * (t - 1))
                for k in range(2):
                    e = slice(16 * k, 16 * k + 16)
                    dve.scalar_tensor_tensor(H[:, t % 2, e], PS[:, 2 * (t % 2) + k].rearrange("p (e h) -> p e h", h=EH),
                                             0.0, bc(GW[:, t, e], 2, EH), ALU.max, ALU.mult).then_inc(sem("weighted"), 1)
                if t >= 6 and (t - 6) % 4 == 0:
                    added((t - 6) // 4)
            added(NCH - 1)


PACKS = [("l0", l0_pack), ("l1", l1_pack), ("l2a", l2a_pack), ("l2f", l2f_pack), ("l3a", l3a_pack), ("l3f", l3f_pack)]


def build(nc, x_dram, packs, offsets, out_dram):
    with ExitStack() as ctx:
        sb = lambda name, shape: ctx.enter_context(nc.sbuf_tensor(name, shape, F32))
        sem = lambda name: ctx.enter_context(nc.semaphore(name))
        X = sb("residual", [P, T])
        PS = ctx.enter_context(nc.psum_tensor("banks", [P, 8, CH], F32))
        x_in, stored = sem("x_in"), sem("stored")

        def dump(what):
            with nc.Block() as block:
                @block.sync
                def _(sp):
                    for b in range(NB):
                        sp.dma_start(out_dram[b].rearrange("c h w -> c (h w)"), what[:, b * PIX:(b + 1) * PIX]
                                     ).then_inc(stored, 16)
                    sp.wait_ge(stored, 32)

        def load(stage, name):
            tile = stage.enter_context(nc.sbuf_tensor("pack_" + name, [P, packs[name].shape[1]], F32))
            arrived = stage.enter_context(nc.semaphore("arrived_" + name))
            with nc.Block() as block:
                @block.sync
                def _(sp):
                    sp.dma_start(tile[:], packs[name]).then_inc(arrived, 16)
                    sp.wait_ge(arrived, 16)
            return Weights(tile, offsets[name]), arrived

        with ExitStack() as l0:
            W, arrived = load(l0, "l0")
            with ExitStack() as att:
                own = lambda name, shape: att.enter_context(nc.sbuf_tensor(name, shape, F32))
                KM = own("l0_km", [P, NB, HEADS, KEYS])
                VT = own("l0_vt", [P, NB * PAIRS, P])
                Q = own("l0_q", [P, T])
                SALL = own("l0_scores", [P, NB * PAIRS * 2, HALF])
                with ExitStack() as sc:
                    A = sc.enter_context(nc.sbuf_tensor("l0_a", [P, NB * PAIRS, 32, HW], F32))
                    B = sc.enter_context(nc.sbuf_tensor("l0_b", [P, NB * PAIRS, 32, HW], F32))
                    l0_prepare(nc, X, PS, W, arrived, KM, VT, Q, A, B, x_dram, x_in)
                    l0_scores(nc, PS, W, KM, Q, A, B, SALL)
                l0_attend(nc, X, PS, W, SALL, VT)
            l0_mlp(nc, X, PS, W)
        with ExitStack() as l1:
            W, arrived = load(l1, "l1")
            l1_attention(nc, X, PS, W)
        XN = sb("normed", [P, T])
        scratch = nc.dram_tensor("distances", (NB, P, ITILES, ROW), F32, kind="Internal").ap()
        with ExitStack() as l2a:
            W, arrived = load(l2a, "l2a")
            layer_norm(nc, "l2a_norm", X, XN, PS, W["mean"])
            l2_attention(nc, X, XN, PS, W, scratch)
        with ExitStack() as l2f:
            W, arrived = load(l2f, "l2f")
            layer_norm(nc, "l2f_norm", X, XN, PS, W["mean"])
            l2_trajectory(nc, X, XN, PS, W)
        with ExitStack() as l3a:
            W, arrived = load(l3a, "l3a")
            layer_norm(nc, "l3a_norm", X, XN, PS, W["mean"])
            l3_attention(nc, X, XN, PS, W)
        with ExitStack() as l3f:
            W, arrived = load(l3f, "l3f")
            layer_norm(nc, "l3f_norm", X, XN, PS, W["mean"])
            l3_experts(nc, X, XN, PS, W)
        dump(X)


def kernel(**inputs):
    import concourse.bacc as bacc
    from concourse.bass_utils import run_bass_kernel_spmd

    nc = bacc.Bacc("TRN2", target_bir_lowering=False, num_devices=1)
    w = {k: np.asarray(v) for k, v in inputs.items()}
    arrays, packs, offsets = {"x": np.ascontiguousarray(w["x"])}, {}, {}
    x = nc.dram_tensor("x", arrays["x"].shape, F32, kind="ExternalInput").ap()
    for name, lay_out in PACKS:
        p = lay_out(w)
        a = arrays["pack_dram_" + name] = p.array()
        packs[name] = nc.dram_tensor("pack_dram_" + name, a.shape, F32, kind="ExternalInput").ap()
        offsets[name] = p.at
    out = nc.dram_tensor("out", arrays["x"].shape, F32, kind="ExternalOutput").ap()
    build(nc, x, packs, offsets, out)
    return run_bass_kernel_spmd(nc, [arrays], core_ids=[0]).results[0]["out"]
```

```python
from contextlib import ExitStack

import numpy as np
import concourse.bass as bass
from concourse import mybir

F32 = mybir.dt.float32
I32 = mybir.dt.int32
ALU = mybir.AluOpType
ACT = mybir.ActivationFunctionType
AX = mybir.AxisListType

P = 128
NB = 2
PIX = 1024
T = NB * PIX
CH = 512
NCH = T // CH
BN_SCALE = float(1.0 / np.sqrt(np.float32(1.0 + 1e-5)))


class Stage:

    def __init__(self, nc, ctx):
        self.nc, self.ctx, self.sems = nc, ctx, {}
        ctx.callback(self.clear)

    def sb(self, name, shape, dt=F32):
        return self.ctx.enter_context(self.nc.sbuf_tensor(name, shape, dt))

    def sem(self, name):
        if name not in self.sems:
            self.sems[name] = self.nc.alloc_semaphore(name)
        return self.sems[name]

    def clear(self):
        with self.nc.Block() as block:
            @block.gpsimd
            def _(pool):
                for s in self.sems.values():
                    pool.sem_clear(s)
        for s in self.sems.values():
            self.nc.release_semaphore(s)


class Chain:

    def __init__(self, eng, sem):
        self.eng, self.sem, self.n = eng, sem, 0

    def __call__(self, ins):
        ins.then_inc(self.sem, 1)
        self.n += 1
        self.eng.wait_ge(self.sem, self.n)


def bc(ap, axis, n):
    shape = list(ap.shape)
    ap = ap.unsqueeze(axis)
    shape.insert(axis, n)
    return ap.broadcast_to(shape)


class Pack:
    def __init__(self):
        self.parts, self.at, self.n = [], {}, 0

    def add(self, name, a):
        a = a.reshape(a.shape[0], -1)
        full = np.zeros((P, a.shape[1]), np.float32)
        full[: a.shape[0]] = a
        self.at[name] = (self.n, a.shape[0], a.shape[1])
        self.parts.append(full)
        self.n += a.shape[1]

    def array(self):
        return np.ascontiguousarray(np.concatenate(self.parts, axis=1))


class Weights:

    def __init__(self, tile, at):
        self.tile, self.at = tile, at

    def __getitem__(self, name):
        c, rows, n = self.at[name]
        return self.tile[0:rows, c:c + n]


HEADS = 8
DH = 16
HW = 32
HK = 8
KEYS = HK * HK
TAPS = 36
PADW = HW + 2
HID = 32
PAIRS = HEADS // 2
BATCHES = 8
HALF = PIX // 2
GCOLS = NB * HEADS * KEYS


def block_diag(w):
    g, o, i = w.shape
    full = np.zeros((g * i, g * o), w.dtype)
    for n in range(g):
        full[n * i:(n + 1) * i, n * o:(n + 1) * o] = w[n].T
    return full


def l0_pack(w):
    p = Pack()
    L = lambda n: w["L0_conv_" + n]
    for n in ("bn1_g", "bn1_b", "out_b"):
        p.add(n, L(n).reshape(P, 1))
    p.add("off_dw_b", np.tile(L("off_dw_b"), HEADS).reshape(P, 1))
    p.add("off_dw_w", np.tile(L("off_dw_w").reshape(DH, TAPS), (HEADS, 1)))
    p.add("qw", block_diag(L("qw")))
    p.add("kw", block_diag(L("kw")))
    p.add("vw", block_diag(L("vw")))
    p.add("off_pw", np.repeat(np.tile(L("off_pw_w").T, (HEADS, 1))[:, :, None], P, axis=2))
    p.add("out_w", L("out_w").T)
    w1 = np.zeros((2, NB, HEADS, 4, HEADS, 4, HID), np.float32)
    for c in range(2):
        for g in range(HEADS):
            for t in range(4):
                w1[c, :, g, t, g, t] = L("cpb_w1")[c]
    p.add("cpb_w1", w1.reshape(P, HEADS * P))
    p.add("cpb_w2", block_diag(np.tile(L("cpb_w2").T[None], (4, 1, 1))))
    w3 = np.zeros((4, HID, BATCHES, HID), np.float32)
    for j in range(4):
        for n in range(BATCHES):
            w3[j, :, n, 4 * n + j] = L("cpb_w3")[:, 0]
    p.add("cpb_w3", w3.reshape(P, BATCHES * HID))
    p.add("cpb_b1", np.tile(L("cpb_b1"), 4).reshape(P, 1))
    p.add("cpb_b2", np.tile(L("cpb_b2"), 4).reshape(P, 1))
    p.add("cpb_b3", np.tile(L("cpb_b3"), P).reshape(P, 1))
    p.add("ident", np.eye(P, dtype=np.float32))
    p.add("quarter", np.repeat(np.eye(4, dtype=np.float32), 32, axis=0))
    p.add("gmask", np.repeat(np.eye(HEADS, dtype=np.float32), DH, axis=0))
    ar = np.arange(KEYS)
    p.add("kgrid", np.tile(np.stack([ar % HK, ar // HK]).astype(np.float32).reshape(1, 2 * KEYS), (P, 1)))
    cq = (np.float32(2.0) * np.arange(HW, dtype=np.float32) / np.float32(HW - 1) - np.float32(1.0)).astype(np.float32)
    p.add("qgrid", np.tile(cq.reshape(1, HW), (P, 1)))
    rows = np.arange(P)
    p.add("minus_x", -(rows % HW + 0.5).astype(np.float32).reshape(P, 1))
    p.add("minus_y", np.stack([-(4 * c + rows // HW + 0.5) for c in range(8)], axis=1).astype(np.float32))
    return p


def mlp_pack(w):
    p = Pack()
    L = lambda n: w["L0_conv_" + n]
    for n in ("bn2_g", "bn2_b", "mlp_b2"):
        p.add(n, L(n).reshape(P, 1))
    p.add("mlp_w1", L("mlp_w1").T)
    p.add("mlp_b1", L("mlp_b1").reshape(4, P).T)
    p.add("mlp_w2", L("mlp_w2").T.reshape(4, P, P).transpose(1, 0, 2))
    return p


def l0_prepare(nc, X, PS, W, loaded, KM, VT, Q, A, B, x_in):
    with ExitStack() as ctx:
        st = Stage(nc, ctx)
        sb, sem = st.sb, st.sem
        s1 = sb("l0_s1", [P, 1])
        XN = sb("l0_xn", [P, T])
        qpad = sb("l0_qpad", [P, NB, PADW, PADW])
        conv = sb("l0_conv", [P, NB, HK, HK])
        off = sb("l0_off", [P, NB, KEYS])
        offm = sb("l0_offm", [P, NB, HEADS, KEYS])
        V = sb("l0_v", [P, 2, NB * HEADS, KEYS])
        PX = sb("l0_px", [P, 2, GCOLS])
        hx = sb("l0_hx", [P, GCOLS])
        hy = sb("l0_hy", [P, 2, GCOLS])
        wt = sb("l0_wt", [P, 2, GCOLS])
        XT = sb("l0_xt", [P, NB * 8, P])
        kvm = offm
        kv = sb("l0_kv", [P, NB, KEYS])
        vm = hx[:].rearrange("p (b g k) -> p b g k", b=NB, g=HEADS)
        sel = wt[:].rearrange("p c (g k t) -> p (c g) k t", t=4, k=16)
        own = sb("l0_own", [P, 16])
        pos = sb("l0_pos", [P, 16, HW])
        mag = sb("l0_mag", [P, 16 * HW])
        sgn = sb("l0_sgn", [P, 16 * HW])
        F = XN[:].rearrange("p (r n) -> p r n", n=HALF)
        inner = lambda b, y0, n: qpad[:, b, 1 + y0:1 + y0 + n, 1:1 + HW]

        block = ctx.enter_context(nc.Block())

        @block.gpsimd
        def _(pool):
            pool.memset(qpad[:], 0.0).then_inc(sem("border"), 1)

        @block.vector
        def _(dve):
            link = Chain(dve, sem("dve_chain"))
            dve.wait_ge(loaded, 16)
            link(dve.tensor_scalar(s1[:], W["bn1_g"], BN_SCALE, None, ALU.mult))
            for b in range(NB):
                c = slice(b * PIX, (b + 1) * PIX)
                dve.wait_ge(x_in[b], 16)
                dve.tensor_scalar(XN[:, c], X[:, c], s1[:, 0:1], W["bn1_b"], ALU.mult, ALU.add).then_inc(sem("xn"), 1)
            dve.wait_ge(sem("q_out"), NCH)
            for t in range(TAPS):
                ky, kx = divmod(t, 6)
                src = qpad[:, :, ky:ky + 29:4, kx:kx + 29:4]
                for b in range(NB):
                    if t == 0:
                        ins = dve.tensor_scalar(conv[:, b], src[:, b], W["off_dw_w"][:, 0:1], None, ALU.mult)
                    else:
                        ins = dve.scalar_tensor_tensor(conv[:, b], src[:, b], W["off_dw_w"][:, t:t + 1], conv[:, b],
                                                       ALU.mult, ALU.add)
                    if b == 0:
                        ins.then_inc(sem("tap0"), 1)
                link(ins)
                dve.wait_ge(sem("tap0"), t + 1)
            dve.sem_inc(sem("conv"), 1)
            dve.wait_ge(sem("off"), 1)
            link(dve.tensor_tensor(offm[:], bc(off[:], 2, HEADS), bc(bc(W["gmask"], 1, NB), 3, KEYS), ALU.mult))
            dve.sem_inc(sem("offm"), 1)
            dve.wait_ge(sem("tanh"), 1)
            for c in range(2):
                grid = bc(W["kgrid"][:, c * KEYS:(c + 1) * KEYS], 1, NB * HEADS)
                link(dve.scalar_tensor_tensor(V[:, c], V[:, c], 4.0, grid, ALU.mult, ALU.add))
            link(dve.tensor_scalar(V[:], V[:], 2.0 / 7.0, -1.0, ALU.mult, ALU.add))
            link(dve.tensor_scalar(PX[:], V[:].rearrange("p c g k -> p c (g k)"), 1.0, HW / 2.0, ALU.add, ALU.mult))
            dve.sem_inc(sem("pixels"), 1)
            link(dve.tensor_tensor(sel, V[:].rearrange("p c g (k t) -> p (c g) k t", t=4),
                                   bc(W["ident"].rearrange("p (g t) -> p g t", t=4), 2, 16), ALU.mult))
            link(dve.tensor_reduce(own[:], sel.rearrange("p g k t -> p k g t"), AX.XY, ALU.add))
            link(dve.tensor_tensor(pos[:], bc(W["qgrid"], 1, 16), bc(own[:], 2, HW), ALU.subtract))
            dve.sem_inc(sem("pos"), 1)

            def weights(c):
                dve.wait_ge(sem("hy"), c + 1)
                if c >= 2:
                    dve.wait_ge(sem("sampled"), c - 1)
                dve.tensor_tensor(wt[:, c % 2], hx[:], hy[:, c % 2], ALU.mult).then_inc(sem("wt"), 1)

            def b_out(n):
                dve.wait_ge(sem("ab"), n + 1)
                dve.tensor_copy(B[:, n // 2, (n % 2) * 16:(n % 2) * 16 + 16].rearrange("p u q -> p (u q)"),
                                PS[:, 2 * (n % 2) + 1]).then_inc(sem("b_out"), 1)

            dve.wait_ge(sem("hx"), 1)
            weights(0)
            weights(1)
            dve.wait_ge(sem("logs"), 1)
            for b in range(NB):
                for c in range(2):
                    q = NB * c + b
                    dve.scalar_tensor_tensor(F[:, q], sgn[:], W["quarter"][:, q:q + 1], mag[:], ALU.mult,
                                             ALU.mult).then_inc(sem("f"), 1)
            for c in range(8):
                b_out(c)
                if c + 2 < 8:
                    weights(c + 2)
            dve.wait_ge(sem("sampled"), 8)
            for b in range(NB):
                dve.tensor_tensor(kvm[:, b], PS[:, 4 + b].rearrange("p (g k) -> p g k", g=HEADS),
                                  bc(W["gmask"], 2, KEYS), ALU.mult).then_inc(sem("kvm"), 1)
            dve.wait_ge(sem("kvm"), NB)
            link(dve.tensor_reduce(kv[:], kvm[:].rearrange("p b g k -> p b k g"), AX.X, ALU.add))
            dve.sem_inc(sem("kv"), 1)
            b_out(8)
            b_out(9)
            dve.wait_ge(sem("k"), 1)
            for b in range(NB):
                m = bc(W["gmask"], 2, KEYS)
                dve.tensor_tensor(vm[:, b], bc(PS[:, 7, b * KEYS:(b + 1) * KEYS], 1, HEADS), m,
                                  ALU.mult).then_inc(sem("vm"), 1)
                dve.scalar_tensor_tensor(KM[:, b], bc(PS[:, 6, b * KEYS:(b + 1) * KEYS], 1, HEADS), DH ** -0.5, m,
                                         ALU.mult, ALU.mult).then_inc(sem("km"), 1)
            for n in range(10, NB * HEADS):
                b_out(n)

        @block.scalar
        def _(act):
            for n in range(NCH):
                act.wait_ge(sem("q"), n + 1)
                if n == 0:
                    act.wait_ge(sem("border"), 1)
                act.activation(inner(n // 2, 16 * (n % 2), 16), PS[:, n].rearrange("p (y x) -> p y x", x=HW),
                               ACT.Copy).then_inc(sem("q_out"), 1)
            for n in range(NCH):
                act.activation(Q[:, n * CH:(n + 1) * CH], PS[:, n], ACT.Copy).then_inc(sem("q_flat"), 1)
            for n in range(4):
                act.wait_ge(sem("xt"), n + 1)
                act.activation(XT[:, 4 * n:4 * n + 4].rearrange("p c k -> p (c k)"), PS[:, n],
                               ACT.Copy).then_inc(sem("xt_out"), 1)
            act.wait_ge(sem("conv"), 1)
            act.activation(off[:].rearrange("p b k -> p (b k)"), conv[:].rearrange("p b y x -> p (b y x)"), ACT.Gelu,
                           bias=W["off_dw_b"]).then_inc(sem("off"), 1)
            act.wait_ge(sem("shift"), 1)
            act.activation(V[:].rearrange("p c g k -> p (c g k)"), PS[:, 4:8].rearrange("p a n -> p (a n)"),
                           ACT.Tanh).then_inc(sem("tanh"), 1)
            act.wait_ge(sem("pixels"), 1)
            act.activation(hy[:, 0], PX[:, 0], ACT.Abs, bias=W["minus_x"]).then_inc(sem("ax"), 1)
            act.wait_ge(sem("ax"), 1)
            act.activation(hx[:], hy[:, 0], ACT.Relu, bias=1.0, scale=-1.0).then_inc(sem("hx"), 1)
            act.wait_ge(sem("hx"), 1)

            def hat(c):
                if c >= 2:
                    act.wait_ge(sem("wt"), c - 1)
                act.activation(hy[:, c % 2], PX[:, 1], ACT.Abs, bias=W["minus_y"][:, c:c + 1]).then_inc(sem("ay"), 1)
                act.wait_ge(sem("ay"), c + 1)
                act.activation(hy[:, c % 2], hy[:, c % 2], ACT.Relu, bias=1.0, scale=-1.0).then_inc(sem("hy"), 1)

            def a_out(n):
                act.wait_ge(sem("ab"), n + 1)
                act.activation(A[:, n // 2, (n % 2) * 16:(n % 2) * 16 + 16].rearrange("p u q -> p (u q)"),
                               PS[:, 2 * (n % 2)], ACT.Identity, bias=W["cpb_b1"]).then_inc(sem("a_out"), 1)

            hat(0)
            hat(1)
            act.wait_ge(sem("pos"), 1)
            flat = pos[:].rearrange("p k q -> p (k q)")
            act.activation(mag[:], flat, ACT.Abs).then_inc(sem("mag"), 1)
            act.activation(sgn[:], flat, ACT.Sign).then_inc(sem("sgn"), 1)
            act.wait_ge(sem("mag"), 1)
            act.wait_ge(sem("sgn"), 1)
            act.activation(mag[:], mag[:], ACT.Ln, bias=1.0).then_inc(sem("logs"), 1)
            for c in range(8):
                if c + 2 < 8:
                    hat(c + 2)
                a_out(c)
            for n in range(8, 12):
                a_out(n)
            for n in range(2):
                act.wait_ge(sem("vt"), n + 1)
                act.activation(VT[:, 4 * n:4 * n + 4].rearrange("p c k -> p (c k)"), PS[:, 4 + n],
                               ACT.Copy).then_inc(sem("vt_out"), 1)
            for n in range(12, NB * HEADS):
                a_out(n)

        @block.tensor
        def _(pe):
            for n in range(NCH):
                pe.wait_ge(sem("xn"), n // 2 + 1)
                pe.matmul(PS[:, n], W["qw"], XN[:, n * CH:(n + 1) * CH], start=True, stop=True).then_inc(sem("q"), 1)
            for n in range(16):
                if n % 4 == 0:
                    pe.wait_ge(sem("q_flat"), n // 4 + 1)
                ins = pe.transpose(PS[:, n // 4, (n % 4) * P:(n % 4 + 1) * P], XN[:, n * P:(n + 1) * P], W["ident"])
                if n % 4 == 3:
                    ins.then_inc(sem("xt"), 1)
            pe.wait_ge(sem("offm"), 1)
            for c in range(2):
                for b in range(NB):
                    ins = pe.matmul(PS[:, 4 + 2 * c + b], W["off_pw"][:, c * P:(c + 1) * P],
                                    offm[:, b].rearrange("p g k -> p (g k)"), start=True, stop=True)
            ins.then_inc(sem("shift"), 1)
            pe.wait_ge(sem("xt_out"), 4)
            pe.wait_ge(sem("tanh"), 1)

            def sample(c):
                pe.wait_ge(sem("wt"), c + 1)
                for b in range(NB):
                    ins = pe.matmul(PS[:, 4 + b], XT[:, b * 8 + c], wt[:, c % 2, b * CH:(b + 1) * CH],
                                    start=(c == 0), stop=(c == 7))
                ins.then_inc(sem("sampled"), 1)

            def layer1(n):
                b, g = divmod(n, HEADS)
                if n >= 2:
                    pe.wait_ge(sem("a_out"), n - 1)
                    pe.wait_ge(sem("b_out"), n - 1)
                for c in range(2):
                    if g == 0:
                        pe.wait_ge(sem("f"), NB * b + c + 1)
                    ins = pe.matmul(PS[:, 2 * (n % 2) + c], W["cpb_w1"][:, g * P:(g + 1) * P], F[:, NB * c + b],
                                    start=True, stop=True)
                ins.then_inc(sem("ab"), 1)

            for c in range(8):
                sample(c)
                layer1(c)
            layer1(8)
            layer1(9)
            pe.wait_ge(sem("kv"), 1)
            kflat = kv[:].rearrange("p b k -> p (b k)")
            pe.matmul(PS[:, 6, 0:NB * KEYS], W["kw"], kflat, start=True, stop=True)
            pe.matmul(PS[:, 7, 0:NB * KEYS], W["vw"], kflat, start=True, stop=True).then_inc(sem("k"), 1)
            layer1(10)
            layer1(11)
            pe.wait_ge(sem("vm"), NB)
            for n in range(NB * PAIRS):
                ins = pe.transpose(PS[:, 4 + n // 4, (n % 4) * P:(n % 4 + 1) * P],
                                   vm[:, n // 4, 2 * (n % 4):2 * (n % 4) + 2].rearrange("p g k -> p (g k)"), W["ident"])
                if n % 4 == 3:
                    ins.then_inc(sem("vt"), 1)
            for n in range(12, NB * HEADS):
                layer1(n)


def reg_wait(eng, sem, value, passed):
    eng.wait_ge(sem, value)
    eng.sem_inc(passed, 1)


def l0_scores(nc, PS, W, KM, Q, A, B, SALL):
    with ExitStack() as ctx:
        st = Stage(nc, ctx)
        sb, sem = st.sb, st.sem
        kcur = sb("sc_k", [P, P])
        H1 = sb("sc_h1", [P, 2, 4, HALF])
        H2 = sb("sc_h2", [P, 8, HALF])
        NBT = 2 * BATCHES
        STEPS = NB * PAIRS
        Z2, H1N, QK, TILE, BIASED = 8, 4, 1, 2, 2
        block = ctx.enter_context(nc.Block())

        @block.gpsimd
        def _(pool):
            with pool.Fori(0, STEPS) as n:
                reg_wait(pool, sem("qk"), n + 1, sem("pool_passed"))
                pool.tensor_copy(kcur[:].rearrange("p (g k) -> p g k", g=2),
                                 KM[:].rearrange("p b (q g) k -> p (b q) g k", g=2)[:, bass.ds(n, 1)].squeeze(1)
                                 ).then_inc(sem("kcur"), 1)
                for m in range(NBT):
                    half, bt = divmod(m, BATCHES)
                    reg_wait(pool, sem("z2"), (n * NBT + m) * 4 + Z2 - 4, sem("pool_passed"))
                    a = A[:, bass.ds(n, 1), bt:32:BATCHES, :].squeeze(1)
                    b = B[:, bass.ds(n, 1), bt:32:BATCHES, 16 * half:16 * half + 16].squeeze(1)
                    pool.tensor_tensor(H1[:, m % 2].rearrange("p u (y x) -> p u y x", x=HW), bc(a, 2, 16),
                                       bc(b, 3, HW), ALU.add).then_inc(sem("z1"), 1)

        @block.vector
        def _(dve):
            with dve.Fori(0, STEPS) as n:
                for m in range(NBT):
                    dve.wait_ge(sem("z1"), n * NBT + m + 1)
                    h = H1[:, m % 2].rearrange("p u q -> p (u q)")
                    dve.tensor_scalar(h, h, 0.0, None, ALU.max).then_inc(sem("h1"), 1)

        @block.tensor
        def _(pe):
            pe.sem_inc(sem("qk"), QK)
            pe.sem_inc(sem("z2"), Z2)
            pe.sem_inc(sem("biased"), BIASED)

            def scores(n, half):
                pe.wait_ge(sem("tile_out"), n * 2 + half + 1)
                ins = pe.matmul(PS[:, half], kcur[:], Q[:, bass.ds((n // PAIRS) * PIX + half * HALF, HALF)],
                                start=True, stop=False, skip_group_check=True)
                if half:
                    ins.then_inc(sem("qk"), 1)

            def layer2(n, m):
                pe.wait_ge(sem("h1"), n * NBT + m + 1)
                for i in range(4):
                    pe.wait_ge(sem("h2"), (n * NBT + m) * 4 + i + 1)
                    pe.matmul(PS[:, 2 + i], W["cpb_w2"], H1[:, m % 2, i], start=True, stop=True).then_inc(sem("z2"), 1)

            def layer3(n, m):
                half, bt = divmod(m, BATCHES)
                pe.wait_ge(sem("h2"), (n * NBT + m) * 4 + 4 + H1N)
                for i in range(4):
                    ins = pe.matmul(PS[32 * i:32 * i + 32, half], W["cpb_w3"][:, bt * HID:(bt + 1) * HID],
                                    H2[:, 4 * (m % 2) + i], start=False, stop=(bt == BATCHES - 1),
                                    tile_position=(0, 32 * i), skip_group_check=True)
                ins.then_inc(sem("biased"), 1)

            with pe.Fori(0, STEPS) as n:
                pe.wait_ge(sem("kcur"), n + 1)
                scores(n, 0)
                for m in range(NBT):
                    layer2(n, m)
                    if m:
                        layer3(n, m - 1)
                    if m == BATCHES - 1:
                        scores(n, 1)
                layer3(n, NBT - 1)

        @block.scalar
        def _(act):
            act.sem_inc(sem("h2"), H1N)
            act.sem_inc(sem("tile_out"), TILE)

            def tile_out(n, half):
                reg_wait(act, sem("biased"), n * NBT + (half + 1) * BATCHES + BIASED, sem("act_passed"))
                act.activation(SALL[:, bass.ds(n * 2 + half, 1)].squeeze(1), PS[:, half], ACT.Identity,
                               bias=W["cpb_b3"]).then_inc(sem("tile_out"), 1)

            with act.Fori(0, STEPS) as n:
                for m in range(NBT):
                    for i in range(4):
                        act.wait_ge(sem("z2"), (n * NBT + m) * 4 + i + 1 + Z2)
                        if i == 0:
                            act.wait_ge(sem("biased"), n * NBT + m - 1 + BIASED)
                        act.activation(H2[:, 4 * (m % 2) + i], PS[:, 2 + i], ACT.Relu,
                                       bias=W["cpb_b2"]).then_inc(sem("h2"), 1)
                    if m == BATCHES + 1:
                        tile_out(n, 0)
                tile_out(n, 1)


def l0_attend(nc, X, PS, W, SALL, VT):
    with ExitStack() as ctx:
        st = Stage(nc, ctx)
        sb, sem = st.sb, st.sem
        mx = sb("at_max", [P, 8])
        E = sb("at_e", [P, 3, 8, KEYS])
        den = sb("at_den", [P, 2, 8])
        rden = sb("at_rden", [P, 2, 8])
        PT = sb("at_pt", [P, 2, HALF])
        ATT = sb("at_att", [P, T])
        TILES = NB * PAIRS * 2
        block = ctx.enter_context(nc.Block())

        @block.tensor
        def _(pe):
            def turn(s):
                if s >= 2:
                    pe.wait_ge(sem("shifted"), s - 1)
                for t in range(4):
                    ins = pe.transpose(PS[:, s % 2, t * P:(t + 1) * P], SALL[:, s, t * P:(t + 1) * P], W["ident"])
                ins.then_inc(sem("turned"), 1)

            def back(s):
                pe.wait_ge(sem("probs"), s + 1)
                if s >= 2:
                    pe.wait_ge(sem("pt"), s - 1)
                for t in range(4):
                    ins = pe.transpose(PS[:, 2 + s % 2, t * P:(t + 1) * P],
                                       E[:, s % 3, 2 * t:2 * t + 2].rearrange("p g k -> p (g k)"), W["ident"])
                ins.then_inc(sem("back"), 1)

            def values(s):
                b, pair, half = s // 8, s // 2 % 4, s % 2
                pe.wait_ge(sem("pt"), s + 1)
                pe.matmul(PS[:, 4 + 2 * b + half], VT[:, b * PAIRS + pair], PT[:, s % 2], start=(pair == 0),
                          stop=(pair == PAIRS - 1)).then_inc(sem("valued"), 1)

            turn(0)
            for s in range(TILES + 2):
                if s + 1 < TILES:
                    turn(s + 1)
                if 1 <= s <= TILES:
                    back(s - 1)
                if s >= 2:
                    values(s - 2)
            for n in range(NCH):
                pe.wait_ge(sem("att"), n + 1)
                pe.matmul(PS[:, n], W["out_w"], ATT[:, n * CH:(n + 1) * CH], start=True,
                          stop=True).then_inc(sem("proj"), 1)

        @block.vector
        def _(dve):
            link = Chain(dve, sem("dve_chain"))

            def shift(s):
                dve.wait_ge(sem("turned"), s + 1)
                t = PS[:, s % 2].rearrange("p (g k) -> p g k", k=KEYS)
                link(dve.tensor_reduce(mx[:], t, AX.X, ALU.max))
                if s >= 3:
                    dve.wait_ge(sem("back"), s - 2)
                dve.tensor_tensor(E[:, s % 3], t, bc(mx[:], 2, KEYS), ALU.subtract).then_inc(sem("shifted"), 1)
                dve.wait_ge(sem("shifted"), s + 1)

            def norm(s):
                dve.wait_ge(sem("exp"), s + 1)
                link(dve.tensor_reduce(den[:, s % 2], E[:, s % 3], AX.X, ALU.add))
                if s >= 2:
                    dve.wait_ge(sem("probs"), s - 1)
                dve.reciprocal(rden[:, s % 2], den[:, s % 2]).then_inc(sem("inverse"), 1)

            for s in range(TILES + 1):
                if s < TILES:
                    shift(s)
                if s >= 1:
                    norm(s - 1)
            for n in range(NCH):
                dve.wait_ge(sem("proj"), n + 1)
                x = X[:, n * CH:(n + 1) * CH]
                dve.scalar_tensor_tensor(x, PS[:, n], W["out_b"], x, ALU.add, ALU.add)

        @block.gpsimd
        def _(pool):
            for s in range(TILES):
                pool.wait_ge(sem("inverse"), s + 1)
                pool.tensor_tensor(E[:, s % 3], E[:, s % 3], bc(rden[:, s % 2], 2, KEYS), ALU.mult
                                   ).then_inc(sem("probs"), 1)

        @block.scalar
        def _(act):
            for s in range(TILES + 1):
                if s < TILES:
                    act.wait_ge(sem("shifted"), s + 1)
                    e = E[:, s % 3].rearrange("p g k -> p (g k)")
                    act.activation(e, e, ACT.Exp).then_inc(sem("exp"), 1)
                if s >= 1:
                    act.wait_ge(sem("back"), s)
                    if s >= 3:
                        act.wait_ge(sem("valued"), s - 2)
                    act.activation(PT[:, (s - 1) % 2], PS[:, 2 + (s - 1) % 2], ACT.Copy).then_inc(sem("pt"), 1)
            for n in range(NCH):
                act.wait_ge(sem("valued"), 16 if n >= 2 else 8)
                act.activation(ATT[:, n * CH:(n + 1) * CH], PS[:, 4 + n], ACT.Copy).then_inc(sem("att"), 1)


def l0_mlp(nc, X, PS, W):
    with ExitStack() as ctx:
        st = Stage(nc, ctx)
        sb, sem = st.sb, st.sem
        s2 = sb("ml_s2", [P, 1])
        XN = sb("ml_xn", [P, T])
        H = sb("ml_h", [P, 2, 4, CH])
        block = ctx.enter_context(nc.Block())

        @block.vector
        def _(dve):
            link = Chain(dve, sem("dve_chain"))
            link(dve.tensor_scalar(s2[:], W["bn2_g"], BN_SCALE, None, ALU.mult))
            for n in range(NCH):
                c = slice(n * CH, (n + 1) * CH)
                dve.tensor_scalar(XN[:, c], X[:, c], s2[:, 0:1], W["bn2_b"], ALU.mult, ALU.add).then_inc(sem("xn"), 1)
            for n in range(NCH):
                dve.wait_ge(sem("down"), n + 1)
                x = X[:, n * CH:(n + 1) * CH]
                dve.scalar_tensor_tensor(x, PS[:, 6 + n % 2], W["mlp_b2"], x, ALU.add, ALU.add).then_inc(sem("added"), 1)

        @block.tensor
        def _(pe):
            def up(n):
                pe.wait_ge(sem("xn"), n + 1)
                for k in range(4):
                    g = 4 * n + k
                    if g >= 6:
                        pe.wait_ge(sem("gelu"), g - 5)
                    pe.matmul(PS[:, g % 6], W["mlp_w1"][:, k * P:(k + 1) * P], XN[:, n * CH:(n + 1) * CH], start=True,
                              stop=True).then_inc(sem("up"), 1)

            def down(n):
                pe.wait_ge(sem("gelu"), 4 * n + 4)
                if n >= 2:
                    pe.wait_ge(sem("added"), n - 1)
                for k in range(4):
                    ins = pe.matmul(PS[:, 6 + n % 2], W["mlp_w2"][:, k * P:(k + 1) * P], H[:, n % 2, k],
                                    start=(k == 0), stop=(k == 3))
                ins.then_inc(sem("down"), 1)

            for n in range(NCH + 1):
                if n < NCH:
                    up(n)
                if n >= 1:
                    down(n - 1)

        @block.scalar
        def _(act):
            for g in range(4 * NCH):
                n, k = divmod(g, 4)
                act.wait_ge(sem("up"), g + 1)
                if n >= 2:
                    act.wait_ge(sem("down"), n - 1)
                act.activation(H[:, n % 2, k], PS[:, g % 6], ACT.Gelu, bias=W["mlp_b1"][:, k:k + 1]
                               ).then_inc(sem("gelu"), 1)


ITILES = PIX // P


def l1_pack(w):
    p = Pack()
    L = lambda n: w["L1_conv_" + n]
    for n in ("gn_w", "gn_b", "bq", "bk", "bv", "bo"):
        p.add(n, L(n).reshape(P, 1))
    for n in ("wq", "wk", "wv", "wo"):
        p.add(n, L(n).T)
    p.add("ident", np.eye(P, dtype=np.float32))
    p.add("group", np.kron(np.eye(32), np.full((4, 4), 0.25)).astype(np.float32))
    return p


def l1_attention(nc, X, PS, W):
    with ExitStack() as ctx:
        st = Stage(nc, ctx)
        sb, sem = st.sb, st.sem
        stats = sb("gn_stats", [P, NB, 2, 6])
        mv = sb("gn_mv", [P, NB, 2])
        mom = sb("gn_mom", [P, 2, NB])
        mu = sb("gn_mu", [P, NB])
        dev = sb("gn_dev", [P, NB])
        rstd = sb("gn_rstd", [P, NB])
        gain = sb("gn_gain", [P, NB])
        shift = sb("gn_shift", [P, NB])
        HF = sb("a1_hf", [P, T])
        Qm = sb("a1_q", [P, T])
        Km = sb("a1_k", [P, T])
        Vt = sb("a1_vt", [P, NB * ITILES, P])
        mx = sb("a1_max", [P, 2])
        nmx = sb("a1_nmax", [P, 2])
        den = sb("a1_den", [P, NB * ITILES])
        rden = sb("a1_rden", [P, NB * ITILES])
        E = sb("a1_e", [P, 2, PIX])
        PT = sb("a1_pt", [P, 2, ITILES, P])
        O = HF[:].rearrange("p (t c) -> p t c", c=P)
        AO = sb("a1_ao", [P, T])
        SCALE = float(P) ** -0.5
        TILES = NB * ITILES
        block = ctx.enter_context(nc.Block())

        @block.vector
        def _(dve):
            link = Chain(dve, sem("dve_chain"))
            for b in range(NB):
                for h in range(2):
                    c = (b * 2 + h) * CH
                    ins = dve.bn_stats(stats[:, b, h], X[:, c:c + CH])
            link(ins)
            for b in range(NB):
                link(dve.bn_aggr(mv[:, b], stats[:, b]))
            dve.tensor_copy(mom[:, 0], mv[:, :, 0]).then_inc(sem("means"), 1)
            dve.wait_ge(sem("group_mean"), 1)
            link(dve.tensor_copy(mu[:], PS[:, 0, 0:NB]))
            link(dve.tensor_tensor(dev[:], mv[:, :, 0], mu[:], ALU.subtract))
            link(dve.tensor_tensor(dev[:], dev[:], dev[:], ALU.mult))
            dve.tensor_tensor(mom[:, 1], dev[:], mv[:, :, 1], ALU.add).then_inc(sem("vars"), 1)
            dve.wait_ge(sem("group_var"), 1)
            link(dve.tensor_scalar(rstd[:], PS[:, 1, 0:NB], 1e-6, None, ALU.add))
            link(dve.reciprocal(rstd[:], rstd[:]))
            dve.sem_inc(sem("inverse"), 1)
            dve.wait_ge(sem("root"), 1)
            link(dve.tensor_scalar(gain[:], rstd[:], W["gn_w"], None, ALU.mult))
            link(dve.tensor_tensor(shift[:], mu[:], gain[:], ALU.mult))
            link(dve.tensor_scalar(shift[:], shift[:], -1.0, W["gn_b"], ALU.mult, ALU.add))
            for b in range(NB):
                c = slice(b * PIX, (b + 1) * PIX)
                dve.tensor_scalar(HF[:, c], X[:, c], gain[:, b:b + 1], shift[:, b:b + 1], ALU.mult,
                                  ALU.add).then_inc(sem("hf"), 1)
            for n in range(NCH):
                dve.wait_ge(sem("k"), n + 1)
                dve.tensor_scalar(Km[:, n * CH:(n + 1) * CH], PS[:, 4 + n], W["bk"], None,
                                  ALU.add).then_inc(sem("k_out"), 1)

            def top(s):
                dve.wait_ge(sem("scores"), s + 1)
                if s >= 2:
                    dve.wait_ge(sem("exp"), s - 1)
                v = PS[:, 2 * (s % 2):2 * (s % 2) + 2].rearrange("p a n -> p (a n)")
                link(dve.tensor_reduce(mx[:, s % 2:s % 2 + 1], v, AX.X, ALU.max))
                dve.tensor_scalar(nmx[:, s % 2:s % 2 + 1], mx[:, s % 2:s % 2 + 1], -SCALE, None,
                                  ALU.mult).then_inc(sem("top"), 1)

            def back_out(s):
                dve.wait_ge(sem("back"), 2 * s + 2)
                if s >= 2:
                    dve.wait_ge(sem("valued"), s - 1)
                dve.tensor_copy(PT[:, s % 2, 4:8].rearrange("p j i -> p (j i)"), PS[:, 5]).then_inc(sem("pt_dve"), 1)

            def output(s):
                dve.wait_ge(sem("exp"), s + 1)
                link(dve.reciprocal(rden[:, s:s + 1], den[:, s:s + 1]))
                dve.wait_ge(sem("valued"), s + 1)
                dve.tensor_scalar(O[:, s], PS[:, 6 + s % 2, 0:P], rden[:, s:s + 1], None, ALU.mult).then_inc(sem("o"), 1)

            for s in range(TILES + 3):
                if 2 <= s < TILES + 2:
                    back_out(s - 2)
                if s < TILES:
                    top(s)
                if s >= 3:
                    output(s - 3)
            for n in range(NCH):
                dve.wait_ge(sem("proj"), n + 1)
                x = X[:, n * CH:(n + 1) * CH]
                dve.scalar_tensor_tensor(x, PS[:, 4 + n], W["bo"], x, ALU.add, ALU.add)

        @block.scalar
        def _(act):
            act.wait_ge(sem("inverse"), 1)
            act.activation(rstd[:], rstd[:], ACT.Sqrt).then_inc(sem("root"), 1)
            for n in range(NCH):
                act.wait_ge(sem("q"), n + 1)
                act.activation(Qm[:, n * CH:(n + 1) * CH], PS[:, n], ACT.Identity, bias=W["bq"]).then_inc(sem("q_out"), 1)
            for n in range(4):
                act.wait_ge(sem("vt"), n + 1)
                act.activation(Vt[:, 4 * n:4 * n + 4].rearrange("p c k -> p (c k)"), PS[:, n],
                               ACT.Copy).then_inc(sem("vt_out"), 1)

            def exp(s):
                act.wait_ge(sem("top"), s + 1)
                if s >= 2:
                    act.wait_ge(sem("back"), 2 * (s - 2) + 2)
                v = PS[:, 2 * (s % 2):2 * (s % 2) + 2].rearrange("p a n -> p (a n)")
                act.activation(E[:, s % 2], v, ACT.Exp, bias=nmx[:, s % 2:s % 2 + 1], scale=SCALE,
                               accum_out=den[:, s:s + 1]).then_inc(sem("exp"), 1)

            def back_out(s):
                act.wait_ge(sem("back"), 2 * s + 1)
                if s >= 2:
                    act.wait_ge(sem("valued"), s - 1)
                act.activation(PT[:, s % 2, 0:4].rearrange("p j i -> p (j i)"), PS[:, 4],
                               ACT.Copy).then_inc(sem("pt_act"), 1)

            def out(n):
                act.wait_ge(sem("o_turned"), n + 1)
                act.activation(AO[:, n * CH:(n + 1) * CH], PS[:, n], ACT.Identity,
                               bias=W["bv"]).then_inc(sem("ao"), 1)

            for s in range(TILES + 1):
                if s >= 1:
                    back_out(s - 1)
                if s < TILES:
                    exp(s)
            for n in range(NCH):
                out(n)

        @block.tensor
        def _(pe):
            pe.wait_ge(sem("means"), 1)
            pe.matmul(PS[:, 0, 0:NB], W["group"], mom[:, 0], start=True, stop=True).then_inc(sem("group_mean"), 1)
            pe.wait_ge(sem("vars"), 1)
            pe.matmul(PS[:, 1, 0:NB], W["group"], mom[:, 1], start=True, stop=True).then_inc(sem("group_var"), 1)
            for n in range(NCH):
                pe.wait_ge(sem("hf"), n // 2 + 1)
                pe.matmul(PS[:, n], W["wq"], HF[:, n * CH:(n + 1) * CH], start=True, stop=True).then_inc(sem("q"), 1)
            for n in range(NCH):
                pe.matmul(PS[:, 4 + n], W["wk"], HF[:, n * CH:(n + 1) * CH], start=True, stop=True).then_inc(sem("k"), 1)
            for n in range(4):
                pe.wait_ge(sem("q_out"), n + 1)
                for j in range(4):
                    t = 4 * n + j
                    ins = pe.matmul(PS[:, n, j * P:(j + 1) * P], HF[:, t * P:(t + 1) * P], W["wv"], start=True, stop=True)
                ins.then_inc(sem("vt"), 1)
            pe.wait_ge(sem("k_out"), NCH)
            pe.wait_ge(sem("vt_out"), 4)

            def scores(s):
                b = s // ITILES
                if s >= 2:
                    pe.wait_ge(sem("exp"), s - 1)
                for h in range(2):
                    c = b * PIX + h * CH
                    ins = pe.matmul(PS[:, 2 * (s % 2) + h], Qm[:, s * P:(s + 1) * P], Km[:, c:c + CH], start=True,
                                    stop=True)
                ins.then_inc(sem("scores"), 1)

            def back(s):
                pe.wait_ge(sem("exp"), s + 1)
                for h in range(2):
                    if s >= 1:
                        pe.wait_ge(sem("pt_dve" if h else "pt_act"), s)
                    for j in range(4):
                        t = 4 * h + j
                        ins = pe.transpose(PS[:, 4 + h, j * P:(j + 1) * P], E[:, s % 2, t * P:(t + 1) * P], W["ident"])
                    ins.then_inc(sem("back"), 1)

            def values(s):
                b = s // ITILES
                pe.wait_ge(sem("pt_act"), s + 1)
                pe.wait_ge(sem("pt_dve"), s + 1)
                if s >= 2:
                    pe.wait_ge(sem("o"), s - 1)
                for j in range(ITILES):
                    ins = pe.matmul(PS[:, 6 + s % 2, 0:P], PT[:, s % 2, j], Vt[:, b * ITILES + j], start=(j == 0),
                                    stop=(j == ITILES - 1))
                ins.then_inc(sem("valued"), 1)

            for s in range(TILES + 2):
                if s < TILES:
                    scores(s)
                if 1 <= s <= TILES:
                    back(s - 1)
                if s >= 2:
                    values(s - 2)
            for n in range(NCH):
                pe.wait_ge(sem("o"), 4 * n + 4)
                for j in range(4):
                    ins = pe.transpose(PS[:, n, j * P:(j + 1) * P], O[:, 4 * n + j], W["ident"])
                ins.then_inc(sem("o_turned"), 1)
            for n in range(NCH):
                pe.wait_ge(sem("ao"), n + 1)
                pe.matmul(PS[:, 4 + n], W["wo"], AO[:, n * CH:(n + 1) * CH], start=True, stop=True).then_inc(sem("proj"), 1)


def layer_norm(nc, name, X, XN, PS, centre, mean, eps):
    with ExitStack() as ctx:
        st = Stage(nc, ctx)
        sb, sem = st.sb, st.sem
        SQ = sb(name + "_sq", [P, 2, CH])
        R = sb(name + "_r", [P, T])
        block = ctx.enter_context(nc.Block())

        @block.tensor
        def _(pe):
            for s in range(NCH + 2):
                if s < NCH:
                    pe.matmul(PS[:, s], centre, X[:, s * CH:(s + 1) * CH], start=True, stop=True).then_inc(sem("centred"), 1)
                if s >= 2:
                    n = s - 2
                    pe.wait_ge(sem("square"), n + 1)
                    pe.matmul(PS[:, 4 + n], mean, SQ[:, n % 2], start=True, stop=True).then_inc(sem("var"), 1)

        @block.vector
        def _(dve):
            for n in range(NCH):
                c = slice(n * CH, (n + 1) * CH)
                dve.wait_ge(sem("inverse"), n + 1)
                dve.tensor_tensor(XN[:, c], PS[:, n], R[:, c], ALU.mult)

        @block.scalar
        def _(act):
            for n in range(NCH):
                act.wait_ge(sem("centred"), n + 1)
                if n >= 2:
                    act.wait_ge(sem("var"), n - 1)
                act.activation(SQ[:, n % 2], PS[:, n], ACT.Square).then_inc(sem("square"), 1)
            for n in range(NCH):
                act.wait_ge(sem("var"), n + 1)
                act.activation(R[:, n * CH:(n + 1) * CH], PS[:, 4 + n], ACT.Ln, bias=eps).then_inc(sem("log"), 1)
            for n in range(NCH):
                c = slice(n * CH, (n + 1) * CH)
                act.wait_ge(sem("log"), n + 1)
                act.activation(R[:, c], R[:, c], ACT.Exp, scale=-0.5).then_inc(sem("inverse"), 1)


REL = 257
WIN = 3 * P
GT = 4
ROW = 512


def l2a_pack(w):
    p = Pack()
    L = lambda n: w["L2_attn_" + n]
    p.add("b_out", L("b_out").reshape(P, 1))
    for n, name in enumerate(("wq", "wk", "wv")):
        p.add(name, L("W_qkv")[:, n * P:(n + 1) * P])
    p.add("w_out", L("W_out"))
    p.add("rel", np.tile(L("rel_table").T[:, ::-1], (HEADS, 1)))
    p.add("ident", np.eye(P, dtype=np.float32))
    p.add("mean", np.full((P, P), 1.0 / P, np.float32))
    p.add("centre", np.eye(P, dtype=np.float32) - np.float32(1.0 / P))
    p.add("eps", np.full((P, 1), 1e-5, np.float32))
    hm = np.zeros((P, HEADS + 1), np.float32)
    hm[:, :HEADS] = np.repeat(np.eye(HEADS, dtype=np.float32), DH, axis=0)
    p.add("hmask", hm)
    p.add("pick", np.tile(np.eye(HID, DH, dtype=np.float32), (4, 1)))
    return p


def l2_attention(nc, X, XN, PS, W, scratch):
    with ExitStack() as ctx:
        st = Stage(nc, ctx)
        sb, sem = st.sb, st.sem
        Qm = sb("r_q", [P, T])
        K = sb("r_k", [P, 3, T])
        V = sb("r_v", [P, NB, ITILES, P])
        VH = sb("r_vh", [P, NB, ITILES, HID])
        qh = sb("r_qh", [P, NB, PIX])
        qd = sb("r_qd", [P, NB, PIX])
        RD = sb("r_rd", [P, NB, ITILES, ROW])
        band = sb("r_band", [P, NB, ITILES, WIN])
        raw = sb("r_raw", [P, 2])
        mx = sb("r_max", [P, 2])
        den = sb("r_den", [P, NB, ITILES])
        rden = sb("r_rden", [P, NB, ITILES])
        E = sb("r_e", [P, 2, PIX])
        PT = sb("r_pt", [P, 2, ITILES, GT, P])
        OG = sb("r_og", [P, CH])
        O = XN[:].rearrange("p (t c) -> p t c", c=P)
        AO = Qm
        SCALE = float(DH) ** -0.5
        l2_project(nc, st, PS, W, XN, Qm, K, V, VH, RD)
        with nc.Block() as block:
            l2_heads(nc, st, block, PS, W, scratch, Qm, K, V, VH, qh, qd, RD, band, raw, mx, den, rden, E, PT, OG, O, SCALE)
        l2_output(nc, st, X, PS, W, O, AO)


def l2_project(nc, st, PS, W, XN, Qm, K, V, VH, RD):
    sem = st.sem
    with nc.Block() as block:
        @block.tensor
        def _(pe):
            for k, name in enumerate(("wq", "wk")):
                for n in range(NCH):
                    pe.matmul(PS[:, 4 * k + n], W[name], XN[:, n * CH:(n + 1) * CH], start=True,
                              stop=True).then_inc(sem(name), 1)
            for n in range(4):
                pe.wait_ge(sem("q_out"), n + 1)
                for j in range(4):
                    t = 4 * n + j
                    ins = pe.matmul(PS[:, n, j * P:(j + 1) * P], XN[:, t * P:(t + 1) * P], W["wv"], start=True, stop=True)
                ins.then_inc(sem("v"), 1)

        @block.scalar
        def _(act):
            for n in range(NCH):
                act.wait_ge(sem("wq"), n + 1)
                act.activation(Qm[:, n * CH:(n + 1) * CH], PS[:, n], ACT.Copy).then_inc(sem("q_out"), 1)
            for n in range(4):
                act.wait_ge(sem("v"), n + 1)
                act.activation(V[:, n // 2, 4 * (n % 2):4 * (n % 2) + 4].rearrange("p c k -> p (c k)"), PS[:, n], ACT.Copy)

        @block.vector
        def _(dve):
            for n in range(NCH):
                dve.wait_ge(sem("wk"), n + 1)
                dve.tensor_copy(K[:, 0, n * CH:(n + 1) * CH], PS[:, 4 + n]).then_inc(sem("k_out"), 1)
            dve.wait_ge(sem("k_out"), NCH)
            dve.tensor_scalar(K[:, 1], K[:, 0], W["rel"][:, 0:1], None, ALU.add)
            dve.tensor_scalar(K[:, 2], K[:, 0], W["rel"][:, REL - 1:REL], None, ALU.add)

        @block.gpsimd
        def _(pool):
            pool.memset(VH[:], 0.0)
            pool.memset(RD[:, :, :, ROW - 1:ROW], 0.0)


def l2_heads(nc, st, block, PS, W, scratch, Qm, K, V, VH, qh, qd, RD, band, raw, mx, den, rden, E, PT, OG, O, SCALE):
    sem = st.sem
    SCORES, EXP, BACK, PTS, RDS, SENT, ADDED, VALUED, OUT, PICKED = 16, 2, 4, 1, 1, 32, 16, 3, 1, 1
    ALL = NB * ITILES
    tiles = lambda i, t: i * ITILES + t
    groups = lambda i, t: i * (ITILES // GT) + t // GT

    def place(n, k):
        return n * NB + k // ITILES, (k // ITILES) % NB, k % ITILES

    def heads(eng, lag, emit):
        for s in range(lag):
            emit(0, s, 2)
        with eng.Fori(0, HEADS - 2) as n:
            for s in range(lag, lag + ALL):
                emit(n, s, 2)
        for n in (HEADS - 2, HEADS - 1):
            for s in range(lag, lag + ALL):
                emit(n, s, HEADS - 1 - n)

    LEFT = P - 1

    def wide(t):
        return PS[:, 2 * (t % 2):2 * (t % 2) + 2].rearrange("p a n -> p (a n)")

    def ends(eng, b, name):
        r = LEFT + REL
        eng.tensor_copy(RD[:, b, :, 0:LEFT], RD[:, b, :, LEFT:LEFT + 1].broadcast_to([P, ITILES, LEFT])
                        ).then_inc(sem(name), 1)
        eng.tensor_copy(RD[:, b, :, r:r + LEFT], RD[:, b, :, r - 1:r].broadcast_to([P, ITILES, LEFT])
                        ).then_inc(sem(name), 1)

    def exists(k, more):
        return 0 <= k < ALL * (more + 1)

    @block.tensor
    def _(pe):
        pe.sem_inc(sem("scores"), SCORES)
        pe.sem_inc(sem("qr"), ALL)
        pe.sem_inc(sem("backs"), BACK)
        pe.sem_inc(sem("valued"), VALUED)
        pe.sem_inc(sem("picked"), PICKED)

        def distances(f, b, t):
            if t == 0:
                pe.wait_ge(sem("qd"), f + 1)
            pe.wait_ge(sem("rd"), tiles(f, t) + RDS)
            pe.matmul(PS[:, 6, 0:REL], qd[:, b, t * P:(t + 1) * P], W["rel"], start=True, stop=True).then_inc(sem("qr"), 1)

        def scores(i, b, t):
            if t == 0:
                pe.wait_ge(sem("qh"), i + 1)
            pe.wait_ge(sem("exp"), tiles(i, t) - 1 + EXP)
            edges = sorted({0, max(0, (t - 1) * P), CH, min(PIX, (t + 2) * P), PIX})
            for lo, hi in zip(edges, edges[1:]):
                kind = 1 if hi <= (t - 1) * P else 2 if lo >= (t + 2) * P else 0
                ins = pe.matmul(PS[:, 2 * (t % 2) + lo // CH, lo % CH:lo % CH + hi - lo], qh[:, b, t * P:(t + 1) * P],
                                K[:, kind, b * PIX + lo:b * PIX + hi], start=True, stop=True, skip_group_check=True)
            ins.then_inc(sem("scores"), 1)

        def back(i, b, t):
            pe.wait_ge(sem("exp"), tiles(i, t) + 1 + EXP)
            for h in range(2):
                pe.wait_ge(sem("pt_dve" if h else "pt_act"), tiles(i, t) + PTS)
                for j in range(4):
                    c = (4 * h + j) * P
                    ins = pe.transpose(PS[:, 4 + h, j * P:(j + 1) * P], E[:, t % 2, c:c + P], W["ident"])
                ins.then_inc(sem("backs"), 1)

        def values(i, b, t):
            if t < GT:
                pe.wait_ge(sem("vh"), i + 1)
            pe.wait_ge(sem("o_out"), groups(i, t) + OUT)
            pe.wait_ge(sem("pt_act"), tiles(i, t) + 1 + PTS)
            pe.wait_ge(sem("pt_dve"), tiles(i, t) + 1 + PTS)
            for j in range(ITILES):
                r = 32 * (j % 4)
                ins = pe.matmul(PS[r:r + 32, 7], VH[:, b, j], PT[:, t // GT, j].rearrange("p t i -> p (t i)"),
                                start=(j < 4), stop=(j >= 4), tile_position=(0, r), skip_group_check=True)
            ins.then_inc(sem("valued"), 1)

        def pick(i, b, t):
            pe.wait_ge(sem("og"), groups(i, t) + 1)
            for q in range(GT):
                ins = pe.matmul(PS[:, 7, q * DH:(q + 1) * DH], OG[:, q * P:(q + 1) * P], W["pick"], start=True,
                                stop=True, skip_group_check=True)
            ins.then_inc(sem("picked"), 1)

        for k in range(NB * ITILES):
            b, t = divmod(k, ITILES)
            if t == 0:
                pe.wait_ge(sem("qd"), b + 1)
            if k >= 4:
                pe.wait_ge(sem("first_dve" if k % 2 else "first_act"), k // 2 - 1)
            pe.matmul(PS[:, k % 4, 0:REL], qd[:, b, t * P:(t + 1) * P], W["rel"], start=True, stop=True
                      ).then_inc(sem("first"), 1)
        pe.wait_ge(sem("first_act"), NB * ITILES // 2)
        pe.wait_ge(sem("first_dve"), NB * ITILES // 2)

        def position(n, s, more):
            if exists(s, more):
                i, b, t = place(n, s)
                scores(i, b, t)
            if exists(s + ALL, more):
                distances(i + 2, b, t)
            if exists(s - 1, more):
                back(*place(n, s - 1))
            if 2 <= s < 2 + ALL and (s - 2) % GT == GT - 1:
                values(*place(n, s - 2))
            if 3 <= s < 3 + ALL and (s - 3) % GT == GT - 1:
                pick(*place(n, s - 3))

        heads(pe, 3, position)

    @block.scalar
    def _(act):
        act.sem_inc(sem("rd"), ALL + RDS)
        act.sem_inc(sem("exp"), EXP)
        act.sem_inc(sem("pt_act"), PTS)

        def distances_out(f, b, t):
            if t == 0:
                act.wait_ge(sem("rd_sent"), (f + 1) * 16)
            act.wait_ge(sem("qr"), tiles(f, t) + 1)
            act.activation(RD[:, b, t, LEFT:LEFT + REL], PS[:, 6, 0:REL], ACT.Copy).then_inc(sem("rd"), 1)

        def exp(i, b, t):
            act.wait_ge(sem("top"), tiles(i, t) + 1)
            act.wait_ge(sem("backs"), tiles(i, t) * 2 - 2 + BACK)
            act.activation(E[:, t % 2], wide(t), ACT.Exp, bias=mx[:, t % 2:t % 2 + 1], scale=SCALE,
                           accum_out=den[:, b, t:t + 1]).then_inc(sem("exp"), 1)

        def back_out(i, b, t):
            act.wait_ge(sem("backs"), tiles(i, t) * 2 + 1 + BACK)
            act.wait_ge(sem("valued"), groups(i, t) - 1 + VALUED)
            act.activation(PT[:, t // GT, 0:4, t % GT], PS[:, 4].rearrange("p (j i) -> p j i", i=P),
                           ACT.Copy).then_inc(sem("pt_act"), 1)

        def group_out(i, b, t):
            act.wait_ge(sem("valued"), groups(i, t) + 1 + VALUED)
            act.wait_ge(sem("picked"), groups(i, t) + PICKED)
            act.activation(OG[:], PS[:, 7], ACT.Copy).then_inc(sem("og"), 1)

        for k in range(0, ALL, 2):
            act.wait_ge(sem("first"), k + 1)
            act.activation(RD[:, k // ITILES, k % ITILES, LEFT:LEFT + REL], PS[:, k % 4, 0:REL], ACT.Copy
                           ).then_inc(sem("first_act"), 1)

        def position(n, s, more):
            if 3 <= s < 3 + ALL and (s - 3) % GT == GT - 1:
                group_out(*place(n, s - 3))
            i, b, t = place(n, s)
            if exists(s + ALL, more):
                distances_out(i + 2, b, t)
            if exists(s - 1, more):
                back_out(*place(n, s - 1))
            if exists(s, more):
                exp(i, b, t)

        heads(act, 3, position)

    @block.vector
    def _(dve):
        dve.sem_inc(sem("pt_dve"), PTS)
        dve.sem_inc(sem("added"), ADDED)
        dve.sem_inc(sem("o_out"), OUT)

        def top(i, b, t):
            dve.wait_ge(sem("scores"), tiles(i, t) + 1 + SCORES)
            if t == 0:
                dve.wait_ge(sem("band_in"), (i + 1) * 16)
            lo, hi = max(0, (t - 1) * P), min(PIX, (t + 2) * P)
            u = lo - (t - 1) * P
            v = wide(t)
            dve.tensor_tensor(v[:, lo:hi], v[:, lo:hi], band[:, b, t, u:u + hi - lo], ALU.add).then_inc(sem("added"), 1)
            dve.wait_ge(sem("added"), tiles(i, t) + 1 + ADDED)
            dve.tensor_reduce(raw[:, t % 2:t % 2 + 1], v, AX.X, ALU.max).then_inc(sem("maxed"), 1)
            dve.wait_ge(sem("maxed"), tiles(i, t) + 1)
            dve.tensor_scalar(mx[:, t % 2:t % 2 + 1], raw[:, t % 2:t % 2 + 1], -SCALE, None, ALU.mult).then_inc(sem("top"), 1)

        def back_out(i, b, t):
            dve.wait_ge(sem("backs"), tiles(i, t) * 2 + 2 + BACK)
            dve.wait_ge(sem("valued"), groups(i, t) - 1 + VALUED)
            dve.tensor_copy(PT[:, t // GT, 4:8, t % GT], PS[:, 5].rearrange("p (j i) -> p j i", i=P)
                            ).then_inc(sem("pt_dve"), 1)

        def outputs(n, i, b, t):
            g = slice(t + 1 - GT, t + 1)
            dve.wait_ge(sem("exp"), tiles(i, t) + 1 + EXP)
            dve.reciprocal(rden[:, b, g], den[:, b, g]).then_inc(sem("inverse"), 1)
            dve.wait_ge(sem("inverse"), groups(i, t) + 1)
            dve.wait_ge(sem("picked"), groups(i, t) + 1 + PICKED)
            dve.tensor_tensor(O[:, b * ITILES + t + 1 - GT:b * ITILES + t + 1, bass.ds(n * DH, DH)],
                              PS[:, 7, 0:GT * DH].rearrange("p (t d) -> p t d", d=DH), bc(rden[:, b, g], 2, DH),
                              ALU.mult).then_inc(sem("o_out"), 1)

        def position(n, s, more):
            if exists(s - 2, more):
                back_out(*place(n, s - 2))
            if exists(s, more):
                top(*place(n, s))
            if 4 <= s < 4 + ALL and (s - 4) % GT == GT - 1:
                outputs(n, *place(n, s - 4))

        for b in range(NB):
            for k in range(b * ITILES + 1, (b + 1) * ITILES, 2):
                dve.wait_ge(sem("first"), k + 1)
                dve.tensor_copy(RD[:, b, k % ITILES, LEFT:LEFT + REL], PS[:, k % 4, 0:REL]).then_inc(sem("first_dve"), 1)
            dve.wait_ge(sem("first_act"), (b + 1) * ITILES // 2)
            dve.wait_ge(sem("first_dve"), (b + 1) * ITILES // 2)
            ends(dve, b, "first_ends")
        heads(dve, 4, position)

    @block.gpsimd
    def _(pool):
        def repeat_ends(f, b):
            reg_wait(pool, sem("rd"), tiles(f, ITILES) + RDS, sem("pool_passed"))
            ends(pool, b, "ends")

        def head_queries(q, name, f, head, b):
            pool.tensor_tensor(q[:, b], Qm[:, b * PIX:(b + 1) * PIX],
                               W["hmask"][:, bass.ds(head, 1)].broadcast_to([P, PIX]), ALU.mult).then_inc(sem(name), 1)

        pool.sem_inc(sem("ends"), 2 * NB)
        for f in range(NB):
            head_queries(qd, "qd", f, 0, f)
        for f in range(NB):
            head_queries(qh, "qh", f, 0, f)

        def head_values(n, b):
            reg_wait(pool, sem("valued"), groups(n * NB + b - 1, 0) + VALUED, sem("pool_passed"))
            pool.tensor_copy(VH[:, b, :, 0:DH], V[:, b, :, bass.ds(n * DH, DH)]).then_inc(sem("vh"), 1)

        pool.wait_ge(sem("first_act"), ALL // 2)
        pool.wait_ge(sem("first_dve"), ALL // 2)
        head_queries(qd, "qd", 2, 1, 0)
        with pool.Fori(0, HEADS - 1) as n:
            for b in range(NB):
                i = n * NB + b
                head_values(n, b)
                head_queries(qd, "qd", i + 3, n + 1 + b, 1 - b)
                repeat_ends(i + 2, b)
                reg_wait(pool, sem("added"), tiles(i, ITILES) + ADDED, sem("pool_passed"))
                head_queries(qh, "qh", i + 2, n + 1, b)
        for b in range(NB):
            head_values(HEADS - 1, b)

    @block.sync
    def _(sp):
        sp.sem_inc(sem("rd_sent"), SENT)

        def skew(f, b, name):
            sp.wait_ge(sem(name), f * 2 + 2)
            sp.dma_start(scratch[b], RD[:, b]).then_inc(sem("rd_sent"), 16)
            sp.wait_ge(sem("rd_sent"), (f + 1) * 16 + SENT)
            sp.wait_ge(sem("added"), tiles(f, 0) - ITILES + ADDED)
            rows = bass.AP(tensor=scratch.tensor, offset=b * P * ITILES * ROW + LEFT,
                           ap=[[ITILES * ROW - 1, P], [ROW, ITILES], [1, WIN]])
            sp.dma_start(band[:, b], rows).then_inc(sem("band_in"), 16)

        for f in range(NB):
            skew(f, f, "first_ends")
        with sp.Fori(0, HEADS - 1) as n:
            for b in range(NB):
                skew(n * 2 + b + 2, b, "ends")
        sp.wait_ge(sem("band_in"), HEADS * NB * 16)


def l2_output(nc, st, X, PS, W, O, AO):
    sem = st.sem
    with nc.Block() as block:
        @block.tensor
        def _(pe):
            for n in range(NCH):
                for j in range(4):
                    ins = pe.transpose(PS[:, n, j * P:(j + 1) * P], O[:, 4 * n + j], W["ident"])
                ins.then_inc(sem("o_turned"), 1)
            for n in range(NCH):
                pe.wait_ge(sem("ao"), n + 1)
                pe.matmul(PS[:, 4 + n], W["w_out"], AO[:, n * CH:(n + 1) * CH], start=True, stop=True).then_inc(sem("out"), 1)

        @block.scalar
        def _(act):
            for n in range(NCH):
                act.wait_ge(sem("o_turned"), n + 1)
                act.activation(AO[:, n * CH:(n + 1) * CH], PS[:, n], ACT.Copy).then_inc(sem("ao"), 1)

        @block.vector
        def _(dve):
            for n in range(NCH):
                dve.wait_ge(sem("out"), n + 1)
                x = X[:, n * CH:(n + 1) * CH]
                dve.scalar_tensor_tensor(x, PS[:, 4 + n], W["b_out"], x, ALU.add, ALU.add)


HB = 4
NODES = 32
GUESSES = 8
STEPS_N = PIX - 1
DT = 1.0 / (PIX - 1)
CLOSE = 2.0 ** -18


def integration(nodes, times):
    x = np.cos(np.pi * (np.arange(nodes) + 0.5) / nodes)
    k = np.arange(nodes)
    to_coef = 2.0 / nodes * np.cos(np.outer(k, np.arccos(x)))
    to_coef[0] *= 0.5
    t = lambda z: np.cos(np.outer(np.arange(nodes + 2), np.arccos(np.clip(z, -1.0, 1.0))))
    z = 2.0 * times - 1.0
    tz, t0 = t(z), t(np.array([-1.0]))
    anti = np.zeros((nodes, len(times)))
    for n in range(nodes):
        if n == 0:
            a = lambda v: v[1]
        elif n == 1:
            a = lambda v: v[2] / 4.0
        else:
            a = lambda v, n=n: v[n + 1] / (2.0 * (n + 1)) - v[n - 1] / (2.0 * (n - 1))
        anti[n] = a(tz) - a(t0)
    return (0.5 * to_coef.T @ anti).astype(np.float32)


def l2f_pack(w):
    p = Pack()
    L = lambda n: w["L2_ffn_" + n]
    p.add("w1", L("W1").T)
    p.add("w2", L("W2").T.reshape(HB, P, HB * P).transpose(1, 0, 2))
    p.add("w3", L("W3").T.reshape(HB, P, P).transpose(1, 0, 2))
    p.add("b1", L("b1").reshape(HB, P).T)
    p.add("b2", L("b2").reshape(HB, P).T)
    p.add("b3", L("b3").reshape(P, 1))
    p.add("b3_row", np.tile(L("b3").reshape(1, P), (NB * NODES, 1)))
    p.add("mean", np.full((P, P), 1.0 / P, np.float32))
    p.add("centre", np.eye(P, dtype=np.float32) - np.float32(1.0 / P))
    p.add("eps", np.full((P, 1), 1e-5, np.float32))
    x = 0.5 + 0.5 * np.cos(np.pi * (np.arange(NODES) + 0.5) / NODES)
    p.add("to_nodes", np.kron(np.eye(NB, dtype=np.float32), integration(NODES, x)))
    p.add("to_steps", np.kron(np.eye(NB, dtype=np.float32), integration(NODES, np.arange(PIX) * DT)))
    return p


def l2_guess(nc, PS, W, Y0, Y):
    with ExitStack() as ctx:
        st = Stage(nc, ctx)
        sb, sem = st.sb, st.sem
        N = NB * NODES
        YN = sb("g_y", [P, N])
        H1 = sb("g_h1", [P, HB, N])
        H2 = sb("g_h2", [P, HB, N])
        F = sb("g_f", [N, P])
        block = ctx.enter_context(nc.Block())

        @block.vector
        def _(dve):
            dve.tensor_copy(YN[:].rearrange("p (b n) -> p b n", b=NB), bc(Y0[:], 2, NODES)).then_inc(sem("y"), 1)
            with dve.Fori(0, GUESSES) as g:
                dve.wait_ge(sem("f"), g + 1)
                dve.tensor_tensor(F[:], PS[0:N, 2, 0:P], W["b3_row"], ALU.add).then_inc(sem("f_out"), 1)
                dve.wait_ge(sem("moved"), g + 1)
                dve.tensor_tensor(YN[:].rearrange("p (b n) -> p b n", b=NB),
                                  PS[:, 3, 0:N].rearrange("p (b n) -> p b n", b=NB), bc(Y0[:], 2, NODES),
                                  ALU.add).then_inc(sem("y"), 1)
            for n in range(NCH):
                dve.wait_ge(sem("steps"), n + 1)
                dve.tensor_scalar(Y[:, n * CH:(n + 1) * CH], PS[:, 4 + n], Y0[:, n // 2:n // 2 + 1], None, ALU.add)

        @block.scalar
        def _(act):
            with act.Fori(0, GUESSES) as g:
                for k in range(HB):
                    act.wait_ge(sem("z1"), g + 1)
                    act.activation(H1[:, k], PS[:, 0, k * N:(k + 1) * N], ACT.Tanh, bias=W["b1"][:, k:k + 1]
                                   ).then_inc(sem("h1"), 1)
                for k in range(HB):
                    act.wait_ge(sem("z2"), g + 1)
                    act.activation(H2[:, k], PS[:, 1, k * N:(k + 1) * N], ACT.Tanh, bias=W["b2"][:, k:k + 1]
                                   ).then_inc(sem("h2"), 1)

        @block.tensor
        def _(pe):
            with pe.Fori(0, GUESSES) as g:
                pe.wait_ge(sem("y"), g + 1)
                for k in range(HB):
                    ins = pe.matmul(PS[:, 0, k * N:(k + 1) * N], W["w1"][:, k * P:(k + 1) * P], YN[:], start=True, stop=True)
                ins.then_inc(sem("z1"), 1)
                pe.wait_ge(sem("h1"), g * HB + HB)
                for k in range(HB):
                    for m in range(HB):
                        c = (m * HB + k) * P
                        ins = pe.matmul(PS[:, 1, k * N:(k + 1) * N], W["w2"][:, c:c + P], H1[:, m], start=(m == 0),
                                        stop=(m == HB - 1))
                ins.then_inc(sem("z2"), 1)
                pe.wait_ge(sem("h2"), g * HB + HB)
                for m in range(HB):
                    ins = pe.matmul(PS[0:N, 2, 0:P], H2[:, m], W["w3"][:, m * P:(m + 1) * P], start=(m == 0),
                                    stop=(m == HB - 1))
                ins.then_inc(sem("f"), 1)
                reg_wait(pe, sem("f_out"), g + 1, sem("pe_passed"))
                pe.matmul(PS[:, 3, 0:N], F[:], W["to_nodes"], start=True, stop=True).then_inc(sem("moved"), 1)
            for n in range(NCH):
                pe.matmul(PS[:, 4 + n], F[:], W["to_steps"][:, n * CH:(n + 1) * CH], start=True,
                          stop=True).then_inc(sem("steps"), 1)


def l2_sweeps(nc, PS, W, Y0, Y):
    with ExitStack() as ctx:
        st = Stage(nc, ctx)
        sb, sem = st.sb, st.sem
        Z = sb("s_z", [P, 2, CH])
        KS = sb("s_k", [P, 2, CH])
        S = sb("s_sum", [P, T])
        H1 = sb("s_h1", [P, 2, HB, CH])
        H2 = sb("s_h2", [P, 2, HB, CH])
        NEW = sb("s_new", [P, T])
        ones = sb("s_ones", [P, PIX])
        gap = sb("s_gap", [P, 2])
        size = sb("s_size", [P, 2])
        off = sb("s_off", [P, 2])
        flag = sb("s_flag", [1, 1], I32)
        EV = 4
        GROUPS = EV * 2 * (2 * HB + 1)
        block = ctx.enter_context(nc.Block())

        def schedule():
            out = []
            for e in range(EV):
                for layer in range(3):
                    for c in range(2):
                        for k in range(HB if layer < 2 else 1):
                            out.append((e, layer, c, k))
            return out

        GR = schedule()
        acts = [g for g, x in enumerate(GR) if x[1] < 2]
        dves = [g for g, x in enumerate(GR) if x[1] == 2]
        NA, ND = len(acts), len(dves)

        @block.tensor
        def _(pe):
            end = pe.alloc_register("pe_end")
            pe.reg_mov(end, STEPS_N)
            with pe.Fori(0, end) as sweep:
                with pe.Fori(0, NB) as b:
                    it = sweep * 2 + b
                    for g, (e, layer, c, k) in enumerate(GR):
                        if g >= 8:
                            before = g - 8
                            if before in acts:
                                pe.wait_ge(sem("tanh"), it * NA + acts.index(before) + 1)
                            else:
                                pe.wait_ge(sem("taken"), it * ND + dves.index(before) + 1)
                        elif g == 0:
                            pe.wait_ge(sem("free"), it + 1)
                        bank = PS[:, g % 8]
                        if layer == 0:
                            if e == 0:
                                if c == 0 and k == 0:
                                    pe.wait_ge(sem("y"), sweep + 1)
                                x = Y[:, bass.ds(b * PIX + c * CH, CH)]
                            else:
                                if k == 0:
                                    pe.wait_ge(sem("z"), (it * (EV - 1) + e - 1) * 2 + c + 1)
                                x = Z[:, c]
                            pe.matmul(bank, W["w1"][:, k * P:(k + 1) * P], x, start=True, stop=True).then_inc(sem("filled"), 1)
                        elif layer == 1:
                            if k == 0:
                                pe.wait_ge(sem("tanh"), it * NA + (e * 2 * 2 + c) * HB + HB)
                            for m in range(HB):
                                col = (m * HB + k) * P
                                ins = pe.matmul(bank, W["w2"][:, col:col + P], H1[:, c, m], start=(m == 0), stop=(m == HB - 1))
                            ins.then_inc(sem("filled"), 1)
                        else:
                            pe.wait_ge(sem("tanh"), it * NA + ((e * 2 + 1) * 2 + c) * HB + HB)
                            for m in range(HB):
                                ins = pe.matmul(bank, W["w3"][:, m * P:(m + 1) * P], H2[:, c, m], start=(m == 0),
                                                stop=(m == HB - 1))
                            ins.then_inc(sem("filled"), 1)
                reg_wait(pe, sem("off"), sweep + 1, sem("pe_passed"))
                pe.matmul(PS[0:1, 0, 0:1], off[:, 0:1], ones[:, 0:1], start=True, stop=False)
                pe.matmul(PS[0:1, 0, 0:1], off[:, 1:2], ones[:, 0:1], start=False, stop=True).then_inc(sem("count"), 1)
                reg_wait(pe, sem("flag"), sweep + 1, sem("pe_passed"))
                pe.reg_load(end, flag[0:1, 0:1])

        @block.scalar
        def _(act):
            end = act.alloc_register("act_end")
            act.reg_mov(end, STEPS_N)
            with act.Fori(0, end) as sweep:
                with act.Fori(0, NB) as b:
                    it = sweep * 2 + b
                    for g in acts:
                        e, layer, c, k = GR[g]
                        act.wait_ge(sem("filled"), it * GROUPS + g + 1)
                        H = H1 if layer == 0 else H2
                        bias = W["b1" if layer == 0 else "b2"][:, k:k + 1]
                        act.activation(H[:, c, k], PS[:, g % 8], ACT.Tanh, bias=bias).then_inc(sem("tanh"), 1)
                reg_wait(act, sem("flag"), sweep + 1, sem("act_passed"))
                act.reg_load(end, flag[0:1, 0:1])

        @block.vector
        def _(dve):
            end = dve.alloc_register("dve_end")
            dve.reg_mov(end, STEPS_N)
            dve.memset(ones[:], 1.0)
            dve.sem_inc(sem("y"), 1)
            dve.sem_inc(sem("free"), 1)
            with dve.Fori(0, end) as sweep:
                for b in range(NB):
                    it = sweep * 2 + b
                    for d, g in enumerate(dves):
                        e, _, c, _ = GR[g]
                        dve.wait_ge(sem("filled"), it * GROUPS + g + 1)
                        s = S[:, bass.ds(b * PIX + c * CH, CH)]
                        y = Y[:, bass.ds(b * PIX + c * CH, CH)]
                        if e < EV - 1:
                            dve.tensor_scalar(KS[:, c], PS[:, g % 8], W["b3"], None, ALU.add).then_inc(sem("k"), 1)
                            dve.wait_ge(sem("k"), (it * (EV - 1) + e) * 2 + c + 1)
                            dve.scalar_tensor_tensor(Z[:, c], KS[:, c], DT / 2.0 if e < 2 else DT, y, ALU.mult,
                                                     ALU.add).then_inc(sem("z"), 1)
                            if e == 0:
                                dve.tensor_copy(s, KS[:, c]).then_inc(sem("taken"), 1)
                            else:
                                dve.scalar_tensor_tensor(s, KS[:, c], 2.0, s, ALU.mult, ALU.add).then_inc(sem("taken"), 1)
                            dve.wait_ge(sem("taken"), it * ND + d + 1)
                        else:
                            dve.scalar_tensor_tensor(s, PS[:, g % 8], W["b3"], s, ALU.add, ALU.add).then_inc(sem("taken"), 1)
                    dve.wait_ge(sem("taken"), it * ND + ND)
                    dve.sem_inc(sem("free"), 1)
                    c = b * PIX
                    steps, new = S[:, c:c + PIX], NEW[:, c:c + PIX]
                    dve.tensor_scalar(steps, steps, DT / 6.0, None, ALU.mult).then_inc(sem("scaled"), 1)
                    dve.tensor_copy(NEW[:, c:c + 1], Y0[:, b:b + 1])
                    dve.wait_ge(sem("scaled"), it + 1)
                    dve.tensor_tensor_scan(NEW[:, c + 1:c + PIX], ones[:, 0:PIX - 1], S[:, c:c + PIX - 1],
                                           Y0[:, b:b + 1], ALU.mult, ALU.add).then_inc(sem("new"), 1)
                    dve.wait_ge(sem("new"), it + 1)
                    dve.tensor_tensor(steps, new, Y[:, c:c + PIX], ALU.subtract).then_inc(sem("moved"), 1)
                    dve.wait_ge(sem("moved"), it + 1)
                    dve.tensor_reduce(gap[:, b:b + 1], steps, AX.X, ALU.max, apply_absolute_value=True)
                    dve.tensor_reduce(size[:, b:b + 1], new, AX.X, ALU.max, apply_absolute_value=True
                                      ).then_inc(sem("gap"), 1)
                dve.wait_ge(sem("gap"), sweep * 3 + 2)
                dve.tensor_scalar(size[:], size[:], 1.0, CLOSE, ALU.add, ALU.mult).then_inc(sem("gap"), 1)
                dve.wait_ge(sem("gap"), sweep * 3 + 3)
                dve.tensor_tensor(off[:], gap[:], size[:], ALU.is_gt).then_inc(sem("off"), 1)
                dve.tensor_copy(Y[:], NEW[:]).then_inc(sem("y"), 1)
                dve.wait_ge(sem("count"), sweep + 1)
                dve.tensor_scalar(flag[:], PS[0:1, 0, 0:1], 0.5, float(STEPS_N), ALU.is_gt, ALU.mult).then_inc(sem("flag"), 1)
                dve.wait_ge(sem("y"), sweep + 2)
                reg_wait(dve, sem("flag"), sweep + 1, sem("dve_passed"))
                dve.reg_load(end, flag[0:1, 0:1])


def first_token_norm(nc, X, PS, W, Y0):
    with ExitStack() as ctx:
        st = Stage(nc, ctx)
        sb, sem = st.sb, st.sem
        C = sb("f_centred", [P, NB])
        SQ = sb("f_square", [P, NB])
        R = sb("f_r", [P, NB])
        block = ctx.enter_context(nc.Block())

        @block.tensor
        def _(pe):
            pe.matmul(PS[:, 0, 0:NB], W["centre"], X[:, 0:T:PIX], start=True, stop=True).then_inc(sem("centred"), 1)
            pe.wait_ge(sem("square"), 1)
            pe.matmul(PS[:, 1, 0:NB], W["mean"], SQ[:], start=True, stop=True).then_inc(sem("var"), 1)

        @block.scalar
        def _(act):
            act.wait_ge(sem("var"), 1)
            act.activation(R[:], PS[:, 1, 0:NB], ACT.Sqrt, bias=W["eps"]).then_inc(sem("root"), 1)

        @block.vector
        def _(dve):
            link = Chain(dve, sem("dve_chain"))
            dve.wait_ge(sem("centred"), 1)
            link(dve.tensor_copy(C[:], PS[:, 0, 0:NB]))
            dve.tensor_tensor(SQ[:], C[:], C[:], ALU.mult).then_inc(sem("square"), 1)
            dve.wait_ge(sem("root"), 1)
            link(dve.reciprocal(R[:], R[:]))
            dve.tensor_tensor(Y0[:], C[:], R[:], ALU.mult)


def l2_trajectory(nc, X, PS, W):
    with ExitStack() as ctx:
        Y0 = ctx.enter_context(nc.sbuf_tensor("t_y0", [P, NB], F32))
        Y = ctx.enter_context(nc.sbuf_tensor("t_y", [P, T], F32))
        first_token_norm(nc, X, PS, W, Y0)
        l2_guess(nc, PS, W, Y0, Y)
        l2_sweeps(nc, PS, W, Y0, Y)
        with nc.Block() as block:
            @block.vector
            def _(dve):
                dve.tensor_tensor(X[:], X[:], Y[:], ALU.add)


GH = 4
GK = 16
GV = 32
GC = 16
GLOW = 16
CPT = P // GC
GD = GH * GK


def l3a_pack(w):
    p = Pack()
    L = lambda n: w["L3_attn_" + n]
    p.add("wq", L("Wq").T)
    p.add("wk", L("Wk").T)
    p.add("wv", L("Wv").T)
    p.add("wg", L("Wg").T)
    p.add("wo", L("Wo").T)
    p.add("wgk1", L("Wgk1").T)
    p.add("wgk2", L("Wgk2").T)
    p.add("bgk2", np.tile(L("bgk2"), NB).reshape(P, 1))
    p.add("g_norm", np.tile(L("g_norm_w"), GH).reshape(P, 1))
    p.add("ident", np.eye(P, dtype=np.float32))
    p.add("mean", np.full((P, P), 1.0 / P, np.float32))
    p.add("centre", np.eye(P, dtype=np.float32) - np.float32(1.0 / P))
    p.add("eps", np.full((P, 1), 1e-5, np.float32))
    p.add("head_mean", np.kron(np.eye(GH), np.full((GV, GV), 1.0 / GV)).astype(np.float32))
    p.add("hmask", np.kron(np.eye(NB * GH), np.ones((GK, 1))).astype(np.float32))
    p.add("cmask", np.kron(np.eye(CPT), np.ones((GC, 1))).astype(np.float32))
    p.add("causal", np.kron(np.eye(CPT), np.triu(np.ones((GC, GC)))).astype(np.float32))
    return p


def l3_gates(nc, PS, W, XN, QE, KE, KD, V, QM, decay):
    with ExitStack() as ctx:
        st = Stage(nc, ctx)
        sb, sem = st.sb, st.sem
        low = sb("ga_low", [GLOW, T])
        KP = sb("ga_k", [P, PIX])
        z = sb("ga_z", [P, PIX])
        mag = sb("ga_mag", [P, PIX])
        gk = sb("ga_gk", [P, PIX])
        keep = sb("ga_keep", [P, PIX])
        cum = sb("ga_cum", [P, PIX])
        ex = sb("ga_ex", [P, 3, PIX])
        rest = sb("ga_rest", [P, PIX])
        block = ctx.enter_context(nc.Block())
        chunks = lambda v: v.rearrange("p (n c) -> p n c", c=GC)

        @block.tensor
        def _(pe):
            for k, name in enumerate(("wq", "wk")):
                for h in range(2):
                    for b in range(NB):
                        c = b * PIX + h * CH
                        ins = pe.matmul(PS[GD * b:GD * b + GD, 2 * k + h], W[name], XN[:, c:c + CH], start=True, stop=True,
                                        skip_group_check=True)
                    ins.then_inc(sem("qk"), 1)
            for n in range(NCH):
                pe.matmul(PS[0:GLOW, 4 + n], W["wgk1"], XN[:, n * CH:(n + 1) * CH], start=True,
                          stop=True).then_inc(sem("low"), 1)
            pe.wait_ge(sem("low_out"), NCH)
            for h in range(2):
                for b in range(NB):
                    c = b * PIX + h * CH
                    ins = pe.matmul(PS[GD * b:GD * b + GD, 4 + h], W["wgk2"], low[:, c:c + CH], start=True, stop=True,
                                    skip_group_check=True)
            ins.then_inc(sem("gate"), 1)
            pe.wait_ge(sem("qk_out"), 4)
            for n in range(4):
                for j in range(4):
                    t = 4 * n + j
                    ins = pe.matmul(PS[:, n, j * P:(j + 1) * P], XN[:, t * P:(t + 1) * P], W["wv"], start=True, stop=True)
                ins.then_inc(sem("v"), 1)

        @block.scalar
        def _(act):
            for n in range(NCH):
                act.wait_ge(sem("low"), n + 1)
                act.activation(low[:, n * CH:(n + 1) * CH], PS[0:GLOW, 4 + n], ACT.Copy).then_inc(sem("low_out"), 1)
            link = Chain(act, sem("act_chain"))
            act.wait_ge(sem("gate"), 1)
            link(act.activation(z[:], PS[:, 4:6].rearrange("p a n -> p (a n)"), ACT.Identity, bias=W["bgk2"]))
            act.sem_inc(sem("z"), 1)
            link(act.activation(mag[:], z[:], ACT.Abs))
            link(act.activation(mag[:], mag[:], ACT.Exp, scale=-1.0))
            act.activation(mag[:], mag[:], ACT.Ln, bias=1.0).then_inc(sem("log"), 1)
            for n in range(4):
                act.wait_ge(sem("v"), n + 1)
                act.activation(V[:, n // 2, 4 * (n % 2):4 * (n % 2) + 4].rearrange("p c k -> p (c k)"), PS[:, n], ACT.Copy)
            act.wait_ge(sem("cum"), 1)
            act.activation(ex[:, 0], cum[:], ACT.Exp).then_inc(sem("ex"), 1)
            act.activation(ex[:, 1], cum[:], ACT.Exp, scale=-1.0).then_inc(sem("ex"), 1)
            act.activation(decay[:], cum[:, GC - 1::GC], ACT.Exp)
            act.wait_ge(sem("rest"), 1)
            act.activation(ex[:, 2], rest[:], ACT.Exp).then_inc(sem("ex"), 1)
            act.wait_ge(sem("qe"), 1)
            for n in range(NB * GH - 2, NB * GH):
                act.activation(QM[:, n], QE[:], ACT.Copy, scale=W["hmask"][:, n:n + 1])

        @block.gpsimd
        def _(pool):
            pool.memset(keep[:], 1.0).then_inc(sem("ones"), 1)
            pool.wait_ge(sem("ones"), 1)
            pool.memset(chunks(keep[:])[:, :, 0:1], 0.0).then_inc(sem("keep"), 1)
            pool.wait_ge(sem("qe"), 1)
            for n in range(NB * GH // 2):
                pool.tensor_tensor(QM[:, n], QE[:], W["hmask"][:, n:n + 1].broadcast_to([P, PIX]), ALU.mult)

        @block.vector
        def _(dve):
            link = Chain(dve, sem("dve_chain"))
            for h in range(2):
                dve.wait_ge(sem("qk"), h + 1)
                dve.tensor_scalar(QE[:, h * CH:(h + 1) * CH], PS[:, h], GK ** -0.5, None, ALU.mult).then_inc(sem("qk_out"), 1)
            for h in range(2):
                dve.wait_ge(sem("qk"), h + 3)
                dve.tensor_copy(KP[:, h * CH:(h + 1) * CH], PS[:, 2 + h]).then_inc(sem("qk_out"), 1)
            dve.wait_ge(sem("z"), 1)
            link(dve.tensor_scalar(gk[:], z[:], 0.0, None, ALU.min))
            dve.wait_ge(sem("log"), 1)
            link(dve.tensor_tensor(gk[:], gk[:], mag[:], ALU.subtract))
            link(dve.tensor_scalar(gk[:], gk[:], 1.0 / 16.0, None, ALU.mult))
            dve.wait_ge(sem("keep"), 1)
            link(dve.tensor_tensor_scan(cum[:], keep[:], gk[:], 0.0, ALU.mult, ALU.add))
            dve.sem_inc(sem("cum"), 1)
            c3 = chunks(cum[:])
            dve.tensor_tensor(chunks(rest[:]), c3[:, :, GC - 1:GC].broadcast_to([P, PIX // GC, GC]), c3,
                              ALU.subtract).then_inc(sem("rest"), 1)
            dve.wait_ge(sem("ex"), 1)
            dve.wait_ge(sem("qk_out"), 4)
            dve.tensor_tensor(QE[:], QE[:], ex[:, 0], ALU.mult).then_inc(sem("qe"), 1)
            dve.wait_ge(sem("ex"), 2)
            dve.tensor_tensor(KE[:], KP[:], ex[:, 1], ALU.mult)
            dve.wait_ge(sem("ex"), 3)
            dve.tensor_tensor(KD[:], KP[:], ex[:, 2], ALU.mult)
            dve.wait_ge(sem("qe"), 1)
            for n in range(NB * GH // 2, NB * GH - 2):
                dve.tensor_scalar(QM[:, n], QE[:], W["hmask"][:, n:n + 1], None, ALU.mult)


def l3_chunks(nc, PS, W, KE, KD, V, QM, decay, OT):
    with ExitStack() as ctx:
        st = Stage(nc, ctx)
        sb, sem = st.sb, st.sem
        KDM = sb("gb_kdm", [P, 2, CPT, P])
        S = sb("gb_s", [P, PIX // GC + 1, P])
        AM = sb("gb_a", [P, 2, NB, GH, P])
        block = ctx.enter_context(nc.Block())

        @block.vector
        def _(dve):
            dve.memset(S[:, 0], 0.0).then_inc(sem("state"), 1)

            def keys(t):
                dve.wait_ge(sem("turned"), t + 1)
                if t >= 2:
                    dve.wait_ge(sem("kv"), t - 1)
                dve.tensor_tensor(KDM[:, t % 2], bc(PS[:, t % 2, 0:P], 1, CPT), bc(W["cmask"], 2, P),
                                  ALU.mult).then_inc(sem("kdm"), 1)

            def states(t):
                dve.wait_ge(sem("kv"), t + 1)
                for j in range(CPT):
                    n = t * CPT + j
                    dve.wait_ge(sem("state"), n + 1)
                    dve.scalar_tensor_tensor(S[:, n + 1], S[:, n], decay[:, n:n + 1],
                                             PS[:, 2 + j // 4, (j % 4) * P:(j % 4 + 1) * P], ALU.mult,
                                             ALU.add).then_inc(sem("state"), 1)

            def masked(t):
                for b in range(NB):
                    dve.wait_ge(sem("scores"), NB * t + b + 1)
                    if t >= 2:
                        dve.wait_ge(sem("outs"), NB * (t - 2) + b + 1)
                    dve.tensor_tensor(AM[:, t % 2, b], PS[:, 4 + b].rearrange("p (h c) -> p h c", h=GH), bc(W["causal"], 1, GH),
                                      ALU.mult).then_inc(sem("am"), 1)

            keys(0)
            keys(1)
            for t in range(ITILES):
                masked(t)
                states(t)
                if t + 2 < ITILES:
                    keys(t + 2)

        @block.scalar
        def _(act):
            for t in range(ITILES):
                for b in range(NB):
                    act.wait_ge(sem("outs"), NB * t + b + 1)
                    c = b * PIX + t * P
                    act.activation(OT[:, c:c + P], PS[:, 6 + b, 0:P], ACT.Copy).then_inc(sem("ot"), 1)

        @block.tensor
        def _(pe):
            def turn(t):
                if t >= 2:
                    pe.wait_ge(sem("kdm"), t - 1)
                pe.transpose(PS[:, t % 2, 0:P], KD[:, t * P:(t + 1) * P], W["ident"]).then_inc(sem("turned"), 1)

            def key_values(t):
                pe.wait_ge(sem("kdm"), t + 1)
                pe.wait_ge(sem("state"), t * CPT + 1)
                for j in range(CPT):
                    for b in range(NB):
                        ins = pe.matmul(PS[GD * b:GD * b + GD, 2 + j // 4, (j % 4) * P:(j % 4 + 1) * P],
                                        KDM[:, t % 2, j, GD * b:GD * b + GD], V[:, b, t], start=True, stop=True,
                                        skip_group_check=True)
                ins.then_inc(sem("kv"), 1)

            def scores(t):
                for b in range(NB):
                    if t >= 1:
                        pe.wait_ge(sem("am"), NB * (t - 1) + b + 1)
                    pe.matmul(PS[:, 4 + b], KE[:, t * P:(t + 1) * P], QM[:, GH * b:GH * b + GH, t * P:(t + 1) * P],
                              start=True, stop=True).then_inc(sem("scores"), 1)

            def outputs(t):
                for b in range(NB):
                    pe.wait_ge(sem("am"), NB * t + b + 1)
                    if t >= 1:
                        pe.wait_ge(sem("ot"), NB * (t - 1) + b + 1)
                    for h in range(GH):
                        pe.matmul(PS[GV * h:GV * h + GV, 6 + b, 0:P], V[:, b, t, GV * h:GV * h + GV], AM[:, t % 2, b, h],
                                  start=True, stop=False, skip_group_check=True)
                    pe.wait_ge(sem("state"), (t + 1) * CPT)
                    for j in range(CPT):
                        c = t * P + j * GC
                        for h in range(GH):
                            ins = pe.matmul(PS[GV * h:GV * h + GV, 6 + b, j * GC:(j + 1) * GC],
                                            S[:, t * CPT + j, GV * h:GV * h + GV], QM[:, GH * b + h, c:c + GC],
                                            start=False, stop=(j == CPT - 1), skip_group_check=True)
                    ins.then_inc(sem("outs"), 1)

            turn(0)
            turn(1)
            scores(0)
            key_values(0)
            for t in range(ITILES):
                if t + 2 < ITILES:
                    turn(t + 2)
                if t + 1 < ITILES:
                    scores(t + 1)
                    key_values(t + 1)
                outputs(t)


def l3_gated_output(nc, X, PS, W, XN, OT):
    with ExitStack() as ctx:
        st = Stage(nc, ctx)
        sb, sem = st.sb, st.sem
        SQ = sb("go_sq", [P, 2, CH])
        R = sb("go_r", [P, T])
        G = sb("go_g", [P, T])
        block = ctx.enter_context(nc.Block())
        col = lambda n: slice(n * CH, (n + 1) * CH)

        @block.tensor
        def _(pe):
            for n in range(NCH):
                pe.matmul(PS[:, n], W["wg"], XN[:, col(n)], start=True, stop=True).then_inc(sem("g"), 1)
            for n in range(NCH):
                pe.wait_ge(sem("square"), n + 1)
                pe.matmul(PS[:, 4 + n], W["head_mean"], SQ[:, n % 2], start=True, stop=True).then_inc(sem("ms"), 1)
            for n in range(NCH):
                pe.wait_ge(sem("gated"), n + 1)
                pe.matmul(PS[:, n], W["wo"], OT[:, col(n)], start=True, stop=True).then_inc(sem("out"), 1)

        @block.scalar
        def _(act):
            for n in range(NCH):
                if n >= 2:
                    act.wait_ge(sem("ms"), n - 1)
                act.activation(SQ[:, n % 2], OT[:, col(n)], ACT.Square).then_inc(sem("square"), 1)
            for n in range(NCH):
                act.wait_ge(sem("g"), n + 1)
                act.activation(G[:, col(n)], PS[:, n], ACT.Silu).then_inc(sem("silu"), 1)
            for n in range(NCH):
                act.wait_ge(sem("ms"), n + 1)
                act.activation(R[:, col(n)], PS[:, 4 + n], ACT.Ln, bias=W["eps"]).then_inc(sem("log"), 1)
            for n in range(NCH):
                act.wait_ge(sem("log"), n + 1)
                act.activation(R[:, col(n)], R[:, col(n)], ACT.Exp, scale=-0.5).then_inc(sem("root"), 1)

        @block.vector
        def _(dve):
            for n in range(NCH):
                dve.wait_ge(sem("silu"), n + 1)
                dve.scalar_tensor_tensor(G[:, col(n)], G[:, col(n)], W["g_norm"], OT[:, col(n)], ALU.mult,
                                         ALU.mult).then_inc(sem("weighted"), 1)
                dve.wait_ge(sem("root"), n + 1)
                dve.wait_ge(sem("weighted"), n + 1)
                dve.tensor_tensor(OT[:, col(n)], G[:, col(n)], R[:, col(n)], ALU.mult).then_inc(sem("gated"), 1)
            for n in range(NCH):
                dve.wait_ge(sem("out"), n + 1)
                dve.tensor_tensor(X[:, col(n)], PS[:, n], X[:, col(n)], ALU.add)


def l3_attention(nc, X, XN, PS, W):
    with ExitStack() as ctx:
        sb = lambda name, shape: ctx.enter_context(nc.sbuf_tensor(name, shape, F32))
        OT = sb("gl_o", [P, T])
        with ExitStack() as inner:
            own = lambda name, shape: inner.enter_context(nc.sbuf_tensor(name, shape, F32))
            QE = own("gl_qe", [P, PIX])
            KE = own("gl_ke", [P, PIX])
            KD = own("gl_kd", [P, PIX])
            V = own("gl_v", [P, NB, ITILES, P])
            QM = own("gl_qm", [P, NB * GH, PIX])
            decay = own("gl_decay", [P, PIX // GC])
            l3_gates(nc, PS, W, XN, QE, KE, KD, V, QM, decay)
            l3_chunks(nc, PS, W, KE, KD, V, QM, decay, OT)
        l3_gated_output(nc, X, PS, W, XN, OT)


EXPERTS = 32
EH = 32
EB = EXPERTS * EH // P
TT = T // P


def l3f_pack(w):
    p = Pack()
    L = lambda n: w["L3_ffn_" + n]
    p.add("select", L("expert_sel").T)
    p.add("keys", L("keys").transpose(1, 0, 2))
    p.add("values", L("values").reshape(EB, P, P).transpose(1, 0, 2))
    p.add("ident", np.eye(P, dtype=np.float32))
    p.add("mean", np.full((P, P), 1.0 / P, np.float32))
    p.add("centre", np.eye(P, dtype=np.float32) - np.float32(1.0 / P))
    p.add("eps", np.full((P, 1), 1e-5, np.float32))
    p.add("index", np.tile(np.arange(EXPERTS, dtype=np.float32), (P, 1)))
    return p


def l3_experts(nc, X, XN, PS, W):
    with ExitStack() as ctx:
        st = Stage(nc, ctx)
        sb, sem = st.sb, st.sem
        SEL = sb("ex_sel", [P, TT, EXPERTS])
        best = sb("ex_best", [P, TT, 8])
        which = sb("ex_which", [P, TT, 8], mybir.dt.uint32)
        at = sb("ex_at", [P, TT, 8])
        hit = sb("ex_hit", [P, 2, TT, EXPERTS])
        GW = sb("ex_w", [P, TT, EXPERTS])
        H = sb("ex_h", [P, 2, EXPERTS, EH])
        HT = sb("ex_ht", [P, 2, EB, CH])
        block = ctx.enter_context(nc.Block())

        @block.tensor
        def _(pe):
            for t in range(TT):
                ins = pe.matmul(PS[:, 6, t * EXPERTS:(t + 1) * EXPERTS], XN[:, t * P:(t + 1) * P], W["select"],
                                start=True, stop=True)
            ins.then_inc(sem("select"), 1)

            def hidden(t):
                if t >= 2:
                    pe.wait_ge(sem("weighted"), 2 * (t - 1))
                for k in range(2):
                    ins = pe.matmul(PS[:, 2 * (t % 2) + k], XN[:, t * P:(t + 1) * P], W["keys"][:, k * CH:(k + 1) * CH],
                                    start=True, stop=True)
                ins.then_inc(sem("hidden"), 1)

            def turn(t):
                pe.wait_ge(sem("weighted"), 2 * (t + 1))
                for k in range(2):
                    if t >= 1:
                        pe.wait_ge(sem("ht"), 2 * (t - 1) + k + 1)
                    for j in range(4):
                        ins = pe.transpose(PS[:, 4 + k, j * P:(j + 1) * P],
                                           H[:, t % 2, 4 * (4 * k + j):4 * (4 * k + j) + 4].rearrange("p e h -> p (e h)"),
                                           W["ident"])
                    ins.then_inc(sem("turned"), 1)

            def values(n):
                pe.wait_ge(sem("ht"), 2 * 4 * (n + 1))
                if n >= 2:
                    pe.wait_ge(sem("added"), n - 1)
                if n == 0:
                    pe.wait_ge(sem("scores"), 1)
                for j in range(EB):
                    ins = pe.matmul(PS[:, 6 + n % 2], W["values"][:, j * P:(j + 1) * P], HT[:, n % 2, j],
                                    start=(j == 0), stop=(j == EB - 1))
                ins.then_inc(sem("out"), 1)

            for t in range(TT + 1):
                if t < TT:
                    hidden(t)
                if t >= 1:
                    turn(t - 1)
                if t >= 5 and (t - 5) % 4 == 0:
                    values((t - 5) // 4)
            values(NCH - 1)

        @block.scalar
        def _(act):
            act.wait_ge(sem("select"), 1)
            act.activation(SEL[:].rearrange("p t e -> p (t e)"), PS[:, 6], ACT.Sigmoid).then_inc(sem("scores"), 1)
            for t in range(TT):
                n = t // 4
                for k in range(2):
                    act.wait_ge(sem("turned"), 2 * t + k + 1)
                    if n >= 2 and t % 4 == 0:
                        act.wait_ge(sem("out"), n - 1)
                    act.activation(HT[:, n % 2, 4 * k:4 * k + 4, (t % 4) * P:(t % 4 + 1) * P],
                                   PS[:, 4 + k].rearrange("p (j c) -> p j c", j=4), ACT.Copy).then_inc(sem("ht"), 1)

        @block.vector
        def _(dve):
            link = Chain(dve, sem("dve_chain"))
            dve.wait_ge(sem("scores"), 1)
            for t in range(TT):
                ins = dve.max(best[:, t], SEL[:, t])
            link(ins)
            for t in range(TT):
                ins = dve.max_index(which[:, t], best[:, t], SEL[:, t])
            link(ins)
            link(dve.tensor_copy(at[:], which[:]))
            index = bc(W["index"], 1, TT)
            for k in range(2):
                link(dve.tensor_tensor(hit[:, k], index, at[:, :, k:k + 1].broadcast_to([P, TT, EXPERTS]), ALU.is_equal))
            link(dve.tensor_tensor(hit[:, 0], hit[:, 0], hit[:, 1], ALU.add))
            link(dve.tensor_tensor(GW[:], SEL[:], hit[:, 0], ALU.mult))

            def added(n):
                dve.wait_ge(sem("out"), n + 1)
                x = X[:, n * CH:(n + 1) * CH]
                dve.tensor_tensor(x, PS[:, 6 + n % 2], x, ALU.add).then_inc(sem("added"), 1)

            for t in range(TT):
                dve.wait_ge(sem("hidden"), t + 1)
                if t >= 2:
                    dve.wait_ge(sem("turned"), 2 * (t - 1))
                for k in range(2):
                    e = slice(16 * k, 16 * k + 16)
                    dve.scalar_tensor_tensor(H[:, t % 2, e], PS[:, 2 * (t % 2) + k].rearrange("p (e h) -> p e h", h=EH),
                                             0.0, bc(GW[:, t, e], 2, EH), ALU.max, ALU.mult).then_inc(sem("weighted"), 1)
                if t >= 6 and (t - 6) % 4 == 0:
                    added((t - 6) // 4)
            added(NCH - 1)


PACKS = [("l0", l0_pack), ("mlp", mlp_pack), ("l1", l1_pack), ("l2a", l2a_pack), ("l2f", l2f_pack), ("l3a", l3a_pack), ("l3f", l3f_pack)]


def build(nc, x_dram, packs, offsets, out_dram):
    with ExitStack() as ctx:
        sb = lambda name, shape: ctx.enter_context(nc.sbuf_tensor(name, shape, F32))
        sem = lambda name: ctx.enter_context(nc.semaphore(name))
        X = sb("residual", [P, T])
        PS = ctx.enter_context(nc.psum_tensor("banks", [P, 8, CH], F32))
        x_in, stored = [sem("x_in_%d" % b) for b in range(NB)], sem("stored")

        def dump(what):
            with nc.Block() as block:
                @block.sync
                def _(sp):
                    for b in range(NB):
                        sp.dma_start(out_dram[b].rearrange("c h w -> c (h w)"), what[:, b * PIX:(b + 1) * PIX]
                                     ).then_inc(stored, 16)
                    sp.wait_ge(stored, 32)

        def columns(*names):
            return max(packs[name].shape[1] for name in names)

        def send(places):
            with nc.Block() as block:
                @block.sync
                def _(sp):
                    for name, tile in places.items():
                        sp.dma_start(tile[:, 0:columns(name)], packs[name]).then_inc(arrived[name], 16)

        def ready(name, tile):
            with nc.Block() as block:
                @block.sync
                def _(sp):
                    sp.wait_ge(arrived[name], 16)
            return Weights(tile, offsets[name])

        arrived = {name: sem("arrived_" + name) for name in packs}
        shared = sb("pack_mlp_l3a", [P, columns("mlp", "l3a")])
        with ExitStack() as l0:
            tile = l0.enter_context(nc.sbuf_tensor("pack_l0", [P, packs["l0"].shape[1]], F32))
            W = Weights(tile, offsets["l0"])
            with nc.Block() as block:
                @block.sync
                def _(sp):
                    sp.dma_start(tile[:], packs["l0"]).then_inc(arrived["l0"], 16)
                    sp.dma_start(shared[:, 0:columns("mlp")], packs["mlp"]).then_inc(arrived["mlp"], 16)
                    sp.wait_ge(arrived["l0"], 16)

                @block.scalar
                def _(act):
                    for b in range(NB):
                        act.dma_start(X[:, b * PIX:(b + 1) * PIX], x_dram[b].rearrange("c h w -> c (h w)")
                                      ).then_inc(x_in[b], 16)

            with ExitStack() as att:
                own = lambda name, shape: att.enter_context(nc.sbuf_tensor(name, shape, F32))
                KM = own("l0_km", [P, NB, HEADS, KEYS])
                VT = own("l0_vt", [P, NB * PAIRS, P])
                Q = own("l0_q", [P, T])
                SALL = own("l0_scores", [P, NB * PAIRS * 2, HALF])
                with ExitStack() as sc:
                    A = sc.enter_context(nc.sbuf_tensor("l0_a", [P, NB * PAIRS, 32, HW], F32))
                    B = sc.enter_context(nc.sbuf_tensor("l0_b", [P, NB * PAIRS, 32, HW], F32))
                    l0_prepare(nc, X, PS, W, arrived["l0"], KM, VT, Q, A, B, x_in)
                    l0_scores(nc, PS, W, KM, Q, A, B, SALL)
                l0_attend(nc, X, PS, W, SALL, VT)
        stay = {name: sb("pack_" + name, [P, columns(name)]) for name in ("l1", "l2a")}
        stay["l2f"] = sb("pack_l2f_l3f", [P, columns("l2f", "l3f")])
        send(stay)
        l0_mlp(nc, X, PS, ready("mlp", shared))
        send({"l3a": shared})
        l1_attention(nc, X, PS, ready("l1", stay["l1"]))
        XN = sb("normed", [P, T])
        scratch = nc.dram_tensor("distances", (NB, P, ITILES, ROW), F32, kind="Internal").ap()
        W = ready("l2a", stay["l2a"])
        layer_norm(nc, "l2a_norm", X, XN, PS, W["centre"], W["mean"], W["eps"])
        l2_attention(nc, X, XN, PS, W, scratch)
        W = ready("l2f", stay["l2f"])
        l2_trajectory(nc, X, PS, W)
        send({"l3f": stay["l2f"]})
        W = ready("l3a", shared)
        layer_norm(nc, "l3a_norm", X, XN, PS, W["centre"], W["mean"], W["eps"])
        l3_attention(nc, X, XN, PS, W)
        W = ready("l3f", stay["l2f"])
        layer_norm(nc, "l3f_norm", X, XN, PS, W["centre"], W["mean"], W["eps"])
        l3_experts(nc, X, XN, PS, W)
        dump(X)


def kernel(**inputs):
    import concourse.bacc as bacc
    from concourse.bass_utils import run_bass_kernel_spmd

    nc = bacc.Bacc("TRN2", target_bir_lowering=False, num_devices=1)
    w = {k: np.asarray(v) for k, v in inputs.items()}
    arrays, packs, offsets = {"x": np.ascontiguousarray(w["x"])}, {}, {}
    x = nc.dram_tensor("x", arrays["x"].shape, F32, kind="ExternalInput").ap()
    for name, lay_out in PACKS:
        p = lay_out(w)
        a = arrays["pack_dram_" + name] = p.array()
        packs[name] = nc.dram_tensor("pack_dram_" + name, a.shape, F32, kind="ExternalInput").ap()
        offsets[name] = p.at
    out = nc.dram_tensor("out", arrays["x"].shape, F32, kind="ExternalOutput").ap()
    build(nc, x, packs, offsets, out)
    return run_bass_kernel_spmd(nc, [arrays], core_ids=[0]).results[0]["out"]
```
